# Optimizing a Trainium2 kernel written in Bass

```python
import numpy as np
import jax
import jax.numpy as jnp

def _softmax(x, axis=-1):
    return jax.nn.softmax(x, axis=axis)

def _gelu(x):
    return jax.nn.gelu(x, approximate=True)

def _silu(x):
    return jax.nn.silu(x)

def _sigmoid(x):
    return jax.nn.sigmoid(x)

def _layernorm(x, axis=-1, eps=1e-05):
    m = jnp.mean(x, axis=axis, keepdims=True)
    v = jnp.var(x, axis=axis, keepdims=True)
    return (x - m) / jnp.sqrt(v + eps)

def _scatter_add(tgt, idx, src, axis=0):
    return tgt.at[idx].add(src)

def _segment_sum(src, seg, n):
    return jax.ops.segment_sum(src, seg, n)
kernel_name = 'mk_metaformer_d2_conv_nchw256_r2_2eb6fe'

def setup_inputs(seed: int=0):
    np.random.seed(seed)
    _w = jnp.asarray

    def _rec_inputs():
        import jax
        import jax.numpy as jnp
        _gk = jax.random.key(seed)
        x = -0.0001732 + 1 * jax.random.normal(jax.random.fold_in(_gk, 1), (8, 128, 48, 48), jnp.float32)
        return x
    x = _rec_inputs()

    def _L0_conv_setup():
        import jax, jax.numpy as jnp
        import numpy as np
        B, C, H, W = (8, 128, 48, 48)
        C4 = C // 4
        EPS = 1e-05

        def _branch_params(key, cin, cout):
            k1, k2, k3, k4, k5, k6 = jax.random.split(key, 6)
            scale = 1.0 / np.sqrt(cin)
            return dict(W=jax.random.uniform(k1, (cout, cin), jnp.float32, -scale, scale), b=jax.random.uniform(k2, (cout,), jnp.float32, -scale, scale), gamma=1.0 + 0.1 * jax.random.normal(k3, (cout,), jnp.float32), beta=0.1 * jax.random.normal(k4, (cout,), jnp.float32), mean=0.1 * jax.random.normal(k5, (cout,), jnp.float32), var=jax.random.uniform(k6, (cout,), jnp.float32, 0.5, 1.5))

        def _branch(x, W, b, gamma, beta, mean, var):
            y = jnp.einsum('bchw,oc->bohw', x, W) + b[None, :, None, None]
            inv = gamma / jnp.sqrt(var + EPS)
            y = y * inv[None, :, None, None] + (beta - mean * inv)[None, :, None, None]
            return jax.nn.relu(y)
        key = jax.random.key(seed)
        kx, kf, kg, kh = jax.random.split(key, 4)
        pf = _branch_params(kf, C, C4)
        pg = _branch_params(kg, C, C4)
        ph = _branch_params(kh, C, C)
        inp = {'x': jax.random.normal(kx, (B, C, H, W), jnp.float32)}
        for tag, p in (('f', pf), ('g', pg), ('h', ph)):
            for k, v in p.items():
                inp[f'{k}_{tag}'] = v
        return inp
    _L0_conv_all = _L0_conv_setup()
    _L0_conv_in = {k: v for k, v in _L0_conv_all.items() if k in ('W_f', 'b_f', 'gamma_f', 'beta_f', 'mean_f', 'var_f', 'W_g', 'b_g', 'gamma_g', 'beta_g', 'mean_g', 'var_g', 'W_h', 'b_h', 'gamma_h', 'beta_h', 'mean_h', 'var_h')}
    del _L0_conv_all

    def _L0_ffn_setup():
        import jax, jax.numpy as jnp
        import numpy as np
        NUM_EXPERTS = 8
        TOP_K = 2
        B, S, D = (8, 4096, 128)

        def _moe(tokens, router_w, w1, b1, w2, b2):
            N = tokens.shape[0]
            E = router_w.shape[0]
            logits = tokens.astype(jnp.float32) @ router_w.astype(jnp.float32).T
            probs = jax.nn.softmax(logits, axis=-1)
            rw, re = jax.lax.top_k(probs, TOP_K)
            if TOP_K > 1:
                rw = rw / jnp.maximum(rw.sum(-1, keepdims=True), 1e-12)
            rw = rw.astype(tokens.dtype)
            combine = jnp.zeros((N, E), tokens.dtype).at[jnp.arange(N)[:, None], re].set(rw)
            out = tokens
            for e in range(E):
                h = jax.nn.gelu(tokens @ w1[e] + b1[e], approximate=False)
                y = h @ w2[e] + b2[e]
                out = out + combine[:, e:e + 1] * y
            return out
        key = jax.random.key(seed)
        ks = jax.random.split(key, 4)
        scale = 1.0 / np.sqrt(D).astype(np.float32)
        return {'input_embeddings': jax.random.normal(ks[0], (B, S, D), jnp.float32), 'router_w': jax.random.normal(ks[1], (NUM_EXPERTS, D), jnp.float32) * scale, 'w1': jax.random.normal(ks[2], (NUM_EXPERTS, D, D), jnp.float32) * scale, 'b1': jnp.zeros((NUM_EXPERTS, D), jnp.float32), 'w2': jax.random.normal(ks[3], (NUM_EXPERTS, D, D), jnp.float32) * scale, 'b2': jnp.zeros((NUM_EXPERTS, D), jnp.float32)}
    _L0_ffn_all = _L0_ffn_setup()
    _L0_ffn_in = {k: v for k, v in _L0_ffn_all.items() if k in ('router_w', 'w1', 'b1', 'w2', 'b2')}
    del _L0_ffn_all

    def _L1_conv_setup():
        import jax, jax.numpy as jnp
        import numpy as np
        K = 9

        def _conv3x3(x, w, b):
            y = jax.lax.conv_general_dilated(x, w, (1, 1), [(1, 1), (1, 1)], dimension_numbers=('NCHW', 'OIHW', 'NCHW'))
            return y + b[None, :, None, None]

        def _deform_gather(x, off_y, off_x, mask):
            B, C, H, W = x.shape
            kh = (jnp.arange(K, dtype=x.dtype) // 3).reshape(1, K, 1, 1)
            kw = (jnp.arange(K, dtype=x.dtype) % 3).reshape(1, K, 1, 1)
            py = jnp.arange(H, dtype=x.dtype).reshape(1, 1, H, 1) - 1.0 + kh + off_y
            px = jnp.arange(W, dtype=x.dtype).reshape(1, 1, 1, W) - 1.0 + kw + off_x
            y0 = jnp.floor(py)
            x0 = jnp.floor(px)
            wy1 = py - y0
            wx1 = px - x0
            xf = x.reshape(B, C, H * W)

            def corner(iy, ix, wgt):
                valid = (iy >= 0) & (iy <= H - 1) & (ix >= 0) & (ix <= W - 1)
                iyc = jnp.clip(iy, 0, H - 1).astype(jnp.int32)
                ixc = jnp.clip(ix, 0, W - 1).astype(jnp.int32)
                lin = (iyc * W + ixc).reshape(B, 1, K * H * W)
                g = jnp.take_along_axis(xf, lin, axis=2).reshape(B, C, K, H, W)
                return g * jnp.where(valid, wgt, 0.0)[:, None]
            val = corner(y0, x0, (1 - wy1) * (1 - wx1)) + corner(y0, x0 + 1, (1 - wy1) * wx1) + corner(y0 + 1, x0, wy1 * (1 - wx1)) + corner(y0 + 1, x0 + 1, wy1 * wx1)
            return val * mask[:, None]
        key = jax.random.key(seed)
        ks = jax.random.split(key, 4)
        B, C, Cout, H, W = (2, 128, 128, 64, 64)
        x = jax.random.normal(ks[0], (B, C, H, W), jnp.float32)
        w_off = jax.random.normal(ks[1], (3 * K, C, 3, 3), jnp.float32) * 0.01
        b_off = jnp.zeros((3 * K,), jnp.float32)
        weight = jax.random.normal(ks[2], (Cout, C, 3, 3), jnp.float32) * (1.0 / np.sqrt(K * C))
        bias = jnp.zeros((Cout,), jnp.float32)
        gamma = jnp.ones((Cout,), jnp.float32)
        beta = jnp.zeros((Cout,), jnp.float32)
        return {'x': x, 'w_off': w_off, 'b_off': b_off, 'weight': weight, 'bias': bias, 'gamma': gamma, 'beta': beta}
    _L1_conv_all = _L1_conv_setup()
    _L1_conv_in = {k: v for k, v in _L1_conv_all.items() if k in ('w_off', 'b_off', 'weight', 'bias', 'gamma', 'beta')}
    del _L1_conv_all

    def _L1_ffn_setup():
        import jax, jax.numpy as jnp
        import numpy as np
        B, N, D = (16, 2048, 128)
        NUM_EXPERTS, TOP_K, HEADS = (4, 2, 4)
        N_EDGES = 524288
        LN_EPS = 1e-05

        def _layernorm(x, g, b):
            mu = x.mean(-1, keepdims=True)
            var = ((x - mu) ** 2).mean(-1, keepdims=True)
            return (x - mu) * jax.lax.rsqrt(var + LN_EPS) * g + b

        def _forward(x, edge_index, W_gat, att_src, att_dst, b_gat, ln_gamma, ln_beta, W1, b1, W2, b2):
            Bc, Nc, Dc = x.shape
            M = Bc * Nc
            x_flat = x.reshape(M, Dc)
            h = (x_flat @ W_gat).reshape(M, HEADS, NUM_EXPERTS)
            loops = jnp.arange(M, dtype=edge_index.dtype)
            src = jnp.concatenate([edge_index[0], loops])
            dst = jnp.concatenate([edge_index[1], loops])
            a_src = (h * att_src).sum(-1)
            a_dst = (h * att_dst).sum(-1)
            e = jax.nn.leaky_relu(a_src[src] + a_dst[dst], negative_slope=0.2)
            e_max = jax.ops.segment_max(e, dst, num_segments=M)
            ee = jnp.exp(e - e_max[dst])
            denom = jax.ops.segment_sum(ee, dst, num_segments=M)
            alpha = ee / (denom[dst] + 1e-16)
            msg = h[src] * alpha[:, :, None]
            agg = jax.ops.segment_sum(msg, dst, num_segments=M).reshape(M, HEADS * NUM_EXPERTS) + b_gat
            scores = _layernorm(agg, ln_gamma, ln_beta).reshape(M, HEADS, NUM_EXPERTS).mean(1)
            scores = scores.reshape(Bc, Nc, NUM_EXPERTS)
            topk_s, topk_i = jax.lax.top_k(scores, TOP_K)
            w = jax.nn.softmax(topk_s, axis=-1)
            out = jnp.zeros_like(x)
            for ei in range(NUM_EXPERTS):
                g = jnp.where(topk_i == ei, w, 0.0).sum(-1)
                hh = jax.nn.gelu(x @ W1[ei] + b1[ei], approximate=False)
                out = out + g[..., None] * (hh @ W2[ei] + b2[ei])
            return out
        key = jax.random.key(seed)
        ks = jax.random.split(key, 8)
        s = 0.05
        return {'x': jax.random.normal(ks[0], (B, N, D), jnp.float32), 'W_gat': jax.random.normal(ks[1], (D, HEADS * NUM_EXPERTS), jnp.float32) * s, 'att_src': jax.random.normal(ks[2], (HEADS, NUM_EXPERTS), jnp.float32) * s, 'att_dst': jax.random.normal(ks[3], (HEADS, NUM_EXPERTS), jnp.float32) * s, 'b_gat': jnp.zeros((HEADS * NUM_EXPERTS,), jnp.float32), 'ln_gamma': jnp.ones((HEADS * NUM_EXPERTS,), jnp.float32), 'ln_beta': jnp.zeros((HEADS * NUM_EXPERTS,), jnp.float32), 'W1': jax.random.normal(ks[4], (NUM_EXPERTS, D, 2 * D), jnp.float32) * s, 'b1': jnp.zeros((NUM_EXPERTS, 2 * D), jnp.float32), 'W2': jax.random.normal(ks[5], (NUM_EXPERTS, 2 * D, D), jnp.float32) * s, 'b2': jnp.zeros((NUM_EXPERTS, D), jnp.float32), 'edge_index': jax.random.randint(ks[6], (2, N_EDGES), 0, B * N, jnp.int32)}
    _L1_ffn_all = _L1_ffn_setup()
    _L1_ffn_in = {k: v for k, v in _L1_ffn_all.items() if k in ('W_gat', 'att_src', 'att_dst', 'b_gat', 'ln_gamma', 'ln_beta', 'W1', 'b1', 'W2', 'b2', 'edge_index')}
    del _L1_ffn_all
    return {'x': x, 'L0_conv_W_f': _L0_conv_in['W_f'], 'L0_conv_b_f': _L0_conv_in['b_f'], 'L0_conv_gamma_f': _L0_conv_in['gamma_f'], 'L0_conv_beta_f': _L0_conv_in['beta_f'], 'L0_conv_mean_f': _L0_conv_in['mean_f'], 'L0_conv_var_f': _L0_conv_in['var_f'], 'L0_conv_W_g': _L0_conv_in['W_g'], 'L0_conv_b_g': _L0_conv_in['b_g'], 'L0_conv_gamma_g': _L0_conv_in['gamma_g'], 'L0_conv_beta_g': _L0_conv_in['beta_g'], 'L0_conv_mean_g': _L0_conv_in['mean_g'], 'L0_conv_var_g': _L0_conv_in['var_g'], 'L0_conv_W_h': _L0_conv_in['W_h'], 'L0_conv_b_h': _L0_conv_in['b_h'], 'L0_conv_gamma_h': _L0_conv_in['gamma_h'], 'L0_conv_beta_h': _L0_conv_in['beta_h'], 'L0_conv_mean_h': _L0_conv_in['mean_h'], 'L0_conv_var_h': _L0_conv_in['var_h'], 'L0_ffn_router_w': _L0_ffn_in['router_w'], 'L0_ffn_w1': _L0_ffn_in['w1'], 'L0_ffn_b1': _L0_ffn_in['b1'], 'L0_ffn_w2': _L0_ffn_in['w2'], 'L0_ffn_b2': _L0_ffn_in['b2'], 'L1_conv_w_off': _L1_conv_in['w_off'], 'L1_conv_b_off': _L1_conv_in['b_off'], 'L1_conv_weight': _L1_conv_in['weight'], 'L1_conv_bias': _L1_conv_in['bias'], 'L1_conv_gamma': _L1_conv_in['gamma'], 'L1_conv_beta': _L1_conv_in['beta'], 'L1_ffn_W_gat': _L1_ffn_in['W_gat'], 'L1_ffn_att_src': _L1_ffn_in['att_src'], 'L1_ffn_att_dst': _L1_ffn_in['att_dst'], 'L1_ffn_b_gat': _L1_ffn_in['b_gat'], 'L1_ffn_ln_gamma': _L1_ffn_in['ln_gamma'], 'L1_ffn_ln_beta': _L1_ffn_in['ln_beta'], 'L1_ffn_W1': _L1_ffn_in['W1'], 'L1_ffn_b1': _L1_ffn_in['b1'], 'L1_ffn_W2': _L1_ffn_in['W2'], 'L1_ffn_b2': _L1_ffn_in['b2'], 'L1_ffn_edge_index': _L1_ffn_in['edge_index']}

def reference(x, L0_conv_W_f, L0_conv_b_f, L0_conv_gamma_f, L0_conv_beta_f, L0_conv_mean_f, L0_conv_var_f, L0_conv_W_g, L0_conv_b_g, L0_conv_gamma_g, L0_conv_beta_g, L0_conv_mean_g, L0_conv_var_g, L0_conv_W_h, L0_conv_b_h, L0_conv_gamma_h, L0_conv_beta_h, L0_conv_mean_h, L0_conv_var_h, L0_ffn_router_w, L0_ffn_w1, L0_ffn_b1, L0_ffn_w2, L0_ffn_b2, L1_conv_w_off, L1_conv_b_off, L1_conv_weight, L1_conv_bias, L1_conv_gamma, L1_conv_beta, L1_ffn_W_gat, L1_ffn_att_src, L1_ffn_att_dst, L1_ffn_b_gat, L1_ffn_ln_gamma, L1_ffn_ln_beta, L1_ffn_W1, L1_ffn_b1, L1_ffn_W2, L1_ffn_b2, L1_ffn_edge_index):
    import jax
    import jax.numpy as jnp

    def _L0_conv_ref(x, W_f, b_f, gamma_f, beta_f, mean_f, var_f, W_g, b_g, gamma_g, beta_g, mean_g, var_g, W_h, b_h, gamma_h, beta_h, mean_h, var_h):
        import jax, jax.numpy as jnp
        import numpy as np
        B, C, H, W = (8, 128, 48, 48)
        C4 = C // 4
        EPS = 1e-05

        def _branch_params(key, cin, cout):
            k1, k2, k3, k4, k5, k6 = jax.random.split(key, 6)
            scale = 1.0 / np.sqrt(cin)
            return dict(W=jax.random.uniform(k1, (cout, cin), jnp.float32, -scale, scale), b=jax.random.uniform(k2, (cout,), jnp.float32, -scale, scale), gamma=1.0 + 0.1 * jax.random.normal(k3, (cout,), jnp.float32), beta=0.1 * jax.random.normal(k4, (cout,), jnp.float32), mean=0.1 * jax.random.normal(k5, (cout,), jnp.float32), var=jax.random.uniform(k6, (cout,), jnp.float32, 0.5, 1.5))

        def _branch(x, W, b, gamma, beta, mean, var):
            y = jnp.einsum('bchw,oc->bohw', x, W) + b[None, :, None, None]
            inv = gamma / jnp.sqrt(var + EPS)
            y = y * inv[None, :, None, None] + (beta - mean * inv)[None, :, None, None]
            return jax.nn.relu(y)
        b_, c_, h_, w_ = x.shape
        n = h_ * w_
        f = _branch(x, W_f, b_f, gamma_f, beta_f, mean_f, var_f).reshape(b_, -1, n)
        g = _branch(x, W_g, b_g, gamma_g, beta_g, mean_g, var_g).reshape(b_, -1, n)
        h = _branch(x, W_h, b_h, gamma_h, beta_h, mean_h, var_h).reshape(b_, -1, n)
        s = jnp.einsum('bci,bcj->bij', g, f)
        att = jax.nn.softmax(s, axis=-1)
        o = jnp.einsum('bij,bcj->bci', att, h)
        o = o.reshape(b_, c_, h_, w_)
        return o * x

    def _L0_ffn_ref(input_embeddings, router_w, w1, b1, w2, b2):
        import jax, jax.numpy as jnp
        import numpy as np
        NUM_EXPERTS = 8
        TOP_K = 2
        B, S, D = (8, 4096, 128)

        def _moe(tokens, router_w, w1, b1, w2, b2):
            N = tokens.shape[0]
            E = router_w.shape[0]
            logits = tokens.astype(jnp.float32) @ router_w.astype(jnp.float32).T
            probs = jax.nn.softmax(logits, axis=-1)
            rw, re = jax.lax.top_k(probs, TOP_K)
            if TOP_K > 1:
                rw = rw / jnp.maximum(rw.sum(-1, keepdims=True), 1e-12)
            rw = rw.astype(tokens.dtype)
            combine = jnp.zeros((N, E), tokens.dtype).at[jnp.arange(N)[:, None], re].set(rw)
            out = tokens
            for e in range(E):
                h = jax.nn.gelu(tokens @ w1[e] + b1[e], approximate=False)
                y = h @ w2[e] + b2[e]
                out = out + combine[:, e:e + 1] * y
            return out
        b, s, d = input_embeddings.shape
        tokens = input_embeddings.reshape(b * s, d)
        return _moe(tokens, router_w, w1, b1, w2, b2).reshape(b, s, d)

    def _L1_conv_ref(x, w_off, b_off, weight, bias, gamma, beta):
        import jax, jax.numpy as jnp
        import numpy as np
        K = 9

        def _conv3x3(x, w, b):
            y = jax.lax.conv_general_dilated(x, w, (1, 1), [(1, 1), (1, 1)], dimension_numbers=('NCHW', 'OIHW', 'NCHW'))
            return y + b[None, :, None, None]

        def _deform_gather(x, off_y, off_x, mask):
            B, C, H, W = x.shape
            kh = (jnp.arange(K, dtype=x.dtype) // 3).reshape(1, K, 1, 1)
            kw = (jnp.arange(K, dtype=x.dtype) % 3).reshape(1, K, 1, 1)
            py = jnp.arange(H, dtype=x.dtype).reshape(1, 1, H, 1) - 1.0 + kh + off_y
            px = jnp.arange(W, dtype=x.dtype).reshape(1, 1, 1, W) - 1.0 + kw + off_x
            y0 = jnp.floor(py)
            x0 = jnp.floor(px)
            wy1 = py - y0
            wx1 = px - x0
            xf = x.reshape(B, C, H * W)

            def corner(iy, ix, wgt):
                valid = (iy >= 0) & (iy <= H - 1) & (ix >= 0) & (ix <= W - 1)
                iyc = jnp.clip(iy, 0, H - 1).astype(jnp.int32)
                ixc = jnp.clip(ix, 0, W - 1).astype(jnp.int32)
                lin = (iyc * W + ixc).reshape(B, 1, K * H * W)
                g = jnp.take_along_axis(xf, lin, axis=2).reshape(B, C, K, H, W)
                return g * jnp.where(valid, wgt, 0.0)[:, None]
            val = corner(y0, x0, (1 - wy1) * (1 - wx1)) + corner(y0, x0 + 1, (1 - wy1) * wx1) + corner(y0 + 1, x0, wy1 * (1 - wx1)) + corner(y0 + 1, x0 + 1, wy1 * wx1)
            return val * mask[:, None]
        B, C, H, W = x.shape
        om = _conv3x3(x, w_off, b_off)
        off_y = om[:, :K]
        off_x = om[:, K:2 * K]
        m = jax.nn.sigmoid(om[:, 2 * K:])
        sampled = _deform_gather(x, off_y, off_x, m)
        Cout = weight.shape[0]
        y = jnp.einsum('bckhw,ock->bohw', sampled, weight.reshape(Cout, C, K))
        y = y + bias[None, :, None, None]
        mu = jnp.mean(y, axis=(0, 2, 3), keepdims=True)
        var = jnp.var(y, axis=(0, 2, 3), keepdims=True)
        yn = (y - mu) * jax.lax.rsqrt(var + 1e-05)
        return jax.nn.relu(yn * gamma[None, :, None, None] + beta[None, :, None, None])

    def _L1_ffn_ref(x, W_gat, att_src, att_dst, b_gat, ln_gamma, ln_beta, W1, b1, W2, b2, edge_index):
        import jax, jax.numpy as jnp
        import numpy as np
        B, N, D = (16, 2048, 128)
        NUM_EXPERTS, TOP_K, HEADS = (4, 2, 4)
        N_EDGES = 524288
        LN_EPS = 1e-05

        def _layernorm(x, g, b):
            mu = x.mean(-1, keepdims=True)
            var = ((x - mu) ** 2).mean(-1, keepdims=True)
            return (x - mu) * jax.lax.rsqrt(var + LN_EPS) * g + b

        def _forward(x, edge_index, W_gat, att_src, att_dst, b_gat, ln_gamma, ln_beta, W1, b1, W2, b2):
            Bc, Nc, Dc = x.shape
            M = Bc * Nc
            x_flat = x.reshape(M, Dc)
            h = (x_flat @ W_gat).reshape(M, HEADS, NUM_EXPERTS)
            loops = jnp.arange(M, dtype=edge_index.dtype)
            src = jnp.concatenate([edge_index[0], loops])
            dst = jnp.concatenate([edge_index[1], loops])
            a_src = (h * att_src).sum(-1)
            a_dst = (h * att_dst).sum(-1)
            e = jax.nn.leaky_relu(a_src[src] + a_dst[dst], negative_slope=0.2)
            e_max = jax.ops.segment_max(e, dst, num_segments=M)
            ee = jnp.exp(e - e_max[dst])
            denom = jax.ops.segment_sum(ee, dst, num_segments=M)
            alpha = ee / (denom[dst] + 1e-16)
            msg = h[src] * alpha[:, :, None]
            agg = jax.ops.segment_sum(msg, dst, num_segments=M).reshape(M, HEADS * NUM_EXPERTS) + b_gat
            scores = _layernorm(agg, ln_gamma, ln_beta).reshape(M, HEADS, NUM_EXPERTS).mean(1)
            scores = scores.reshape(Bc, Nc, NUM_EXPERTS)
            topk_s, topk_i = jax.lax.top_k(scores, TOP_K)
            w = jax.nn.softmax(topk_s, axis=-1)
            out = jnp.zeros_like(x)
            for ei in range(NUM_EXPERTS):
                g = jnp.where(topk_i == ei, w, 0.0).sum(-1)
                hh = jax.nn.gelu(x @ W1[ei] + b1[ei], approximate=False)
                out = out + g[..., None] * (hh @ W2[ei] + b2[ei])
            return out
        return _forward(x, edge_index, W_gat, att_src, att_dst, b_gat, ln_gamma, ln_beta, W1, b1, W2, b2)

    def _gn(v, G=32, eps=1e-05):
        B_, C_, H_, W_ = v.shape
        g = v.reshape(B_, G, C_ // G, H_, W_)
        m = jnp.mean(g, axis=(2, 3, 4), keepdims=True)
        s = jnp.var(g, axis=(2, 3, 4), keepdims=True)
        return ((g - m) / jnp.sqrt(s + eps)).reshape(v.shape)

    def _ln_c(v, eps=1e-06):
        m = jnp.mean(v, axis=1, keepdims=True)
        s = jnp.var(v, axis=1, keepdims=True)
        return (v - m) / jnp.sqrt(s + eps)

    def _ln_t(v, eps=1e-05):
        m = jnp.mean(v, axis=-1, keepdims=True)
        s = jnp.var(v, axis=-1, keepdims=True)
        return (v - m) / jnp.sqrt(s + eps)

    def _to_tokens(v):
        B_, C_, H_, W_ = v.shape
        return v.reshape(B_, C_, H_ * W_).transpose(0, 2, 1)

    def _from_tokens(t, like):
        B_, C_, H_, W_ = like.shape
        return t.transpose(0, 2, 1).reshape(B_, C_, H_, W_)
    x = x + _L0_conv_ref(_ln_c(x), L0_conv_W_f, L0_conv_b_f, L0_conv_gamma_f, L0_conv_beta_f, L0_conv_mean_f, L0_conv_var_f, L0_conv_W_g, L0_conv_b_g, L0_conv_gamma_g, L0_conv_beta_g, L0_conv_mean_g, L0_conv_var_g, L0_conv_W_h, L0_conv_b_h, L0_conv_gamma_h, L0_conv_beta_h, L0_conv_mean_h, L0_conv_var_h)
    t = _to_tokens(x)
    t = t + _L0_ffn_ref(_ln_t(t), L0_ffn_router_w, L0_ffn_w1, L0_ffn_b1, L0_ffn_w2, L0_ffn_b2)
    x = _from_tokens(t, x)
    x = x + _L1_conv_ref(_ln_c(x), L1_conv_w_off, L1_conv_b_off, L1_conv_weight, L1_conv_bias, L1_conv_gamma, L1_conv_beta)
    t = _to_tokens(x)
    t = t + _L1_ffn_ref(_ln_t(t), L1_ffn_W_gat, L1_ffn_att_src, L1_ffn_att_dst, L1_ffn_b_gat, L1_ffn_ln_gamma, L1_ffn_ln_beta, L1_ffn_W1, L1_ffn_b1, L1_ffn_W2, L1_ffn_b2, L1_ffn_edge_index)
    x = _from_tokens(t, x)
    return x

_drawn_inputs = setup_inputs


def setup_inputs(seed=0):
    import zlib

    import numpy as np

    out = dict(_drawn_inputs(seed))
    spreads = {'L0_ffn_b1': (0.0, 0.351),
     'L0_ffn_b2': (0.0, 0.1),
     'L1_conv_b_off': (0.0, 0.1),
     'L1_conv_bias': (0.0, 2.0),
     'L1_conv_gamma': (1.0, 0.2),
     'L1_conv_beta': (0.0, 0.278),
     'L1_ffn_b_gat': (0.0, 0.1),
     'L1_ffn_ln_gamma': (1.0, 0.6),
     'L1_ffn_ln_beta': (0.0, 1.624),
     'L1_ffn_b1': (0.0, 0.56),
     'L1_ffn_b2': (0.0, 0.279)}
    factors = {'L0_conv_b_f': 8.0,
     'L0_conv_gamma_f': 5.65,
     'L0_conv_beta_f': 6.776,
     'L0_conv_mean_f': 6.023,
     'L0_conv_var_f': 4.367,
     'L0_conv_b_g': 7.94,
     'L0_conv_gamma_g': 5.49,
     'L0_conv_beta_g': 4.511,
     'L0_conv_mean_g': 4.713,
     'L0_conv_var_g': 4.457,
     'L1_ffn_att_src': 8.0,
     'L1_ffn_att_dst': 37.927}
    for name, (base, spread) in spreads.items():
        noise = np.random.default_rng([zlib.crc32(name.encode()), seed]).standard_normal(out[name].shape)
        drawn = base * np.exp(spread * noise) if base else spread * noise
        out[name] = jnp.asarray(drawn.astype(out[name].dtype))
    for name, factor in factors.items():
        out[name] = (out[name] * factor).astype(out[name].dtype)
    return out
```

```python
import concourse.bass as bass
from concourse import mybir
from contextlib import ExitStack

F32 = mybir.dt.float32
I32 = mybir.dt.int32
BF16 = mybir.dt.bfloat16
ALU = mybir.AluOpType
ACT = mybir.ActivationFunctionType
AX = mybir.AxisListType

IMAGES, D, SIDE = 8, 128, 48
PIX = SIDE * SIDE
T = IMAGES * PIX
TILE = 128
TILES = T // TILE
CHUNK = 384
TPC = CHUNK // TILE
CHUNKS = T // CHUNK
CPI = PIX // CHUNK
TPI = PIX // TILE
DK = 32
TAPS = 9
BIG = 1.0e30


class Steps:

    def __init__(self, eng, sem, base=0):
        self.eng, self.sem, self.base, self.n = eng, sem, base, 0

    def mark(self, ins):
        ins.then_inc(self.sem, 1)
        self.n += 1
        return ins

    def done(self):
        self.eng.wait_ge(self.sem, self.base + self.n)

    def __call__(self, ins):
        self.mark(ins)
        self.done()


class Core:

    def __init__(self, nc, ctx):
        self.nc, self.ctx = nc, ctx
        self.X = ctx.enter_context(nc.sbuf_tensor("X", [128, T], F32))
        self.XN = ctx.enter_context(nc.sbuf_tensor("XN", [128, T], F32))
        self.psum = ctx.enter_context(nc.psum_tensor("psum", [128, 8, 512], F32))
        self.ident = ctx.enter_context(nc.sbuf_tensor("ident", [128, 128], F32))
        self.mean_w = ctx.enter_context(nc.sbuf_tensor("mean_w", [128, 128], F32))
        self.ones = ctx.enter_context(nc.sbuf_tensor("ones", [128, 128], F32))
        self.eps = ctx.enter_context(nc.sbuf_tensor("eps", [128, 2], F32))
        self.open = {}

    def semaphore(self, ctx, name):
        if id(ctx) not in self.open:
            mine = self.open[id(ctx)] = []

            def close():
                self.nc.clear_and_free_semaphores(mine)
                self.nc.all_engine_barrier()
                del self.open[id(ctx)]
            ctx.callback(close)
        handle = self.nc.alloc_semaphore(name=name)
        self.open[id(ctx)].append(handle)
        return handle


def setup(core, x):
    nc = core.nc
    with ExitStack() as ctx:
        zeroed = core.semaphore(ctx, "zeroed")
        made = core.semaphore(ctx, "made")
        loaded = core.semaphore(ctx, "x_loaded")
        block = ctx.enter_context(nc.Block())

        @block.gpsimd
        def _(pool):
            pool.memset(core.ident[:, :], 0.0).then_inc(zeroed, 1)
            pool.wait_ge(zeroed, 1)
            pool.affine_select(out=core.ident[:, :], in_=core.ident[:, :], compare_op=ALU.not_equal,
                               fill=1.0, base=0, pattern=[[-1, 128]], channel_multiplier=1).then_inc(made, 1)
            pool.wait_ge(made, 1)

        @block.vector
        def _(dve):
            dve.memset(core.mean_w[:, :], 1.0 / D)
            dve.memset(core.ones[:, :], 1.0)
            dve.memset(core.eps[:, 0:1], 1e-6)
            dve.memset(core.eps[:, 1:2], 1e-5)

        @block.sync
        def _(sp):
            for b in range(IMAGES):
                sp.dma_start(core.X[:, b * PIX:(b + 1) * PIX], x[b, :, :]).then_inc(loaded, 16)
            sp.wait_ge(loaded, 16 * IMAGES)


def normalise(core, name, eps_col, weights, row, rows_to, rows_dma=None):
    nc, X, XN, ps = core.nc, core.X, core.XN, core.psum
    LOT = 4
    with ExitStack() as ctx:
        sem = lambda n: core.semaphore(ctx, f"{name}_{n}")
        xs = ctx.enter_context(nc.sbuf_tensor(f"{name}_xs", [128, LOT, CHUNK], F32))
        sq = ctx.enter_context(nc.sbuf_tensor(f"{name}_sq", [128, LOT, CHUNK], F32))
        w = ctx.enter_context(nc.sbuf_tensor(f"{name}_w", [128, row], F32)) if weights is not None else core.ident
        if rows_dma:
            rows = ctx.enter_context(nc.sbuf_tensor(f"{name}_rows", [128, LOT, TPC, row], F32))
        w_in, mean_done, xc_done, sq_done, var_done, std_done, rstd_done, xn_done = map(sem, (
            "w_in", "mean", "xc", "sq", "var", "std", "rstd", "xn"))
        rows_done, bank_free = map(sem, ("rows_done", "bank_free"))
        stored = [sem(f"stored{b}") for b in range(LOT)] if rows_dma else []
        rows_out, rows_free = sem("rows_out"), sem("rows_free")
        n_dma = 4 if rows_dma else 0
        block = ctx.enter_context(nc.Block())

        @block.sync
        def _(sp):
            if weights is not None:
                sp.dma_start(w[:, :], weights).then_inc(w_in, 16)
                sp.wait_ge(w_in, 16)
            if rows_dma:
                with sp.Fori(0, CHUNKS // LOT) as i:
                    for b in range(LOT):
                        n = i * LOT + b
                        sp.wait_ge(rows_out, n + 1)
                        for dst in rows_dma(n):
                            sp.dma_start(dst, rows[:, b, :, :]).then_inc(stored[b], 16)
                    for b in range(LOT):
                        sp.wait_ge(stored[b], 16 * n_dma * (i + 1))
                        sp.sem_inc(rows_free, 1)

        @block.tensor
        def _(pe):
            if weights is not None:
                pe.wait_ge(w_in, 16)
            with pe.Fori(0, CHUNKS // LOT) as i:
                for b in range(LOT):
                    n = i * LOT + b
                    pe.wait_ge(bank_free, n + 1)
                    nc.tensor.matmul(ps[:, b, 0:CHUNK], core.mean_w[:, :], X[:, bass.ds(n * CHUNK, CHUNK)],
                                     start=True, stop=True).then_inc(mean_done, 1)
                for b in range(LOT):
                    n = i * LOT + b
                    pe.wait_ge(sq_done, n + 1)
                    nc.tensor.matmul(ps[:, LOT + b, 0:CHUNK], core.mean_w[:, :], sq[:, b, :],
                                     start=True, stop=True).then_inc(var_done, 1)
                if row:
                    for b in range(LOT):
                        n = i * LOT + b
                        pe.wait_ge(xn_done, n + 1)
                        for t in range(TPC):
                            mm = nc.tensor.matmul(ps[:, b, t * row:(t + 1) * row],
                                                  xs[:, b, t * TILE:(t + 1) * TILE], w[:, :],
                                                  start=True, stop=True)
                        mm.then_inc(rows_done, 1)

        @block.vector
        def _(dve):
            with dve.Fori(0, CHUNKS // LOT) as i:
                for b in range(LOT):
                    n = i * LOT + b
                    dve.wait_ge(mean_done, n + 1)
                    nc.vector.tensor_tensor(xs[:, b, :], X[:, bass.ds(n * CHUNK, CHUNK)], ps[:, b, 0:CHUNK],
                                            ALU.subtract).then_inc(xc_done, 1)
                for b in range(LOT):
                    n = i * LOT + b
                    dve.wait_ge(std_done, n + 1)
                    nc.vector.reciprocal(sq[:, b, :], sq[:, b, :]).then_inc(rstd_done, 1)
                for b in range(LOT):
                    n = i * LOT + b
                    dve.wait_ge(rstd_done, n + 1)
                    nc.vector.tensor_tensor(xs[:, b, :], xs[:, b, :], sq[:, b, :],
                                            ALU.mult).then_inc(xn_done, 1)

        @block.scalar
        def _(act):
            act.sem_inc(bank_free, LOT)
            if rows_dma:
                act.sem_inc(rows_free, LOT)
            with act.Fori(0, CHUNKS // LOT) as i:
                for b in range(LOT):
                    n = i * LOT + b
                    act.wait_ge(xc_done, n + 1)
                    nc.scalar.activation(sq[:, b, :], xs[:, b, :], ACT.Square).then_inc(sq_done, 1)
                for b in range(LOT):
                    n = i * LOT + b
                    act.wait_ge(var_done, n + 1)
                    nc.scalar.activation(sq[:, b, :], ps[:, LOT + b, 0:CHUNK], ACT.Sqrt,
                                         bias=core.eps[:, eps_col:eps_col + 1]).then_inc(std_done, 1)
                for b in range(LOT):
                    n = i * LOT + b
                    act.wait_ge(xn_done, n + 1)
                    keep = nc.scalar.activation(XN[:, bass.ds(n * CHUNK, CHUNK)], xs[:, b, :], ACT.Copy)
                    if not row:
                        keep.then_inc(bank_free, 1)
                        continue
                    act.wait_ge(rows_done, n + 1)
                    src = ps[:, b, 0:TPC * row].rearrange("p (t r) -> p t r", t=TPC)
                    if rows_dma:
                        act.wait_ge(rows_free, n + 1)
                        nc.scalar.activation(rows[:, b, :, :], src, ACT.Copy).then_inc(rows_out, 1)
                        act.wait_ge(rows_out, n + 1)
                        act.sem_inc(bank_free, 1)
                    else:
                        nc.scalar.activation(rows_to[:, bass.ds(n * TPC, TPC), :], src,
                                             ACT.Copy).then_inc(bank_free, 1)


def attention(core, p):
    nc, X, XN, ps = core.nc, core.X, core.XN, core.psum
    EPS = 1e-5
    RING = 6
    with ExitStack() as ctx:
        sem = lambda n: core.semaphore(ctx, f"at_{n}")
        sb = lambda n, s, d=F32: ctx.enter_context(nc.sbuf_tensor(f"at_{n}", s, d))
        w_f, w_g, w_h = sb("w_f", [128, DK]), sb("w_g", [128, DK]), sb("w_h", [128, D])
        fg_par = sb("fg_par", [DK, 2, 5])
        h_par = sb("h_par", [128, 5, D])
        fg_inv, fg_shift = sb("fg_inv", [DK, 2]), sb("fg_shift", [DK, 2])
        h_inv, h_shift = sb("h_inv", [128, D]), sb("h_shift", [128, D])
        xi = sb("xi", [128, PIX])
        f_aug, g_aug = sb("f_aug", [128, PIX]), sb("g_aug", [128, PIX])
        hT = sb("hT", [128, TPI, D])
        probs = sb("probs", [128, RING, CHUNK])
        psum_rows = sb("den", [128, CHUNK])
        mx, nmax = sb("mx", [128, TPI, 2]), sb("nmax", [128, TPI])
        mrow = sb("mrow", [TPI, TILE])
        att = sb("att", [128, CHUNK])
        w_in, par, xi_ready, fg_mm, fg_out, h_mm, h_out = map(sem, (
            "w_in", "par", "xi_ready", "fg_mm", "fg_out", "h_mm", "h_out"))
        s_mm, s_max, nmax_done, nmaxT, mrow_done, mrow_in, ones_row = map(sem, (
            "s_mm", "s_max", "nmax", "nmaxT", "mrow", "mrow_in", "ones_row"))
        st_mm, exp_done, pv_done, add_done, o_done, o_free, steps, bigs = map(sem, (
            "st_mm", "exp", "pv", "add", "o_done", "o_free", "steps", "hsteps"))
        var_ready, sd_ready = sem("var_ready"), sem("sd_ready")
        turns = sem("turns")
        block = ctx.enter_context(nc.Block())

        @block.sync
        def _(sp):
            sp.dma_start(w_f[:, :], p["w_f"]).then_inc(w_in, 16)
            sp.dma_start(w_g[:, :], p["w_g"]).then_inc(w_in, 16)
            sp.dma_start(w_h[:, :], p["w_h"]).then_inc(w_in, 16)
            for k, which in enumerate("fg"):
                for j, q in enumerate(("b", "gamma", "beta", "mean", "var")):
                    sp.dma_start(fg_par[:, k, j:j + 1],
                                 p[f"{q}_{which}"].rearrange("(c a) -> c a", a=1)).then_inc(w_in, 16)
            for j, q in enumerate(("b", "gamma", "beta", "mean", "var")):
                sp.dma_start(h_par[:, j, :], p[f"{q}_h"].rearrange("(a c) -> a c", a=1)
                             .to_broadcast([128, D])).then_inc(w_in, 16)
            sp.wait_ge(w_in, 16 * 18)
            with sp.Fori(0, IMAGES) as i:
                sp.wait_ge(mrow_done, i + 1)
                sp.dma_start(g_aug[DK:DK + 1, :].rearrange("a (t n) -> a t n", t=TPI),
                             mrow[:, :]).then_inc(mrow_in, 16)
            sp.wait_ge(mrow_in, 16 * IMAGES)

        @block.tensor
        def _(pe):
            pe.wait_ge(w_in, 16 * 18)
            pe.wait_ge(ones_row, 3)
            with pe.Fori(0, IMAGES) as i:
                pe.wait_ge(xi_ready, i + 1)
                pe.wait_ge(o_free, CPI * i + 1)
                for c in range(CPI):
                    for k, w in enumerate((w_f, w_g)):
                        q = 2 * c + k
                        if q >= 6:
                            pe.wait_ge(fg_out, 2 * CPI * i + q - 5)
                        nc.tensor.matmul(ps[0:DK, q % 6, 0:CHUNK], w[:, :], xi[:, c * CHUNK:(c + 1) * CHUNK],
                                         start=True, stop=True).then_inc(fg_mm, 1)
                pe.wait_ge(fg_out, 2 * CPI * (i + 1))
                for c in range(CPI):
                    for t in range(TPC):
                        j = c * TPC + t
                        mm = nc.tensor.matmul(ps[:, c, t * TILE:(t + 1) * TILE], xi[:, j * TILE:(j + 1) * TILE],
                                              w_h[:, :], start=True, stop=True)
                    mm.then_inc(h_mm, 1)
                pe.wait_ge(h_out, CPI * (i + 1))
                for t in range(TPI):
                    for k in range(2):
                        q = 2 * t + k
                        if q >= 2:
                            pe.wait_ge(s_max, 2 * TPI * i + q - 1)
                        for c in range(3):
                            mm = nc.tensor.matmul(ps[:, 3 * k + c, 0:CHUNK], g_aug[0:DK, t * TILE:(t + 1) * TILE],
                                                  f_aug[0:DK, (3 * k + c) * CHUNK:(3 * k + c + 1) * CHUNK],
                                                  start=True, stop=True)
                        mm.then_inc(s_mm, 1)
                pe.wait_ge(nmax_done, i + 1)
                nc.tensor.transpose(ps[0:TPI, 6, 0:TILE], nmax[:, :], core.ident[:, :]).then_inc(nmaxT, 1)
                pe.wait_ge(mrow_in, 16 * (i + 1))
                pe.sem_inc(turns, 1)
                with pe.Fori(0, CPI) as c:
                    r = i * CPI + c
                    LAG = 2
                    pe.wait_ge(o_free, r + 1)
                    for j in range(TPI + LAG):
                        if j < TPI:
                            pe.wait_ge(exp_done, r * TPI + j + 1)
                            nc.tensor.matmul(ps[:, j % 3, 0:CHUNK], f_aug[:, j * TILE:(j + 1) * TILE],
                                             g_aug[:, bass.ds(c * CHUNK, CHUNK)],
                                             start=True, stop=True).then_inc(st_mm, 1)
                        if j >= LAG:
                            k = j - LAG
                            pe.wait_ge(exp_done, r * TPI + k + 1 + 3)
                            nc.tensor.matmul(ps[:, 3, 0:CHUNK], hT[:, k, :], probs[:, k % RING, :],
                                             start=k == 0, stop=k == TPI - 1).then_inc(pv_done, 1)
                    pe.wait_ge(add_done, (r + 1) * TPI + RING)
                    nc.tensor.matmul(ps[:, 4, 0:CHUNK], core.ones[:, :], psum_rows[:, :],
                                     start=True, stop=True).then_inc(o_done, 1)

        @block.scalar
        def _(act):
            act.sem_inc(exp_done, 3)
            act.wait_ge(var_ready, 2)
            for inv in (fg_inv, h_inv):
                act.activation(inv[:, :], inv[:, :], ACT.Sqrt).then_inc(sd_ready, 1)
            act.wait_ge(par, 1)
            with act.Fori(0, IMAGES) as i:
                act.wait_ge(o_free, CPI * i + 1)
                act.activation(xi[:, :], XN[:, bass.ds(i * PIX, PIX)], ACT.Copy).then_inc(xi_ready, 1)
                for c in range(CPI):
                    for k, dst in enumerate((f_aug, g_aug)):
                        q = 2 * c + k
                        act.wait_ge(fg_mm, 2 * CPI * i + q + 1)
                        act.activation(dst[0:DK, c * CHUNK:(c + 1) * CHUNK], ps[0:DK, q % 6, 0:CHUNK], ACT.Relu,
                                       bias=fg_shift[:, k:k + 1], scale=fg_inv[:, k:k + 1]).then_inc(fg_out, 1)
                act.wait_ge(nmaxT, i + 1)
                act.activation(mrow[:, :], ps[0:TPI, 6, 0:TILE], ACT.Copy).then_inc(mrow_done, 1)
                with act.Fori(0, CPI) as c:
                    r = i * CPI + c
                    for j in range(TPI):
                        act.wait_ge(st_mm, r * TPI + j + 1)
                        act.wait_ge(pv_done, r * TPI + j + 1)
                        act.wait_ge(add_done, r * TPI + j + 1)
                        act.activation(probs[:, j % RING, :], ps[:, j % 3, 0:CHUNK],
                                       ACT.Exp).then_inc(exp_done, 1)

        @block.gpsimd
        def _(pool):
            pool.sem_inc(pv_done, RING)
            pool.memset(g_aug[:, :], 0.0).then_inc(ones_row, 1)
            pool.memset(f_aug[:, :], 0.0).then_inc(ones_row, 1)
            pool.wait_ge(ones_row, 2)
            pool.memset(f_aug[DK:DK + 1, :], 1.0).then_inc(ones_row, 1)

        @block.vector
        def _(dve):
            st = Steps(dve, steps)
            dve.sem_inc(add_done, RING)
            dve.wait_ge(w_in, 16 * 18)
            sets = ((fg_inv[:, :], fg_shift[:, :], lambda j: fg_par[:, :, j]),
                    (h_inv[:, :], h_shift[:, :], lambda j: h_par[:, j, :]))
            for inv, shift, q in sets:
                dve.tensor_scalar(inv, q(4), EPS, None, ALU.add).then_inc(var_ready, 1)
            dve.wait_ge(sd_ready, 2)
            for inv, shift, q in sets:
                st(dve.reciprocal(inv, inv))
                st(dve.tensor_tensor(inv, inv, q(1), ALU.mult))
                st(dve.tensor_tensor(shift, q(3), inv, ALU.mult))
                st(dve.tensor_tensor(shift, q(2), shift, ALU.subtract))
                st(dve.tensor_tensor(q(0), q(0), inv, ALU.mult))
                st(dve.tensor_tensor(shift, shift, q(0), ALU.add))
            dve.sem_inc(o_free, 1)
            dve.sem_inc(par, 1)

            with dve.Fori(0, IMAGES) as i:
                hs = Steps(dve, bigs, i * (2 * CPI))
                for c in range(CPI):
                    dve.wait_ge(h_mm, CPI * i + c + 1)
                    dst = hT[:, c * TPC:(c + 1) * TPC, :]
                    src = ps[:, c, 0:CHUNK].rearrange("p (t o) -> p t o", t=TPC)
                    wide = lambda a: a.rearrange("p (a o) -> p a o", a=1).to_broadcast([128, TPC, D])
                    hs(dve.tensor_tensor(dst, src, wide(h_inv[:, :]), ALU.mult))
                    hs(dve.tensor_tensor(dst, dst, wide(h_shift[:, :]), ALU.add))
                    dve.tensor_scalar(dst, dst, 0.0, None, ALU.max).then_inc(h_out, 1)
                assert hs.n == 2 * CPI
                for t in range(TPI):
                    for k in range(2):
                        q = 2 * t + k
                        dve.wait_ge(s_mm, 2 * TPI * i + q + 1)
                        dve.tensor_reduce(mx[:, t, k:k + 1], ps[:, 3 * k:3 * k + 3, 0:CHUNK], AX.XY,
                                          ALU.max).then_inc(s_max, 1)
                dve.wait_ge(s_max, 2 * TPI * (i + 1))
                dve.tensor_reduce(nmax[:, :], mx[:, :, :], AX.X, ALU.max, negate=True).then_inc(nmax_done, 1)
                with dve.Fori(0, CPI) as c:
                    r = i * CPI + c
                    for j in range(TPI):
                        dve.wait_ge(exp_done, r * TPI + j + 1 + 3)
                        if j == 0:
                            dve.tensor_copy(psum_rows[:, :], probs[:, 0, :]).then_inc(add_done, 1)
                        else:
                            dve.wait_ge(add_done, r * TPI + j + RING)
                            dve.tensor_tensor(psum_rows[:, :], psum_rows[:, :], probs[:, j % RING, :],
                                              ALU.add).then_inc(add_done, 1)
                    dve.wait_ge(o_done, r + 1)
                    at = Steps(dve, steps, st.n + r * 3)
                    here = bass.ds(i * PIX + c * CHUNK, CHUNK)
                    at(dve.reciprocal(att[:, :], ps[:, 4, 0:CHUNK]))
                    at(dve.tensor_tensor(att[:, :], att[:, :], ps[:, 3, 0:CHUNK], ALU.mult))
                    at(dve.tensor_tensor(att[:, :], att[:, :], XN[:, here], ALU.mult))
                    dve.tensor_tensor(X[:, here], X[:, here], att[:, :], ALU.add).then_inc(o_free, 1)




def pick_two(nc, dve, st, val, n, first, second, key, best, rank, m1, m2):
    wide = lambda a: a.rearrange("p (t e) -> p t e", e=1).to_broadcast([128, TILES, n])
    ranks = rank.rearrange("p (t e) -> p t e", t=1).to_broadcast([128, TILES, n])
    for mask, m in ((first, m1), (second, m2)):
        st(dve.tensor_reduce(m, val, AX.X, ALU.max))
        st(dve.tensor_tensor(key, val, wide(m), ALU.is_equal))
        st(dve.tensor_tensor(key, key, ranks, ALU.mult))
        st(dve.tensor_reduce(best, key, AX.X, ALU.max))
        st(dve.tensor_tensor(mask, key, wide(best), ALU.is_equal))
        if mask is first:
            st(dve.tensor_scalar(key, mask, -BIG, None, ALU.mult))
            st(dve.tensor_tensor(val, val, key, ALU.add))


def route_by_logits(core, logits, gates):
    nc, n = core.nc, 8
    with ExitStack() as ctx:
        sb = lambda k, s: ctx.enter_context(nc.sbuf_tensor(f"r0_{k}", s, F32))
        first, key = sb("first", [128, TILES, n]), sb("key", [128, TILES, n])
        best, m1, m2, total = (sb(k, [128, TILES]) for k in ("best", "m1", "m2", "total"))
        rank = sb("rank", [128, n])
        steps, shifted, exped = (core.semaphore(ctx, f"r0_{k}") for k in ("steps", "shifted", "exped"))
        block = ctx.enter_context(nc.Block())
        wide = lambda a: a.rearrange("p (t e) -> p t e", e=1).to_broadcast([128, TILES, n])

        @block.scalar
        def _(act):
            act.wait_ge(shifted, 1)
            act.activation(logits[:, :, :], logits[:, :, :], ACT.Exp).then_inc(exped, 1)

        @block.vector
        def _(dve):
            st = Steps(dve, steps)
            for e in range(n):
                st.mark(dve.memset(rank[:, e:e + 1], float(n - e)))
            st(dve.tensor_reduce(m1[:, :], logits[:, :, :], AX.X, ALU.max))
            dve.tensor_tensor(logits[:, :, :], logits[:, :, :], wide(m1[:, :]), ALU.subtract).then_inc(shifted, 1)
            dve.wait_ge(exped, 1)
            st(dve.tensor_reduce(total[:, :], logits[:, :, :], AX.X, ALU.add))
            st(dve.reciprocal(total[:, :], total[:, :]))
            st(dve.tensor_tensor(logits[:, :, :], logits[:, :, :], wide(total[:, :]), ALU.mult))
            pick_two(nc, dve, st, logits[:, :, :], n, first[:, :, :], gates[:, :, :], key[:, :, :], best[:, :],
                     rank[:, :], m1[:, :], m2[:, :])
            st(dve.tensor_tensor(total[:, :], m1[:, :], m2[:, :], ALU.add))
            st(dve.tensor_scalar(total[:, :], total[:, :], 1e-12, None, ALU.max))
            st(dve.reciprocal(total[:, :], total[:, :]))
            for mask, m in ((first, m1), (gates, m2)):
                st(dve.tensor_tensor(m[:, :], m[:, :], total[:, :], ALU.mult))
                st(dve.tensor_tensor(mask[:, :, :], mask[:, :, :], wide(m[:, :]), ALU.mult))
            st(dve.tensor_tensor(gates[:, :, :], gates[:, :, :], first[:, :, :], ALU.add))


def experts(core, name, n_exp, gates, w1_d, b1_d, w2_d, b2_d, residual):
    nc, X, XN, ps = core.nc, core.X, core.XN, core.psum
    U = 8
    HALVES = U // n_exp
    CREDIT = 2 * HALVES
    with ExitStack() as ctx:
        sem = lambda k: core.semaphore(ctx, f"{name}_{k}")
        sb = lambda k, s: ctx.enter_context(nc.sbuf_tensor(f"{name}_{k}", s, F32))
        w1, w2, b1 = sb("w1", [128, U, 128]), sb("w2", [128, U, 128]), sb("b1", [128, U])
        b2, sel = sb("b2", [128, D]), sb("sel", [128, n_exp, 128])
        gt, gT = sb("gt", [128, 2, TPC, 128]), sb("gT", [128, 2, CHUNK])
        hid, hg = sb("hid", [128, 2, CHUNK]), sb("hg", [128, 2, CHUNK])
        w_in, made, gt_done, gT_mm, gT_out, b_mm, h_mm, h_act, hg_done, o_mm, x_half, x_done, w2_mm = map(sem, (
            "w_in", "made", "gt", "gT_mm", "gT_out", "b_mm", "h_mm", "h_act", "hg", "o_mm", "x_half", "x_done",
            "w2_mm"))
        gated, turns = sem("gated"), sem("turns")
        block = ctx.enter_context(nc.Block())
        BANK_T, BANK_B, BANK_H, BANK_O = 0, 1, 3, 5

        @block.sync
        def _(sp):
            sp.wait_ge(made, 4)
            sp.dma_start(w1[:, :, :].rearrange("p (e a) f -> p e (a f)", e=n_exp), w1_d).then_inc(w_in, 16)
            sp.dma_start(w2[:, :, :], w2_d).then_inc(w_in, 16)
            sp.dma_start(b1[:, :], b1_d).then_inc(w_in, 16)
            sp.dma_start(b2[0:n_exp, :], b2_d).then_inc(w_in, 16)
            sp.wait_ge(w_in, 64)

        @block.gpsimd
        def _(pool):
            pool.memset(sel[:, :, :], 0.0).then_inc(made, 1)
            pool.wait_ge(made, 1)
            pool.affine_select(out=sel[:, :, :], in_=sel[:, :, :], compare_op=ALU.not_equal, fill=1.0, base=0,
                               pattern=[[-1, n_exp], [0, 128]], channel_multiplier=1).then_inc(made, 1)
            pool.memset(gt[:, :, :, :], 0.0).then_inc(made, 1)
            pool.memset(b2[:, :], 0.0).then_inc(made, 1)
            pool.sem_inc(gated, 2)
            pool.wait_ge(made, 4)
            with pool.Fori(0, CHUNKS // 2) as i:
                for b in range(2):
                    n = 2 * i + b
                    pool.wait_ge(gated, n + 1)
                    pool.sem_inc(turns, 1)
                    pool.tensor_copy(gt[:, b, :, 0:n_exp], gates[:, bass.ds(n * TPC, TPC), :]).then_inc(gt_done, 1)

        @block.tensor
        def _(pe):
            pe.wait_ge(w_in, 64)
            pe.wait_ge(made, 4)
            with pe.Fori(0, CHUNKS // 2) as i:
                for b in range(2):
                    n = 2 * i + b
                    pe.wait_ge(gt_done, n + 1)
                    pe.wait_ge(gT_out, n + 1)
                    for t in range(TPC):
                        tr = nc.tensor.transpose(ps[:, BANK_T, t * TILE:(t + 1) * TILE], gt[:, b, t, :],
                                                 core.ident[:, :])
                    tr.then_inc(gT_mm, 1)
                    pe.wait_ge(gT_out, n + 2)
                    pe.wait_ge(x_done, n + 1)
                    pe.sem_inc(gated, 1)
                    out = ps[:, BANK_O + b, 0:CHUNK]
                    nc.tensor.matmul(out, b2[:, :], gT[:, b, :], start=True, stop=False)
                    for u in range(U + 1):
                        q = n * U + u
                        if u < U:
                            if u % HALVES == 0:
                                e = u // HALVES
                                pe.wait_ge(hg_done, (n * n_exp + e + 1) * HALVES)
                                nc.tensor.matmul(ps[:, BANK_B + e % 2, 0:CHUNK], sel[:, e, :], gT[:, b, :],
                                                 start=True, stop=True).then_inc(b_mm, 1)
                            pe.wait_ge(h_act, q + 1)
                            nc.tensor.matmul(ps[:, BANK_H + u % 2, 0:CHUNK], w1[:, u, :],
                                             XN[:, bass.ds(n * CHUNK, CHUNK)],
                                             start=True, stop=True).then_inc(h_mm, 1)
                        if u >= 1:
                            v = u - 1
                            pe.wait_ge(hg_done, q + CREDIT)
                            mm = nc.tensor.matmul(out, w2[:, v, :], hg[:, v % 2, :], start=False, stop=v == U - 1)
                            mm.then_inc(w2_mm, 1)

        @block.scalar
        def _(act):
            act.wait_ge(w_in, 64)
            act.sem_inc(gT_out, 1)
            act.sem_inc(h_act, 2)
            with act.Fori(0, CHUNKS // 2) as i:
                for b in range(2):
                    n = 2 * i + b
                    act.wait_ge(gT_mm, n + 1)
                    act.wait_ge(w2_mm, n * U + 2)
                    act.activation(gT[:, b, :], ps[:, BANK_T, 0:CHUNK], ACT.Copy).then_inc(gT_out, 1)
                    for u in range(U):
                        q = n * U + u
                        act.wait_ge(h_mm, q + 1)
                        act.wait_ge(hg_done, q - 1 + CREDIT)
                        act.activation(hid[:, u % 2, :], ps[:, BANK_H + u % 2, 0:CHUNK], ACT.Gelu,
                                       bias=b1[:, u:u + 1]).then_inc(h_act, 1)

        @block.vector
        def _(dve):
            dve.sem_inc(hg_done, CREDIT)
            dve.sem_inc(x_done, 2)
            dve.sem_inc(w2_mm, 2)
            with dve.Fori(0, CHUNKS // 2) as i:
                for b in range(2):
                    n = 2 * i + b
                    for u in range(U):
                        q = n * U + u
                        dve.wait_ge(h_act, q + 1 + 2)
                        dve.wait_ge(b_mm, n * n_exp + u // HALVES + 1)
                        dve.wait_ge(w2_mm, q + 1)
                        nc.vector.tensor_tensor(hg[:, u % 2, :], hid[:, u % 2, :],
                                                ps[:, BANK_B + u // HALVES % 2, 0:CHUNK],
                                                ALU.mult).then_inc(hg_done, 1)
                    here = bass.ds(n * CHUNK, CHUNK)
                    dve.wait_ge(w2_mm, (n + 1) * U + 2)
                    if residual:
                        nc.vector.tensor_tensor(X[:, here], X[:, here], XN[:, here], ALU.add).then_inc(x_half, 1)
                        dve.wait_ge(x_half, n + 1)
                    nc.vector.tensor_tensor(X[:, here], X[:, here], ps[:, BANK_O + b, 0:CHUNK],
                                            ALU.add).then_inc(x_done, 1)


def expert_phase_0(core, p):
    nc = core.nc
    with ExitStack() as ctx:
        logits = ctx.enter_context(nc.sbuf_tensor("logits", [128, TILES, 8], F32))
        gates = ctx.enter_context(nc.sbuf_tensor("gates0", [128, TILES, 8], F32))
        normalise(core, "ln2", 1, p["router_w"], 8, logits)
        route_by_logits(core, logits, gates)
        experts(core, "e0", 8, gates, p["w1"].rearrange("e d f -> d e f"), p["b1"],
                p["w2"].rearrange("e f c -> f e c"), p["b2"], True)


PAD = 64


CORNERS = (0, 1, SIDE, SIDE + 1)


def offsets(core, p, om, x_dram, table):
    nc, X, XN, ps = core.nc, core.X, core.XN, core.psum
    K3 = 3 * TAPS
    WIDE = SIDE + 2
    ROWS = CHUNK // SIDE
    with ExitStack() as ctx:
        sem = lambda k: core.semaphore(ctx, f"of_{k}")
        sb = lambda k, s: ctx.enter_context(nc.sbuf_tensor(f"of_{k}", s, F32))
        w, bias = sb("w", [128, TAPS, K3]), sb("bias", [K3, 1])
        zeros, zeros_made = sb("zeros", [PAD, D]), sem("zeros")
        padded, cols = sb("padded", [128, 2, WIDE, WIDE]), sb("cols", [K3, 2, CHUNK])
        w_in, zeroed, pad_done, conv_mm, conv_out, t_mm, t_out, saved, turns = map(sem, (
            "w_in", "zeroed", "pad", "conv_mm", "conv_out", "t_mm", "t_out", "saved", "turns"))
        block = ctx.enter_context(nc.Block())

        @block.sync
        def _(sp):
            sp.dma_start(w[:, :, :], p["w_off"]).then_inc(w_in, 16)
            sp.dma_start(bias[:, :], p["b_off"].rearrange("(c a) -> c a", a=1)).then_inc(w_in, 16)
            for b in range(IMAGES):
                sp.dma_start(x_dram[b, :, :], X[:, b * PIX:(b + 1) * PIX]).then_inc(saved, 16)
            sp.wait_ge(zeros_made, 1)
            ends = [(c, lo, hi) for c, back in enumerate(CORNERS)
                    for lo, hi in ((0, PAD - back), (T + PAD - back, T + PAD)) if hi > lo]
            for c, lo, hi in ends:
                sp.dma_start(table[lo:hi, c * D:(c + 1) * D], zeros[0:hi - lo, :]).then_inc(saved, 16)
            sp.wait_ge(w_in, 32)
            sp.wait_ge(saved, 16 * (IMAGES + len(ends)))

        @block.gpsimd
        def _(pool):
            pool.memset(zeros[:, :], 0.0).then_inc(zeros_made, 1)
            pool.memset(padded[:, :, :, :], 0.0).then_inc(zeroed, 1)
            pool.wait_ge(zeroed, 1)
            with pool.Fori(0, IMAGES // 2) as i:
                for b in range(2):
                    img = 2 * i + b
                    pool.wait_ge(conv_mm, (img + 1) * CPI)
                    pool.sem_inc(turns, 1)
                    pool.tensor_copy(padded[:, b, 1:1 + SIDE, 1:1 + SIDE],
                                     XN[:, bass.ds(img * PIX, PIX)].rearrange("p (y x) -> p y x", x=SIDE)
                                     ).then_inc(pad_done, 1)

        @block.tensor
        def _(pe):
            pe.sem_inc(conv_mm, 2 * CPI)
            pe.wait_ge(w_in, 32)
            with pe.Fori(0, IMAGES // 2) as i:
                for b in range(2):
                    img = 2 * i + b
                    pe.wait_ge(pad_done, img + 1)
                    for c in range(CPI + 1):
                        n = img * CPI + c
                        if c < CPI:
                            pe.wait_ge(conv_out, n + 1)
                            for k in range(TAPS):
                                y = ROWS * c + k // 3
                                mm = nc.tensor.matmul(ps[0:K3, c % 2, 0:CHUNK], w[:, k, :],
                                                      padded[:, b, y:y + ROWS, k % 3:k % 3 + SIDE],
                                                      start=k == 0, stop=k == TAPS - 1)
                            mm.then_inc(conv_mm, 1)
                        if c >= 1:
                            m = n - 1
                            pe.wait_ge(conv_out, m + 1 + 2)
                            pe.wait_ge(t_out, m + 1)
                            pe.sem_inc(turns, 1)
                            for t in range(TPC):
                                tr = nc.tensor.transpose(ps[:, 2 + (c - 1) % 2, t * K3:(t + 1) * K3],
                                                         cols[:, (c - 1) % 2, t * TILE:(t + 1) * TILE],
                                                         core.ident[0:K3, 0:K3])
                            tr.then_inc(t_mm, 1)

        @block.scalar
        def _(act):
            act.sem_inc(conv_out, 2)
            act.sem_inc(t_mm, 2)
            act.wait_ge(w_in, 32)
            with act.Fori(0, IMAGES) as img:
                for c in range(CPI):
                    n = img * CPI + c
                    act.wait_ge(conv_mm, n + 1 + 2 * CPI)
                    act.wait_ge(t_mm, n + 1)
                    act.activation(cols[:, c % 2, :], ps[0:K3, c % 2, 0:CHUNK], ACT.Identity,
                                   bias=bias[:, :]).then_inc(conv_out, 1)

        @block.vector
        def _(dve):
            dve.sem_inc(t_out, 2)
            with dve.Fori(0, IMAGES) as img:
                for c in range(CPI):
                    n = img * CPI + c
                    dve.wait_ge(t_mm, n + 1 + 2)
                    dve.tensor_copy(om[:, bass.ds(n * TPC, TPC), :],
                                    ps[:, 2 + c % 2, 0:TPC * K3].rearrange("p (t k) -> p t k", t=TPC)
                                    ).then_inc(t_out, 1)


def sample_points(core, om, index, corner_w):
    nc = core.nc
    N = TILES * TAPS
    TOP = SIDE - 2
    with ExitStack() as ctx:
        sem = lambda k: core.semaphore(ctx, f"sp_{k}")
        free = core.XN
        part = lambda k: free[:, k * N:(k + 1) * N]
        grid = lambda k: part(k).rearrange("p (t k) -> p t k", k=TAPS)
        point, low, over, near, far = (grid(k) for k in range(5))
        wy, wx, mask, base = [grid(5), grid(6)], [grid(7), grid(8)], grid(9), grid(10)
        flat = free[:, 11 * N:11 * N + 4 * TILES].rearrange("p (a t) -> p a t", a=4)
        row, col, pix, start = (flat[:, k, :] for k in range(4))
        cmp = free[:, 0:TILES * (SIDE - 1)].rearrange("p (t m) -> p t m", m=SIDE - 1)
        marks = ctx.enter_context(nc.sbuf_tensor("sp_marks", [128, SIDE - 1], F32))
        ints = ctx.enter_context(nc.sbuf_tensor("sp_ints", [128, TILES, TAPS], I32))
        small = ctx.enter_context(nc.sbuf_tensor("sp_small", [128, 2 * TILES + SIDE - 1], I32))
        made, steps, masked = sem("made"), sem("steps"), sem("masked")
        block = ctx.enter_context(nc.Block())

        @block.gpsimd
        def _(pool):
            pool.iota(small[:, 0:TILES], pattern=[[0, IMAGES], [TILE, TPI]], base=0,
                      channel_multiplier=1).then_inc(made, 1)
            pool.iota(small[:, TILES:2 * TILES], pattern=[[PIX, IMAGES], [0, TPI]], base=PAD,
                      channel_multiplier=0).then_inc(made, 1)
            pool.iota(small[:, 2 * TILES:], pattern=[[SIDE, SIDE - 1]], base=SIDE,
                      channel_multiplier=0).then_inc(made, 1)

        @block.scalar
        def _(act):
            act.activation(mask, om[:, :, 2 * TAPS:], ACT.Sigmoid).then_inc(masked, 1)

        @block.vector
        def _(dve):
            st = Steps(dve, steps)
            wide = lambda a: a.rearrange("p (t e) -> p t e", e=1)
            dve.wait_ge(made, 3)
            st.mark(dve.tensor_copy(pix, small[:, 0:TILES]))
            st.mark(dve.tensor_copy(start, small[:, TILES:2 * TILES]))
            st(dve.tensor_copy(marks[:, :], small[:, 2 * TILES:]))
            st(dve.tensor_tensor(cmp, wide(pix).to_broadcast([128, TILES, SIDE - 1]),
                                 marks[:, :].rearrange("p (t m) -> p t m", t=1).to_broadcast([128, TILES, SIDE - 1]),
                                 ALU.is_ge))
            st(dve.tensor_reduce(row, cmp, AX.X, ALU.add))
            st(dve.scalar_tensor_tensor(out=col, in0=row, scalar=-float(SIDE), in1=pix, op0=ALU.mult, op1=ALU.add))
            for axis, at, weights in ((0, row, wy), (1, col, wx)):
                for k in range(TAPS):
                    shift = float((k // 3 if axis == 0 else k % 3) - 1)
                    st.mark(dve.tensor_scalar(point[:, :, k:k + 1], wide(at), shift, None, ALU.add))
                st.done()
                st(dve.tensor_tensor(point, point, om[:, :, axis * TAPS:(axis + 1) * TAPS], ALU.add))
                st(dve.tensor_scalar(near, point, 0.0, float(TOP), ALU.max, ALU.min))
                st(dve.tensor_copy(ints[:, :, :], near))
                st(dve.tensor_copy(low, ints[:, :, :]))
                st(dve.tensor_tensor(over, low, near, ALU.is_gt))
                st(dve.tensor_tensor(low, low, over, ALU.subtract))
                st(dve.tensor_tensor(near, point, low, ALU.subtract))
                st(dve.tensor_scalar(far, near, 1.0, None, ALU.subtract))
                for k, dist in enumerate((near, far)):
                    st(dve.scalar_tensor_tensor(out=over, in0=dist, scalar=-1.0, in1=dist, op0=ALU.mult, op1=ALU.max))
                    st(dve.tensor_scalar(over, over, -1.0, 1.0, ALU.mult, ALU.add))
                    st(dve.tensor_scalar(weights[k], over, 0.0, None, ALU.max))
                if axis == 0:
                    st(dve.tensor_scalar(base, low, float(SIDE), None, ALU.mult))
                else:
                    st(dve.tensor_tensor(base, base, low, ALU.add))
            st(dve.tensor_tensor(base, base, wide(start).to_broadcast([128, TILES, TAPS]), ALU.add))
            st(dve.tensor_copy(index[:, :, :], base))
            dve.wait_ge(masked, 1)
            for a in range(2):
                st(dve.tensor_tensor(wy[a], wy[a], mask, ALU.mult))
                for b in range(2):
                    st(dve.tensor_tensor(corner_w[:, :, :, 2 * a + b], wy[a], wx[b], ALU.mult))


def deform(core, p, table, index, corner_w):
    nc, Y, ps = core.nc, core.X, core.psum
    RING = 3
    with ExitStack() as ctx:
        sem = lambda k: core.semaphore(ctx, f"df_{k}")
        sb = lambda k, s, d=F32: ctx.enter_context(nc.sbuf_tensor(f"df_{k}", s, d))
        patches = core.XN[:, 0:2 * TAPS * 4 * D].rearrange("p (b k c) -> p b k c", b=2, k=TAPS)
        ibuf = sb("ibuf", [128, 2, TAPS], I32)
        at = 2 * TAPS * 4 * D
        diag = core.XN[:, at:at + RING * 4 * TILE].rearrange("p (r c n) -> p r c n", r=RING, c=4)
        at += RING * 4 * TILE
        blended = core.XN[:, at:at + RING * 3 * TILE].rearrange("p (r k n) -> p r k n", r=RING, k=3)
        w, bias = sb("w", [128, TAPS, D]), sb("bias", [128, 1])
        w_in, i_done, diag_done, tap_mm, blend_out, y_mm, y_out, turns = map(sem, (
            "w_in", "index", "diag", "tap_mm", "blend_out", "y_mm", "y_out", "turns"))
        in_ = [sem("in0"), sem("in1")]
        block = ctx.enter_context(nc.Block())

        @block.sync
        def _(sp):
            sp.dma_start(w[:, :, :], p["weight"]).then_inc(w_in, 16)
            sp.dma_start(bias[:, :], p["bias"].rearrange("(c a) -> c a", a=1)).then_inc(w_in, 16)
            sp.wait_ge(w_in, 32)

        @block.gpsimd
        def _(pool):
            with pool.Fori(0, TILES // 2) as i:
                for b in range(2):
                    t = 2 * i + b
                    pool.wait_ge(i_done, t + 1)
                    pool.wait_ge(tap_mm, TAPS * (t + 1))
                    pool.sem_inc(turns, 1)
                    for k in range(TAPS):
                        pool.indirect_dma_start(
                            out=patches[:, b, k, :], out_offset=None, in_=table,
                            in_offset=bass.IndirectOffsetOnAxis(ap=ibuf[:, b, k:k + 1], axis=0)).then_inc(in_[b], 16)

        @block.tensor
        def _(pe):
            pe.sem_inc(tap_mm, 2 * TAPS)
            pe.wait_ge(w_in, 32)
            with pe.Fori(0, TILES // 2) as i:
                for b in range(2):
                    t = 2 * i + b
                    pe.wait_ge(in_[b], 16 * TAPS * (i + 1))
                    for g in range(4):
                        if g < 3:
                            pe.wait_ge(blend_out, 3 * t + g + 1)
                            for k in range(3 * g, 3 * g + 3):
                                pe.wait_ge(diag_done, TAPS * t + k + 1)
                                for c in range(4):
                                    mm = nc.tensor.matmul(ps[:, g, (k % 3) * TILE:(k % 3 + 1) * TILE],
                                                          patches[:, b, k, c * D:(c + 1) * D], diag[:, k % RING, c, :],
                                                          start=c == 0, stop=c == 3)
                                mm.then_inc(tap_mm, 1)
                        if g == 0:
                            pe.wait_ge(y_out, t + 1)
                        else:
                            pe.wait_ge(blend_out, 3 * t + g + 3)
                            for k in range(3 * g - 3, 3 * g):
                                mm = nc.tensor.matmul(ps[:, 3 + b, 0:TILE], w[:, k, :],
                                                      blended[:, g - 1, k % 3, :],
                                                      start=k == 0, stop=k == TAPS - 1)
                    mm.then_inc(y_mm, 1)

        @block.scalar
        def _(act):
            act.sem_inc(blend_out, 3)
            act.sem_inc(y_out, 2)
            act.wait_ge(w_in, 32)
            with act.Fori(0, TILES // 2) as i:
                for b in range(2):
                    t = 2 * i + b
                    for g in range(3):
                        act.wait_ge(tap_mm, TAPS * t + 3 * g + 3 + 2 * TAPS)
                        act.wait_ge(y_mm, t + 1)
                        act.activation(blended[:, g, :, :], ps[:, g, 0:3 * TILE].rearrange("p (k n) -> p k n", k=3),
                                       ACT.Copy).then_inc(blend_out, 1)
                    act.wait_ge(y_mm, t + 2)
                    act.activation(Y[:, bass.ds(t * TILE, TILE)], ps[:, 3 + b, 0:TILE], ACT.Identity,
                                   bias=bias[:, :]).then_inc(y_out, 1)

        @block.vector
        def _(dve):
            dve.sem_inc(y_mm, 1)
            with dve.Fori(0, TILES // 2) as i:
                for b in range(2):
                    t = 2 * i + b
                    dve.wait_ge(tap_mm, TAPS * (t + 1))
                    dve.tensor_copy(ibuf[:, b, :], index[:, bass.ds(t, 1), :]).then_inc(i_done, 1)
                    for k in range(TAPS):
                        dve.wait_ge(tap_mm, TAPS * t + k + 1 + 2 * TAPS - RING)
                        dve.tensor_tensor(
                            diag[:, k % RING, :, :],
                            core.ident[:, :].rearrange("p (c n) -> p c n", c=1).to_broadcast([128, 4, TILE]),
                            corner_w[:, bass.ds(t, 1), k, :].rearrange("p a (c n) -> p (a c) n", n=1)
                            .to_broadcast([128, 4, TILE]),
                            ALU.mult).then_inc(diag_done, 1)


def batch_norm(core, p, x_dram):
    nc, Y, ps = core.nc, core.X, core.psum
    LOT = 4
    with ExitStack() as ctx:
        sem = lambda k: core.semaphore(ctx, f"bn_{k}")
        sb = lambda k, s: ctx.enter_context(nc.sbuf_tensor(f"bn_{k}", s, F32))
        stats, agg, par = sb("stats", [128, CHUNKS, 6]), sb("agg", [128, 2]), sb("par", [128, 2])
        scale, shift, old = sb("scale", [128, 1]), sb("shift", [128, 1]), sb("old", [128, LOT, CHUNK])
        p_in, counted, steps, var_done, sd_done, ready, relu_done, x_done = map(sem, (
            "p_in", "counted", "steps", "var", "sd", "ready", "relu", "x"))
        old_in = [sem(f"old{b}") for b in range(LOT)]
        block = ctx.enter_context(nc.Block())

        @block.sync
        def _(sp):
            for j, q in enumerate(("gamma", "beta")):
                sp.dma_start(par[:, j:j + 1], p[q].rearrange("(c a) -> c a", a=1)).then_inc(p_in, 16)
            sp.wait_ge(p_in, 32)
            with sp.Fori(0, CHUNKS // LOT) as i:
                for b in range(LOT):
                    n = LOT * i + b
                    sp.wait_ge(x_done, n + 1)
                    sp.dma_start(old[:, b, :], x_dram[:, bass.ds(n * CHUNK, CHUNK)]).then_inc(old_in[b], 16)

        @block.vector
        def _(dve):
            st = Steps(dve, steps)
            dve.sem_inc(x_done, LOT)
            with dve.Fori(0, CHUNKS) as n:
                dve.bn_stats(stats[:, bass.ds(n, 1), :], Y[:, bass.ds(n * CHUNK, CHUNK)]).then_inc(counted, 1)
            dve.wait_ge(counted, CHUNKS)
            st(dve.bn_aggr(agg[:, :], stats[:, :, :]))
            dve.tensor_scalar(scale[:, :], agg[:, 1:2], 1e-5, None, ALU.add).then_inc(var_done, 1)
            dve.wait_ge(sd_done, 1)
            dve.wait_ge(p_in, 32)
            st(dve.reciprocal(scale[:, :], scale[:, :]))
            st(dve.tensor_tensor(scale[:, :], scale[:, :], par[:, 0:1], ALU.mult))
            st(dve.tensor_tensor(shift[:, :], scale[:, :], agg[:, 0:1], ALU.mult))
            dve.tensor_tensor(shift[:, :], par[:, 1:2], shift[:, :], ALU.subtract).then_inc(ready, 1)
            with dve.Fori(0, CHUNKS // LOT) as i:
                for b in range(LOT):
                    n = LOT * i + b
                    here = bass.ds(n * CHUNK, CHUNK)
                    dve.wait_ge(relu_done, n + 1)
                    dve.wait_ge(old_in[b], 16 * (i + 1))
                    dve.tensor_tensor(Y[:, here], Y[:, here], old[:, b, :], ALU.add).then_inc(x_done, 1)

        @block.scalar
        def _(act):
            act.wait_ge(var_done, 1)
            act.activation(scale[:, :], scale[:, :], ACT.Sqrt).then_inc(sd_done, 1)
            act.wait_ge(ready, 1)
            with act.Fori(0, CHUNKS) as n:
                here = bass.ds(n * CHUNK, CHUNK)
                act.activation(Y[:, here], Y[:, here], ACT.Relu, bias=shift[:, :],
                               scale=scale[:, :]).then_inc(relu_done, 1)


def deform_phase(core, p):
    nc = core.nc
    table = nc.dram_tensor("corner_table", (T + PAD, 4 * D), F32, kind="Internal").ap()
    x_dram = nc.dram_tensor("x_saved", (D, T), F32, kind="Internal").ap()
    by_image = x_dram.rearrange("c (b n) -> b c n", b=IMAGES)

    def stores(n):
        for c, back in enumerate(CORNERS):
            yield table[bass.ds(n * CHUNK + PAD - back, CHUNK), c * D:(c + 1) * D] \
                .rearrange("(t p) c -> p t c", p=TILE)

    with ExitStack() as ctx:
        sb = lambda k, s, d=F32: ctx.enter_context(nc.sbuf_tensor(f"dp_{k}", s, d))
        om = sb("om", [128, TILES, 3 * TAPS])
        normalise(core, "ln3", 0, None, D, None, stores)
        offsets(core, p, om, by_image, table)
        index, corner_w = sb("index", [128, TILES, TAPS], I32), sb("corner_w", [128, TILES, TAPS, 4])
        sample_points(core, om, index, corner_w)
        deform(core, p, table, index, corner_w)
    batch_norm(core, p, x_dram)


EDGES = 524288
WIDTH = EDGES // 128
RUN = 128
RUNS = EDGES // RUN
BLOCKS = RUNS // 128
DST_BIAS = 256
ID_BITS = 15
HEADS, GE = 4, 4
HF = HEADS * GE
SRC_ROW = HEADS + HF
STATE = HEADS + HEADS + HF
LEAK = 0.2


def sort_edges(core, edges, d):
    nc, ps = core.nc, core.psum
    K = [core.XN[:, k * WIDTH:(k + 1) * WIDTH] for k in range(2)]
    W_BITS, BITS = WIDTH.bit_length() - 1, EDGES.bit_length() - 1
    half = lambda buf, j: buf.rearrange("p (u two l) -> p u two l", two=2, l=1 << j)
    with ExitStack() as ctx:
        sem = lambda k: core.semaphore(ctx, f"so_{k}")
        sign, bits = (ctx.enter_context(nc.sbuf_tensor(f"so_{k}", [128, 8], t)) for k, t in (("sign", F32), ("bits", I32)))
        loaded, lanes, steps, sorted_, t_mm, t_out, out_ready, stored = map(sem, (
            "loaded", "lanes", "steps", "sorted", "t_mm", "t_out", "out_ready", "stored"))
        block = ctx.enter_context(nc.Block())
        n_swaps = 2 * (BITS - W_BITS)

        @block.gpsimd
        def _(pool):
            pool.iota(bits[:, :], pattern=[[0, 8]], base=0, channel_multiplier=1).then_inc(lanes, 1)

        final, outs, cur_of_swap = [], {}, []

        @block.vector
        def _(dve):
            st = Steps(dve, steps)
            dve.wait_ge(lanes, 1)
            for b in range(7):
                st.mark(dve.tensor_scalar(bits[:, b:b + 1], bits[:, b:b + 1], b, 1, ALU.logical_shift_right,
                                          ALU.bitwise_and))
            st.done()
            st(dve.tensor_copy(sign[:, 0:7], bits[:, 0:7]))
            st(dve.tensor_scalar(sign[:, 0:7], sign[:, 0:7], -2.0, 1.0, ALU.mult, ALU.add))
            dve.wait_ge(loaded, 32)
            src, dst = K[0].bitcast(I32), K[1].bitcast(I32)
            st(dve.tensor_scalar(dst, dst, DST_BIAS, None, ALU.add))
            st(dve.tensor_scalar(dst, dst, ID_BITS, None, ALU.logical_shift_left))
            st(dve.tensor_tensor(src, src, dst, ALU.bitwise_or))
            cur, swaps = 0, 0

            def negate(k):
                part = half(K[cur], k)[:, :, 1, :]
                st(dve.tensor_scalar(part, part, -1.0, None, ALU.mult))

            def by_lane(b):
                st(dve.tensor_scalar(K[cur], K[cur], sign[:, b:b + 1], None, ALU.mult))

            def compare(j):
                nonlocal cur
                a, b = half(K[cur], j), half(K[1 - cur], j)
                st.mark(dve.tensor_tensor(b[:, :, 0, :], a[:, :, 0, :], a[:, :, 1, :], ALU.min))
                st(dve.tensor_tensor(b[:, :, 1, :], a[:, :, 0, :], a[:, :, 1, :], ALU.max))
                cur = 1 - cur

            def swap():
                nonlocal cur, swaps
                dve.sem_inc(sorted_, 1)
                swaps += 1
                cur_of_swap.append(cur)
                cur = 1 - cur
                dve.wait_ge(t_out, 8 * swaps)

            for k in range(1, BITS + 1):
                if k < W_BITS:
                    negate(k)
                elif k < BITS:
                    by_lane(k - W_BITS)
                if k > W_BITS:
                    swap()
                    for j in reversed(range(k - W_BITS)):
                        compare(j)
                    swap()
                for j in reversed(range(min(k, W_BITS))):
                    compare(j)
                if k < W_BITS:
                    negate(k)
                elif k < BITS:
                    by_lane(k - W_BITS)
            assert swaps == n_swaps - 0
            keys = K[cur]
            final.append(keys)
            dve.sem_inc(out_ready, 1)
            ikeys = keys.bitcast(I32)
            at = 2 * WIDTH
            source = core.XN[:, at:at + WIDTH].bitcast(I32)
            same = core.XN[:, at + WIDTH:at + 2 * WIDTH]
            target = K[1 - cur].bitcast(I32)
            at += 2 * WIDTH
            R = WIDTH // RUN
            first, last, run_target = (core.XN[:, at + k * R:at + (k + 1) * R] for k in range(3))
            by_run = lambda a: a.rearrange("p (r f) -> p r f", f=RUN)
            one = lambda a: a.rearrange("p (r f) -> p r f", f=1)
            st(dve.tensor_scalar(source, ikeys, (1 << ID_BITS) - 1, None, ALU.bitwise_and))
            dve.tensor_scalar(source, source, T - 1, None, ALU.min).then_inc(out_ready, 1)
            st(dve.tensor_scalar(target, ikeys, ID_BITS, None, ALU.logical_shift_right))
            st(dve.tensor_tensor(same[:, 1:WIDTH], target[:, 1:WIDTH], target[:, 0:WIDTH - 1], ALU.is_equal))
            dve.memset(by_run(same)[:, :, 0:1], 0.0).then_inc(out_ready, 1)
            st.mark(dve.tensor_copy(one(first), by_run(keys)[:, :, 0:1]))
            st(dve.tensor_copy(one(last), by_run(keys)[:, :, RUN - 1:RUN]))
            dve.sem_inc(out_ready, 1)
            dve.tensor_scalar(one(run_target.bitcast(I32)), by_run(target)[:, :, 0:1], -DST_BIAS, T - 1, ALU.add,
                              ALU.min).then_inc(out_ready, 1)
            outs.update(source=source, same=same, first=first, last=last, run_target=run_target.bitcast(I32))

        @block.tensor
        def _(pe):
            for n, cur in enumerate(cur_of_swap):
                pe.wait_ge(sorted_, n + 1)
                for q in range(8):
                    m = 8 * n + q
                    if m >= 4:
                        pe.wait_ge(t_out, m - 3)
                    for t in range(4):
                        tr = nc.tensor.transpose(ps[:, q % 4, t * 128:(t + 1) * 128],
                                                 K[cur][:, (4 * q + t) * 128:(4 * q + t + 1) * 128], core.ident[:, :])
                    tr.then_inc(t_mm, 1)

        @block.scalar
        def _(act):
            for n, cur in enumerate(cur_of_swap):
                for q in range(8):
                    act.wait_ge(t_mm, 8 * n + q + 1)
                    act.activation(K[1 - cur][:, q * 512:(q + 1) * 512], ps[:, q % 4, :], ACT.Copy).then_inc(t_out, 1)

        @block.sync
        def _(sp):
            for k in range(2):
                sp.dma_start(K[k].bitcast(I32), edges[k, :].rearrange("(p f) -> p f", p=128)).then_inc(loaded, 16)
            sp.wait_ge(loaded, 32)
            sp.wait_ge(out_ready, 1)
            ordered = lambda a: a.rearrange("(p f) -> p f", p=128)
            sp.dma_start(ordered(d["keys"]), final[0]).then_inc(stored, 16)
            sp.wait_ge(out_ready, 5)
            sp.dma_start(ordered(d["source"]), outs["source"]).then_inc(stored, 16)
            sp.dma_start(ordered(d["same"]), outs["same"]).then_inc(stored, 16)
            sp.dma_start(ordered(d["first"]), outs["first"]).then_inc(stored, 16)
            sp.dma_start(ordered(d["last"]), outs["last"]).then_inc(stored, 16)
            sp.dma_start(ordered(d["run_target"]), outs["run_target"]).then_inc(stored, 16)
            sp.wait_ge(stored, 16 * 6)


def gather(core, name, table, width, index, tiles, lot, consume, sems=()):
    nc = core.nc
    lots = tiles // lot
    assert lots * lot == tiles
    with ExitStack() as ctx:
        sem = lambda k: core.semaphore(ctx, f"{name}_{k}")
        ibuf = ctx.enter_context(nc.sbuf_tensor(f"{name}_ibuf", [128, 2, lot], I32))
        rows = ctx.enter_context(nc.sbuf_tensor(f"{name}_rows", [128, 2, lot, width], F32))
        i_done, used, turns = sem("index"), sem("used"), sem("turns")
        in_ = [sem("in0"), sem("in1")]
        block = ctx.enter_context(nc.Block())

        @block.gpsimd
        def _(pool):
            def fetch(b, n):
                pool.wait_ge(i_done, n + 1)
                pool.wait_ge(used, n + 1)
                pool.sem_inc(turns, 1)
                for k in range(lot):
                    pool.indirect_dma_start(out=rows[:, b, k, :], out_offset=None, in_=table,
                                            in_offset=bass.IndirectOffsetOnAxis(ap=ibuf[:, b, k:k + 1], axis=0)
                                            ).then_inc(in_[b], 16)

            if lots > 1:
                with pool.Fori(0, lots // 2) as i:
                    for b in range(2):
                        fetch(b, 2 * i + b)
            if lots % 2:
                fetch(0, lots - 1)

        @block.vector
        def _(dve):
            dve.sem_inc(used, 2)

            def indices(b, n):
                dve.tensor_copy(ibuf[:, b, :], index[:, bass.ds(n * lot, lot)]).then_inc(i_done, 1)

            def take(b, n, times):
                dve.wait_ge(in_[b], 16 * lot * times)
                consume(dve, n, rows[:, b, :, :], used)

            if lots > 1:
                with dve.Fori(0, lots // 2) as i:
                    for b in range(2):
                        indices(b, 2 * i + b)
                    for b in range(2):
                        take(b, 2 * i + b, i + 1)
            if lots % 2:
                indices(0, lots - 1)
                take(0, lots - 1, lots // 2 + 1)


def find_starts(core, d, start, end):
    nc, ps = core.nc, core.psum
    N = TILES + 1
    S1 = RUNS // 64
    with ExitStack() as ctx:
        sb = lambda k, s, t=F32: ctx.enter_context(nc.sbuf_tensor(f"fs_{k}", s, t))
        least, iblk = sb("least", [128, N], I32), sb("iblk", [128, N], I32)
        blk, cnt, pos = sb("blk", [128, N]), sb("cnt", [128, N]), sb("pos", [128, N])
        next_lane, wrap = sb("next_lane", [128, 128]), sb("wrap", [128, 128])
        samples = core.XN[:, 0:RUNS]
        below = core.XN[:, RUNS:RUNS + N * S1].rearrange("p (t s) -> p t s", t=N)
        wide = lambda a, n: a.rearrange("p (t s) -> p t s", s=1).to_broadcast([128, a.shape[1], n])
        key = least[:, :].bitcast(F32)
        with ExitStack() as c2:
            sem = lambda k: core.semaphore(c2, f"fs_{k}")
            made, loaded, steps = sem("made"), sem("loaded"), sem("steps")
            block = c2.enter_context(nc.Block())

            @block.sync
            def _(sp):
                sp.dma_start(samples, d["first"].rearrange("(a f) -> a f", a=1).to_broadcast([128, RUNS])
                             ).then_inc(loaded, 16)
                sp.wait_ge(loaded, 16)

            @block.gpsimd
            def _(pool):
                pool.iota(least[:, :], pattern=[[TILE, N]], base=DST_BIAS, channel_multiplier=1).then_inc(made, 1)
                pool.memset(next_lane[:, :], 0.0).then_inc(made, 1)
                pool.memset(wrap[:, :], 0.0).then_inc(made, 1)
                pool.wait_ge(made, 3)
                pool.affine_select(out=next_lane[:, :], in_=next_lane[:, :], compare_op=ALU.not_equal, fill=1.0,
                                   base=-1, pattern=[[-1, 128]], channel_multiplier=1).then_inc(made, 1)
                pool.affine_select(out=wrap[:, :], in_=wrap[:, :], compare_op=ALU.not_equal, fill=1.0,
                                   base=127, pattern=[[-1, 128]], channel_multiplier=128).then_inc(made, 1)

            @block.vector
            def _(dve):
                st = Steps(dve, steps)
                dve.wait_ge(made, 3)
                st(dve.tensor_scalar(least[:, :], least[:, :], ID_BITS, None, ALU.logical_shift_left))
                dve.wait_ge(loaded, 16)
                coarse = samples.rearrange("p (a s f) -> p a s f", a=1, f=64)[:, :, :, 0].to_broadcast([128, N, S1])
                st(dve.tensor_tensor(below, coarse, wide(key, S1), ALU.is_lt))
                st(dve.tensor_reduce(blk[:, :], below, AX.X, ALU.add))
                st(dve.tensor_scalar(blk[:, :], blk[:, :], -1.0, 0.0, ALU.add, ALU.max))
                st(dve.tensor_copy(iblk[:, :], blk[:, :]))

        def count(width, lot):
            compared = core.semaphore(ctx, f"fs_compared{width}")

            def consume(dve, n, rows, used):
                here = bass.ds(n * lot, lot)
                dve.tensor_tensor(rows, rows, wide(key[:, here], width), ALU.is_lt).then_inc(compared, 1)
                dve.wait_ge(compared, n + 1)
                dve.tensor_reduce(cnt[:, here], rows, AX.X, ALU.add).then_inc(used, 1)
            return consume

        def finer(name, factor, to_int):
            steps = core.semaphore(ctx, name)
            with nc.Block() as block:
                @block.vector
                def _(dve):
                    st = Steps(dve, steps)
                    out = blk if to_int else pos
                    st(dve.scalar_tensor_tensor(out=out[:, :], in0=blk[:, :], scalar=float(factor), in1=cnt[:, :],
                                                op0=ALU.mult, op1=ALU.add))
                    if to_int:
                        st(dve.tensor_scalar(blk[:, :], blk[:, :], -1.0, 0.0, ALU.add, ALU.max))
                        st(dve.tensor_copy(iblk[:, :], blk[:, :]))

        gather(core, "fs_g2", d["first"].rearrange("(r s) -> r s", s=64), 64, iblk, N, 5, count(64, 5))
        finer("fs_finer2", 64, True)
        gather(core, "fs_g3", d["keys"].rearrange("(r s) -> r s", s=RUN), RUN, iblk, N, 5, count(RUN, 5))
        finer("fs_finer3", RUN, False)

        with ExitStack() as c3:
            moved, copied = (core.semaphore(c3, f"fs_{k}") for k in ("moved", "copied"))
            block = c3.enter_context(nc.Block())

            @block.tensor
            def _(pe):
                nc.tensor.matmul(ps[:, 0, 0:TILES], next_lane[:, :], pos[:, 0:TILES], start=True, stop=False)
                nc.tensor.matmul(ps[:, 0, 0:TILES], wrap[:, :], pos[:, 1:N], start=False, stop=True).then_inc(moved, 1)

            @block.vector
            def _(dve):
                dve.tensor_copy(start[:, :], pos[:, 0:TILES])
                dve.wait_ge(moved, 1)
                dve.tensor_copy(end[:, :], ps[:, 0, 0:TILES])


def index_phase(core, edges, start, end):
    nc = core.nc
    shapes = dict(keys=(EDGES, F32), source=(EDGES, I32), same=(EDGES, F32), first=(RUNS, F32), last=(RUNS, F32),
                  run_target=(RUNS, I32))
    d = {k: nc.dram_tensor(f"edge_{k}", (n,), t, kind="Internal").ap() for k, (n, t) in shapes.items()}
    sort_edges(core, edges, d)
    find_starts(core, d, start, end)
    return d


class Carver:

    def __init__(self, buf, parts=128):
        self.buf, self.at, self.parts = buf, 0, parts

    def __call__(self, *shape):
        n = 1
        for k in shape:
            n *= k
        piece = self.buf[0:self.parts, self.at:self.at + n]
        self.at += n
        assert self.at <= self.buf.shape[1]
        names = "abcd"[:len(shape)]
        return piece if len(shape) == 1 else piece.rearrange(
            f"p ({' '.join(names)}) -> p {' '.join(names)}", **dict(zip(names[1:], shape[1:])))


def source_tables(core, p, t, feats, tgt_score, start, end, xn_dram):
    nc, XN = core.nc, core.XN
    LOT = 8
    FILL = (EDGES + T) * HEADS // 128
    with ExitStack() as ctx:
        sem = lambda k: core.semaphore(ctx, f"st_{k}")
        sb = lambda k, s, d=F32: ctx.enter_context(nc.sbuf_tensor(f"st_{k}", s, d))
        rows, prod = sb("rows", [128, TILES, SRC_ROW]), sb("prod", [128, TILES, HF])
        att = sb("att", [128, 2, HF])
        where, empty, place = sb("where", [128, TILES]), sb("empty", [128, TILES]), sb("place", [128, TILES], I32)
        ibuf, sbuf = sb("ibuf", [128, 2, LOT], I32), sb("sbuf", [128, 2, LOT, HEADS])
        zeros = sb("zeros", [128, FILL // 16])
        loaded, steps, made, ready, zeroed, stored, saved, turns, i_done, spare = map(sem, (
            "loaded", "steps", "made", "ready", "zeroed", "stored", "saved", "turns", "i_done", "spare"))
        freed = sem("freed")
        placed_in = [sem("placed0"), sem("placed1")]
        block = ctx.enter_context(nc.Block())

        @block.sync
        def _(sp):
            for k, q in enumerate(("att_src", "att_dst")):
                sp.dma_start(att[:, k, :], p[q].rearrange("(a h) e -> a (h e)", a=1).to_broadcast([128, HF])
                             ).then_inc(loaded, 16)
            sp.wait_ge(made, 2)
            flat = t["placed"].rearrange("r h -> (r h)").rearrange("(k p f) -> k p f", k=16, p=128)
            for k in range(16):
                sp.dma_start(flat[k, :, :], zeros[:, :]).then_inc(zeroed, 16)
            for b in range(IMAGES):
                here = slice(b * PIX, (b + 1) * PIX)
                sp.dma_start(xn_dram[:, here], XN[:, here]).then_inc(saved, 16)
            sp.wait_ge(ready, 1)
            sp.dma_start(t["sources"].rearrange("(t p) c -> p t c", p=TILE), rows[:, :, :]).then_inc(stored, 16)
            sp.dma_start(t["targets"].rearrange("(t p) c -> p t c", p=TILE), tgt_score[:, :, :]).then_inc(stored, 16)
            sp.wait_ge(loaded, 32)
            sp.wait_ge(zeroed, 16 * 16)
            sp.wait_ge(saved, 16 * IMAGES)
            sp.wait_ge(stored, 32)

        @block.gpsimd
        def _(pool):
            pool.iota(place[:, :], pattern=[[TILE, TILES]], base=EDGES, channel_multiplier=1).then_inc(made, 1)
            pool.memset(zeros[:, :], 0.0).then_inc(made, 1)
            pool.wait_ge(zeroed, 16 * 16)
            with pool.Fori(0, TILES // LOT // 2) as i:
                for b in range(2):
                    pool.wait_ge(i_done, 2 * i + b + 1)
                    pool.sem_inc(turns, 1)
                    for k in range(LOT):
                        pool.indirect_dma_start(
                            out=t["placed"], out_offset=bass.IndirectOffsetOnAxis(ap=ibuf[:, b, k:k + 1], axis=0),
                            in_=sbuf[:, b, k, :], in_offset=None).then_inc(placed_in[b], 16)
                for b in range(2):
                    pool.wait_ge(placed_in[b], 16 * LOT * (i + 1))
                    pool.sem_inc(freed, 1)

        @block.vector
        def _(dve):
            st = Steps(dve, steps)
            dve.sem_inc(freed, 2)
            dve.wait_ge(loaded, 32)
            h = feats[:, :, :]
            by_head = lambda x: x.rearrange("p t (h e) -> p t h e", h=HEADS)
            wide = lambda k: att[:, k, :].rearrange("p (t c) -> p t c", t=1).to_broadcast([128, TILES, HF])
            st.mark(dve.tensor_copy(rows[:, :, HEADS:], h))
            st(dve.tensor_tensor(prod[:, :, :], h, wide(0), ALU.mult))
            st(dve.tensor_reduce(rows[:, :, 0:HEADS], by_head(prod[:, :, :]), AX.X, ALU.add))
            st(dve.tensor_tensor(prod[:, :, :], h, wide(1), ALU.mult))
            dve.tensor_reduce(tgt_score[:, :, :], by_head(prod[:, :, :]), AX.X, ALU.add).then_inc(ready, 1)
            dve.wait_ge(ready, 1)
            dve.wait_ge(made, 1)
            st(dve.tensor_copy(where[:, :], place[:, :]))
            st(dve.tensor_tensor(empty[:, :], start[:, :], end[:, :], ALU.is_equal))
            st(dve.tensor_tensor(where[:, :], where[:, :], start[:, :], ALU.subtract))
            st(dve.tensor_tensor(where[:, :], where[:, :], empty[:, :], ALU.mult))
            st(dve.tensor_tensor(where[:, :], where[:, :], start[:, :], ALU.add))
            st(dve.tensor_copy(place[:, :], where[:, :]))
            with dve.Fori(0, TILES // LOT // 2) as i:
                for b in range(2):
                    n = 2 * i + b
                    here = bass.ds(n * LOT, LOT)
                    dve.wait_ge(freed, n + 1)
                    dve.tensor_copy(ibuf[:, b, :], place[:, here]).then_inc(spare, 1)
                    dve.wait_ge(spare, n + 1)
                    dve.tensor_copy(sbuf[:, b, :, :], tgt_score[:, here, :]).then_inc(i_done, 1)


def edge_states(core, d, t):
    nc = core.nc
    with ExitStack() as ctx:
        sem = lambda k: core.semaphore(ctx, f"es_{k}")
        sb = lambda k, s, d_=F32: ctx.enter_context(nc.sbuf_tensor(f"es_{k}", s, d_))
        carve = Carver(core.XN)
        G, A, L = carve(2, RUN, SRC_ROW), carve(2, RUN, HEADS), carve(2, RUN, STATE)
        tgt, top, e, w = (carve(HEADS, RUN) for _ in range(4))
        m, decay = carve(HEADS, RUN + 1), carve(HEADS, RUN)
        msg = carve(HF, RUN)
        same, reset = sb("same", [128, 2, RUN]), sb("reset", [128, RUN])
        ibuf, rbuf = sb("ibuf", [128, 2, RUN], I32), sb("rbuf", [128, 2], I32)
        steps, used, in_rows, act_in, act_out, l_done, turns, zero = map(sem, (
            "steps", "used", "in_rows", "act_in", "act_out", "l_done", "turns", "zero"))
        idx_in, edge_in, rows_in, first_in, l_out = ([sem(f"{k}{b}") for b in range(2)] for k in (
            "idx", "edge", "rows", "first", "l_out"))
        N_STEPS, l_free = 19, sem("l_free")
        block = ctx.enter_context(nc.Block())
        blocks = lambda a: a.rearrange("(s p f) -> p s f", p=128, f=RUN)
        of_run = d["run_target"].rearrange("(s p a) -> p s a", p=128, a=1)
        placed = t["placed"][0:EDGES, :].rearrange("(s p f) h -> p s f h", p=128, f=RUN)
        states = t["states"].rearrange("(s p f) c -> p s f c", p=128, f=RUN)

        @block.sync
        def _(sp):
            with sp.Fori(0, BLOCKS // 2) as i:
                for b in range(2):
                    s = 2 * i + b
                    one = bass.ds(s, 1)
                    sp.wait_ge(used, s + 1)
                    sp.dma_start(ibuf[:, b:b + 1, :], blocks(d["source"])[:, one, :]).then_inc(idx_in[b], 16)
                    sp.dma_start(rbuf[:, b:b + 1].rearrange("p (s a) -> p s a", a=1), of_run[:, one, :]
                                 ).then_inc(idx_in[b], 16)
                    sp.dma_start(same[:, b:b + 1, :], blocks(d["same"])[:, one, :]).then_inc(edge_in[b], 16)
                    sp.dma_start(A[:, b:b + 1, :, :], placed[:, one, :, :]).then_inc(edge_in[b], 16)

        @block.scalar
        def _(act):
            with act.Fori(0, BLOCKS // 2) as i:
                for b in range(2):
                    s = 2 * i + b
                    for k, x in enumerate((w, decay)):
                        act.wait_ge(act_in, 2 * s + k + 1)
                        act.activation(x, x, ACT.Exp).then_inc(act_out, 1)
                    act.wait_ge(l_done, s + 1)
                    act.dma_start(states[:, bass.ds(s, 1), :, :], L[:, b:b + 1, :, :]).then_inc(l_out[b], 16)
                    act.wait_ge(l_out[b], 16 * (i + 1))
                    act.sem_inc(l_free, 1)

        @block.gpsimd
        def _(pool):
            with pool.Fori(0, BLOCKS // 2) as i:
                for b in range(2):
                    s = 2 * i + b
                    pool.wait_ge(idx_in[b], 32 * (i + 1))
                    pool.wait_ge(edge_in[b], 32 * (i + 1))
                    pool.wait_ge(used, s + 1)
                    pool.sem_inc(turns, 1)
                    pool.indirect_dma_start(
                        out=A[:, b, 0, :], out_offset=None, in_=t["targets"],
                        in_offset=bass.IndirectOffsetOnAxis(ap=rbuf[:, b:b + 1], axis=0)).then_inc(first_in[b], 16)
                    for f in range(RUN):
                        pool.indirect_dma_start(
                            out=G[:, b, f, :], out_offset=None, in_=t["sources"],
                            in_offset=bass.IndirectOffsetOnAxis(ap=ibuf[:, b, f:f + 1], axis=0)
                            ).then_inc(rows_in[b], 16)

        @block.vector
        def _(dve):
            dve.memset(m, 0.0).then_inc(zero, 1)
            dve.sem_inc(used, 2)
            dve.sem_inc(l_free, 2)
            dve.wait_ge(zero, 1)
            with dve.Fori(0, BLOCKS // 2) as i:
                for b in range(2):
                    s = 2 * i + b
                    st = Steps(dve, steps, s * N_STEPS)
                    dve.wait_ge(edge_in[b], 32 * (i + 1))
                    st(dve.tensor_scalar(reset[:, :], same[:, b, :], -1.0, BIG, ALU.add, ALU.mult))
                    dve.wait_ge(first_in[b], 16 * (i + 1))
                    for h in range(HEADS):
                        st.mark(dve.tensor_tensor_scan(out=tgt[:, h, :], data0=same[:, b, :], data1=A[:, b, :, h],
                                                       initial=0.0, op0=ALU.mult, op1=ALU.add))
                    dve.wait_ge(rows_in[b], 16 * RUN * (i + 1))
                    for h in range(HEADS):
                        st.mark(dve.tensor_tensor_scan(out=top[:, h, :], data0=reset[:, :], data1=G[:, b, :, h],
                                                       initial=0.0, op0=ALU.add, op1=ALU.max))
                    st.done()
                    src = G[:, b, :, 0:HEADS].rearrange("p f h -> p h f")
                    st.mark(dve.tensor_tensor(top, top, tgt, ALU.add))
                    st(dve.tensor_tensor(e, src, tgt, ALU.add))
                    now, before = m[:, :, 1:], m[:, :, 0:RUN]
                    st.mark(dve.scalar_tensor_tensor(out=now, in0=top, scalar=LEAK, in1=top, op0=ALU.mult,
                                                     op1=ALU.max))
                    st(dve.scalar_tensor_tensor(out=e, in0=e, scalar=LEAK, in1=e, op0=ALU.mult, op1=ALU.max))
                    st.mark(dve.tensor_tensor(decay, before, now, ALU.subtract))
                    dve.tensor_tensor(w, e, now, ALU.subtract).then_inc(act_in, 1)
                    st.done()
                    resets = reset[:, :].rearrange("p (h f) -> p h f", h=1).to_broadcast([128, HEADS, RUN])
                    dve.tensor_tensor(decay, decay, resets, ALU.min).then_inc(act_in, 1)
                    dve.wait_ge(l_free, s + 1)
                    out = L[:, b, :, :]
                    st(dve.tensor_copy(out[:, :, 0:HEADS].rearrange("p f h -> p h f"), now))
                    dve.wait_ge(act_out, 2 * s + 2)
                    for h in range(HEADS):
                        st.mark(dve.tensor_tensor(
                            msg[:, h * GE:(h + 1) * GE, :],
                            G[:, b, :, HEADS + h * GE:HEADS + (h + 1) * GE].rearrange("p f e -> p e f"),
                            w[:, h, :].rearrange("p (e f) -> p e f", e=1).to_broadcast([128, GE, RUN]), ALU.mult))
                    assert st.n == N_STEPS
                    st.done()
                    for c in range(HEADS + HF):
                        h = c if c < HEADS else (c - HEADS) // GE
                        x = w[:, h, :] if c < HEADS else msg[:, c - HEADS, :]
                        scan = dve.tensor_tensor_scan(out=out[:, :, HEADS + c], data0=decay[:, h, :], data1=x,
                                                      initial=0.0, op0=ALU.mult, op1=ALU.add)
                    scan.then_inc(l_done, 1)
                    dve.wait_ge(l_done, s + 1)
                    dve.sem_inc(used, 1)


def stitch_runs(core, d, t):
    nc, ps = core.nc, core.psum
    ROWS = HEADS + HF
    with ExitStack() as ctx:
        sem = lambda k: core.semaphore(ctx, f"sr_{k}")
        sb = lambda k, s, d_=F32: ctx.enter_context(nc.sbuf_tensor(f"sr_{k}", s, d_))
        wide = Carver(core.XN, ROWS)
        top, val, m, decay = wide(RUNS), wide(RUNS), wide(RUNS + 1), wide(RUNS)
        first, last = sb("first", [ROWS, RUNS]), sb("last", [ROWS, RUNS])
        ends = sb("ends", [128, BLOCKS, STATE])
        tops = sb("tops", [128, BLOCKS, ROWS])
        out = sb("out", [128, BLOCKS, 2 * ROWS])
        loaded, ends_in, steps, tops_done, t_mm, t_out, act_in, act_out, done, b_mm, b_out, stored = map(sem, (
            "loaded", "ends_in", "steps", "tops", "t_mm", "t_out", "act_in", "act_out", "done", "b_mm", "b_out",
            "stored"))
        block = ctx.enter_context(nc.Block())

        @block.sync
        def _(sp):
            sp.dma_start(ends[:, :, :], t["states"].rearrange("(s p f) c -> p s f c", p=128, f=RUN)[:, :, RUN - 1, :]
                         ).then_inc(ends_in, 16)
            for k, x in (("first", first), ("last", last)):
                sp.dma_start(x[:, :], d[k].rearrange("(a r) -> a r", a=1).to_broadcast([ROWS, RUNS])
                             ).then_inc(loaded, 16)
            sp.wait_ge(b_out, 2 * BLOCKS // 4)
            sp.dma_start(t["carry"].rearrange("(s p) c -> p s c", p=128), out[:, :, :]).then_inc(stored, 16)
            sp.wait_ge(stored, 16)
            sp.wait_ge(loaded, 32)
            sp.wait_ge(ends_in, 16)

        @block.vector
        def _(dve):
            st = Steps(dve, steps)
            dve.wait_ge(ends_in, 16)
            dve.tensor_copy(tops[:, :, 0:HEADS], ends[:, :, 0:HEADS]).then_inc(tops_done, 1)
            for h in range(HEADS):
                dve.tensor_copy(tops[:, :, HEADS + h * GE:HEADS + (h + 1) * GE],
                                ends[:, :, h:h + 1].to_broadcast([128, BLOCKS, GE])).then_inc(tops_done, 1)
            dve.wait_ge(loaded, 32)
            f, l = first[:, :].bitcast(I32), last[:, :].bitcast(I32)
            st.mark(dve.tensor_scalar(f, f, ID_BITS, None, ALU.logical_shift_right))
            st(dve.tensor_scalar(l, l, ID_BITS, None, ALU.logical_shift_right))
            st(dve.tensor_tensor(decay, f, l, ALU.is_equal))
            st(dve.tensor_tensor(m[:, 1:RUNS], f[:, 1:], l[:, 0:RUNS - 1], ALU.is_equal))
            st(dve.tensor_tensor(decay[:, 1:], decay[:, 1:], m[:, 1:RUNS], ALU.mult))
            st(dve.memset(decay[:, 0:1], 0.0))
            reset = first[:, :]
            st(dve.tensor_scalar(reset, decay, -1.0, BIG, ALU.add, ALU.mult))
            st(dve.memset(m[:, 0:1], 0.0))
            dve.wait_ge(t_out, 2 * BLOCKS // 4)
            st(dve.tensor_tensor_scan(out=m[:, 1:], data0=reset, data1=top, initial=0.0, op0=ALU.add, op1=ALU.max))
            st.mark(dve.tensor_tensor(top, top, m[:, 1:], ALU.subtract))
            st(dve.tensor_tensor(decay, m[:, 0:RUNS], m[:, 1:], ALU.subtract))
            dve.tensor_tensor(decay, decay, reset, ALU.min).then_inc(act_in, 1)
            dve.wait_ge(act_out, 2)
            st(dve.tensor_tensor(val, val, top, ALU.mult))
            dve.tensor_tensor_scan(out=top, data0=decay, data1=val, initial=0.0, op0=ALU.mult,
                                   op1=ALU.add).then_inc(done, 1)

        @block.tensor
        def _(pe):
            pe.wait_ge(tops_done, 1 + HEADS)
            for n in range(2 * BLOCKS // 4):
                k, q = divmod(n, BLOCKS // 4)
                if n >= 4:
                    pe.wait_ge(t_out, n - 3)
                for j in range(4):
                    x = (tops[:, 4 * q + j, :], ends[:, 4 * q + j, HEADS:])[k]
                    tr = nc.tensor.transpose(ps[0:ROWS, n % 4, j * 128:(j + 1) * 128], x, core.ident[:, :])
                tr.then_inc(t_mm, 1)
            pe.wait_ge(done, 1)
            for n in range(2 * BLOCKS // 4):
                k, q = divmod(n, BLOCKS // 4)
                x = (m[:, 1:], top)[k]
                if n >= 4:
                    pe.wait_ge(b_out, n - 3)
                for j in range(4):
                    tr = nc.tensor.transpose(ps[:, 4 + n % 4, j * ROWS:(j + 1) * ROWS],
                                             x[:, (4 * q + j) * 128:(4 * q + j + 1) * 128],
                                             core.ident[0:ROWS, 0:ROWS])
                tr.then_inc(b_mm, 1)

        @block.scalar
        def _(act):
            for n in range(2 * BLOCKS // 4):
                k, q = divmod(n, BLOCKS // 4)
                act.wait_ge(t_mm, n + 1)
                act.activation((top, val)[k][:, q * 512:(q + 1) * 512], ps[0:ROWS, n % 4, :],
                               ACT.Copy).then_inc(t_out, 1)
            act.wait_ge(act_in, 1)
            act.activation(top, top, ACT.Exp).then_inc(act_out, 1)
            act.activation(decay, decay, ACT.Exp).then_inc(act_out, 1)
            for n in range(2 * BLOCKS // 4):
                k, q = divmod(n, BLOCKS // 4)
                act.wait_ge(b_mm, n + 1)
                act.activation(out[:, 4 * q:4 * q + 4, k * ROWS:(k + 1) * ROWS],
                               ps[:, 4 + n % 4, 0:4 * ROWS].rearrange("p (j c) -> p j c", j=4),
                               ACT.Copy).then_inc(b_out, 1)


def edge_ends(core, start, end, at_end, before, has):
    nc = core.nc
    with ExitStack() as ctx:
        sb = lambda k, s, d_=F32: ctx.enter_context(nc.sbuf_tensor(f"ee_{k}", s, d_))
        pos = sb("pos", [128, TILES])
        steps = core.semaphore(ctx, "ee_steps")
        block = ctx.enter_context(nc.Block())

        @block.vector
        def _(dve):
            st = Steps(dve, steps)
            st(dve.tensor_scalar(pos[:, :], end[:, :], -1.0, 0.0, ALU.add, ALU.max))
            st(dve.tensor_copy(at_end[:, :], pos[:, :]))
            st(dve.tensor_scalar(before[:, :], at_end[:, :], RUN.bit_length() - 1, None, ALU.logical_shift_right))
            st(dve.tensor_copy(pos[:, :], before[:, :]))
            st(dve.tensor_scalar(has[:, 1, :], pos[:, :], float(RUN), None, ALU.mult))
            st(dve.tensor_tensor(has[:, 1, :], start[:, :], has[:, 1, :], ALU.is_lt))
            st(dve.tensor_tensor(has[:, 0, :], start[:, :], end[:, :], ALU.is_lt))
            st(dve.tensor_tensor(has[:, 1, :], has[:, 1, :], has[:, 0, :], ALU.mult))
            st(dve.tensor_scalar(pos[:, :], pos[:, :], -1.0, 0.0, ALU.add, ALU.max))
            st(dve.tensor_copy(before[:, :], pos[:, :]))


def graph_gates(core, p, feats, tgt_score, has, at_run, carried, gates):
    nc = core.nc
    carve = Carver(core.XN)
    with ExitStack() as ctx:
        sem = lambda k: core.semaphore(ctx, f"gg_{k}")
        sb = lambda k, s, d_=F32: ctx.enter_context(nc.sbuf_tensor(f"gg_{k}", s, d_))
        par = sb("par", [128, 4, HF])
        rank = sb("rank", [128, GE])
        m0, m1, m2, top, den, tmp = (carve(TILES, HEADS) for _ in range(6))
        agg, prod = carve(TILES, HF), carve(TILES, HF)
        off, mean, var, best, first, second = (carve(TILES) for _ in range(6))
        score, mask, key = (carve(TILES, GE) for _ in range(3))
        loaded, steps, act_in, act_out = map(sem, ("loaded", "steps", "act_in", "act_out"))
        block = ctx.enter_context(nc.Block())

        @block.sync
        def _(sp):
            flat = {"att_src": p["att_src"].rearrange("h e -> (h e)")}
            for k, q in enumerate(("att_src", "b_gat", "ln_gamma", "ln_beta")):
                v = flat.get(q, p[q])
                sp.dma_start(par[:, k, :], v.rearrange("(a c) -> a c", a=1).to_broadcast([128, HF])
                             ).then_inc(loaded, 16)
            sp.wait_ge(loaded, 64)

        @block.scalar
        def _(act):
            act.wait_ge(act_in, 1)
            for n, x in enumerate((m0, m1, m2)):
                act.activation(x, x, ACT.Exp).then_inc(act_out, 1)
            act.wait_ge(act_in, 2)
            act.activation(var, var, ACT.Sqrt, bias=core.eps[:, 1:2]).then_inc(act_out, 1)
            act.wait_ge(act_in, 3)
            act.activation(second, second, ACT.Exp).then_inc(act_out, 1)

        @block.vector
        def _(dve):
            st = Steps(dve, steps)
            heads = lambda x: x.rearrange("p t (h e) -> p t h e", h=HEADS)
            per_head = lambda x: x.rearrange("p t (h e) -> p t h e", e=1).to_broadcast([128, TILES, HEADS, GE])
            wide = lambda x, n: x.rearrange("p (t n) -> p t n", n=1).to_broadcast([128, TILES, n])
            const = lambda k: par[:, k, :].rearrange("p (t c) -> p t c", t=1).to_broadcast([128, TILES, HF])
            h = feats[:, :, :]
            dve.wait_ge(loaded, 64)
            for e in range(GE):
                st.mark(dve.memset(rank[:, e:e + 1], float(GE - e)))
            st(dve.tensor_tensor(prod, h, const(0), ALU.mult))
            st(dve.tensor_reduce(m0, heads(prod), AX.X, ALU.add))
            st(dve.tensor_tensor(m0, m0, tgt_score[:, :, :], ALU.add))
            st(dve.scalar_tensor_tensor(out=m0, in0=m0, scalar=LEAK, in1=m0, op0=ALU.mult, op1=ALU.max))
            for k, (m, x) in enumerate(((m1, at_run), (m2, carried))):
                st(dve.tensor_scalar(off, has[:, k, :], -1.0, BIG, ALU.add, ALU.mult))
                st(dve.tensor_tensor(m, x[:, :, 0:HEADS], wide(off, HEADS), ALU.add))
            st(dve.tensor_tensor(top, m1, m2, ALU.max))
            st(dve.tensor_tensor(top, top, m0, ALU.max))
            for m in (m0, m1, m2):
                st(dve.tensor_tensor(m, m, top, ALU.subtract))
            dve.sem_inc(act_in, 1)
            dve.wait_ge(act_out, 3)
            st(dve.tensor_tensor(heads(agg), heads(h), per_head(m0), ALU.mult))
            den_of, agg_of = (at_run[:, :, HEADS:2 * HEADS], carried[:, :, HEADS + HF:2 * HEADS + HF]), \
                (at_run[:, :, 2 * HEADS:], carried[:, :, 2 * HEADS + HF:])
            st(dve.tensor_copy(den, m0))
            for m, dn, ag in zip((m1, m2), den_of, agg_of):
                st.mark(dve.tensor_tensor(tmp, dn, m, ALU.mult))
                st(dve.tensor_tensor(heads(prod), heads(ag), per_head(m), ALU.mult))
                st.mark(dve.tensor_tensor(den, den, tmp, ALU.add))
                st(dve.tensor_tensor(agg, agg, prod, ALU.add))
            st(dve.tensor_scalar(den, den, 1e-16, None, ALU.add))
            st(dve.reciprocal(den, den))
            st(dve.tensor_tensor(heads(agg), heads(agg), per_head(den), ALU.mult))
            st(dve.tensor_tensor(agg, agg, const(1), ALU.add))
            st(dve.tensor_reduce(mean, agg, AX.X, ALU.add))
            st(dve.tensor_scalar(mean, mean, 1.0 / HF, None, ALU.mult))
            st(dve.tensor_tensor(agg, agg, wide(mean, HF), ALU.subtract))
            st(dve.tensor_tensor(prod, agg, agg, ALU.mult))
            st(dve.tensor_reduce(var, prod, AX.X, ALU.add))
            st(dve.tensor_scalar(var, var, 1.0 / HF, None, ALU.mult))
            dve.sem_inc(act_in, 1)
            dve.wait_ge(act_out, 4)
            st(dve.reciprocal(var, var))
            st(dve.tensor_tensor(agg, agg, wide(var, HF), ALU.mult))
            st(dve.tensor_tensor(agg, agg, const(2), ALU.mult))
            st(dve.tensor_tensor(agg, agg, const(3), ALU.add))
            st(dve.tensor_reduce(score, agg.rearrange("p t (h e) -> p t e h", h=HEADS), AX.X, ALU.add))
            st(dve.tensor_scalar(score, score, 1.0 / HEADS, None, ALU.mult))
            pick_two(nc, dve, st, score, GE, mask, gates[:, :, :], key, best, rank[:, :], first, second)
            st(dve.tensor_tensor(second, second, first, ALU.subtract))
            dve.sem_inc(act_in, 1)
            dve.wait_ge(act_out, 5)
            st(dve.tensor_scalar(first, second, 1.0, None, ALU.add))
            st(dve.reciprocal(first, first))
            st(dve.tensor_tensor(second, second, first, ALU.mult))
            st(dve.tensor_tensor(mask, mask, wide(first, GE), ALU.mult))
            st(dve.tensor_tensor(gates[:, :, :], gates[:, :, :], wide(second, GE), ALU.mult))
            st(dve.tensor_tensor(gates[:, :, :], gates[:, :, :], mask, ALU.add))


def reload(core, xn_dram):
    nc = core.nc
    with ExitStack() as ctx:
        loaded = core.semaphore(ctx, "xn_loaded")
        block = ctx.enter_context(nc.Block())

        @block.sync
        def _(sp):
            for b in range(IMAGES):
                here = slice(b * PIX, (b + 1) * PIX)
                sp.dma_start(core.XN[:, here], xn_dram[:, here]).then_inc(loaded, 16)
            sp.wait_ge(loaded, 16 * IMAGES)


def graph_phase(core, p, d, start, end):
    nc = core.nc
    dram = lambda k, *s: nc.dram_tensor(f"graph_{k}", s, F32, kind="Internal").ap()
    t = dict(sources=dram("sources", T, SRC_ROW), targets=dram("targets", T, HEADS),
             placed=dram("placed", EDGES + T, HEADS), states=dram("states", EDGES, STATE),
             carry=dram("carry", RUNS, 2 * (HEADS + HF)))
    xn_dram = dram("xn", D, T)
    with ExitStack() as outer:
        gates = outer.enter_context(nc.sbuf_tensor("gates1", [128, TILES, GE], F32))
        with ExitStack() as ctx:
            sb = lambda k, s, d_=F32: ctx.enter_context(nc.sbuf_tensor(f"gp_{k}", s, d_))
            feats, tgt_score = sb("feats", [128, TILES, HF]), sb("tgt", [128, TILES, HEADS])
            normalise(core, "ln4", 1, p["W_gat"], HF, feats)
            source_tables(core, p, t, feats, tgt_score, start, end, xn_dram)
            edge_states(core, d, t)
            stitch_runs(core, d, t)
            at_end, before = sb("at_end", [128, TILES], I32), sb("before", [128, TILES], I32)
            has = sb("has", [128, 2, TILES])
            edge_ends(core, start, end, at_end, before, has)
            tail = Carver(core.XN)
            tail.at = T - TILES * (STATE + 2 * (HEADS + HF))
            at_run, carried = tail(TILES, STATE), tail(TILES, 2 * (HEADS + HF))

            def keep(dst, name):
                def consume(dve, n, rows, used):
                    dve.tensor_copy(dst[:, bass.ds(n * 8, 8), :], rows).then_inc(used, 1)
                return consume

            gather(core, "ga", t["states"], STATE, at_end, TILES, 8, keep(at_run, "a"))
            gather(core, "gc", t["carry"], 2 * (HEADS + HF), before, TILES, 8, keep(carried, "c"))
            graph_gates(core, p, feats, tgt_score, has, at_run, carried, gates)
        reload(core, xn_dram)
        experts(core, "e1", GE, gates, p["W1"].rearrange("e d f -> d e f"), p["b1"],
                p["W2"].rearrange("e (a f) c -> f (e a) c", a=2), p["b2"], False)


def store(core, out):
    nc = core.nc
    with ExitStack() as ctx:
        stored = core.semaphore(ctx, "out_stored")
        block = ctx.enter_context(nc.Block())

        @block.sync
        def _(sp):
            for b in range(IMAGES):
                sp.dma_start(out[b, :, :], core.X[:, b * PIX:(b + 1) * PIX]).then_inc(stored, 16)
            sp.wait_ge(stored, 16 * IMAGES)


def metaformer(nc, p, out, stages="IABCD"):
    with ExitStack() as ctx:
        core = Core(nc, ctx)
        setup(core, p["x"])
        if "A" in stages:
            normalise(core, "ln1", 0, None, 0, None)
            attention(core, {k[8:].lower() if k[8] == "W" else k[8:]: v for k, v in p.items() if k.startswith("L0_conv_")})
        if "B" in stages:
            expert_phase_0(core, {k[7:]: v for k, v in p.items() if k.startswith("L0_ffn_")})
        if "I" in stages:
            start, end = (ctx.enter_context(nc.sbuf_tensor(k, [128, TILES], F32)) for k in ("start", "end"))
            edges = index_phase(core, p["L1_ffn_edge_index"], start, end)
        if stages == "I":
            with nc.Block() as block:
                @block.vector
                def _(dve):
                    dve.tensor_copy(core.X[:, 0:TILES], start[:, :])
                    dve.tensor_copy(core.X[:, TILES:2 * TILES], end[:, :])
        if "C" in stages:
            deform_phase(core, {k[8:]: v for k, v in p.items() if k.startswith("L1_conv_")})
        if "D" in stages:
            graph_phase(core, {k[7:]: v for k, v in p.items() if k.startswith("L1_ffn_")}, edges, start, end)
        store(core, out)


def kernel(**inputs):
    import numpy as _np
    import concourse.bacc as _bacc
    from concourse import mybir as _mybir
    from concourse.bass_utils import run_bass_kernel_spmd as _run

    laid = {k: _np.asarray(v) for k, v in inputs.items()}
    laid["x"] = laid["x"].reshape(IMAGES, D, PIX)
    for k in ("L0_conv_W_f", "L0_conv_W_g", "L0_conv_W_h", "L0_ffn_router_w"):
        laid[k] = laid[k].T
    laid["L0_ffn_b1"] = laid["L0_ffn_b1"].T
    laid["L1_ffn_b1"] = laid["L1_ffn_b1"].reshape(-1, 128).T
    for k in ("L1_conv_w_off", "L1_conv_weight"):
        laid[k] = laid[k].reshape(-1, D, TAPS).transpose(1, 2, 0)
    nc = _bacc.Bacc("TRN2", target_bir_lowering=False, num_devices=1)
    arrays, p = {}, {}
    for name, a in laid.items():
        a = _np.ascontiguousarray(a)
        arrays[f"in_{name}"] = a
        p[name] = nc.dram_tensor(f"in_{name}", a.shape, _mybir.dt.from_np(a.dtype), kind="ExternalInput").ap()
    out = nc.dram_tensor("out_0", (IMAGES, D, PIX), F32, kind="ExternalOutput").ap()
    metaformer(nc, p, out)
    r = _run(nc, [arrays], core_ids=[0])
    return r.results[0]["out_0"].reshape(IMAGES, D, SIDE, SIDE)
```

```python
import concourse.bass as bass
from concourse import mybir
from contextlib import ExitStack

F32 = mybir.dt.float32
I32 = mybir.dt.int32
BF16 = mybir.dt.bfloat16
ALU = mybir.AluOpType
ACT = mybir.ActivationFunctionType
AX = mybir.AxisListType

IMAGES, D, SIDE = 8, 128, 48
PIX = SIDE * SIDE
T = IMAGES * PIX
TILE = 128
TILES = T // TILE
CHUNK = 384
TPC = CHUNK // TILE
CHUNKS = T // CHUNK
CPI = PIX // CHUNK
TPI = PIX // TILE
DK = 32
TAPS = 9
BIG = 1.0e30


class Steps:

    def __init__(self, eng, sem, base=0):
        self.eng, self.sem, self.base, self.n = eng, sem, base, 0

    def mark(self, ins):
        ins.then_inc(self.sem, 1)
        self.n += 1
        return ins

    def done(self):
        self.eng.wait_ge(self.sem, self.base + self.n)

    def __call__(self, ins):
        self.mark(ins)
        self.done()


class Core:

    def __init__(self, nc, ctx):
        self.nc, self.ctx = nc, ctx
        self.X = ctx.enter_context(nc.sbuf_tensor("X", [128, T], F32))
        self.XN = ctx.enter_context(nc.sbuf_tensor("XN", [128, T], F32))
        self.psum = ctx.enter_context(nc.psum_tensor("psum", [128, 8, 512], F32))
        self.ident = ctx.enter_context(nc.sbuf_tensor("ident", [128, 128], F32))
        self.mean_w = ctx.enter_context(nc.sbuf_tensor("mean_w", [128, 128], F32))
        self.ones = ctx.enter_context(nc.sbuf_tensor("ones", [128, 128], F32))
        self.eps = ctx.enter_context(nc.sbuf_tensor("eps", [128, 2], F32))
        self.open = {}

    def semaphore(self, ctx, name):
        if id(ctx) not in self.open:
            mine = self.open[id(ctx)] = []

            def close():
                self.nc.clear_and_free_semaphores(mine)
                self.nc.all_engine_barrier()
                del self.open[id(ctx)]
            ctx.callback(close)
        handle = self.nc.alloc_semaphore(name=name)
        self.open[id(ctx)].append(handle)
        return handle


def setup(core, x):
    nc = core.nc
    with ExitStack() as ctx:
        zeroed = core.semaphore(ctx, "zeroed")
        made = core.semaphore(ctx, "made")
        loaded = core.semaphore(ctx, "x_loaded")
        block = ctx.enter_context(nc.Block())

        @block.gpsimd
        def _(pool):
            pool.memset(core.ident[:, :], 0.0).then_inc(zeroed, 1)
            pool.wait_ge(zeroed, 1)
            pool.affine_select(out=core.ident[:, :], in_=core.ident[:, :], compare_op=ALU.not_equal,
                               fill=1.0, base=0, pattern=[[-1, 128]], channel_multiplier=1).then_inc(made, 1)
            pool.wait_ge(made, 1)

        @block.vector
        def _(dve):
            dve.memset(core.mean_w[:, :], 1.0 / D)
            dve.memset(core.ones[:, :], 1.0)
            dve.memset(core.eps[:, 0:1], 1e-6)
            dve.memset(core.eps[:, 1:2], 1e-5)

        @block.sync
        def _(sp):
            for b in range(IMAGES):
                sp.dma_start(core.X[:, b * PIX:(b + 1) * PIX], x[b, :, :]).then_inc(loaded, 16)
            sp.wait_ge(loaded, 16 * IMAGES)


def normalise(core, name, eps_col, weights, row, rows_to, rows_dma=None):
    nc, X, XN, ps = core.nc, core.X, core.XN, core.psum
    LOT = 4
    LOTS = CHUNKS // LOT
    BANK_V = 7
    spread = lambda b: ps[:, LOT + b % 3, 0:CHUNK]
    with ExitStack() as ctx:
        sem = lambda n: core.semaphore(ctx, f"{name}_{n}")
        sb = lambda n, s: ctx.enter_context(nc.sbuf_tensor(f"{name}_{n}", s, F32))
        sq, diag = sb("sq", [128, LOT, CHUNK]), sb("diag", [128, LOT, TPC, TILE])
        std, rstd = sb("std", [128, LOT, TPC]), sb("rstd", [128, LOT, TPC])
        w = sb("w", [128, row]) if weights is not None else core.ident
        if row:
            xs = sb("xs", [128, LOT, CHUNK])
        if rows_dma:
            rows = sb("rows", [128, LOT, TPC, row])
        w_in, mean_done, xc_done, sq_done, var_done, std_done, rstd_done, diag_done = map(sem, (
            "w_in", "mean", "xc", "sq", "var", "std", "rstd", "diag"))
        spread_done, xn_done, xs_done, rows_done, bank_free, turns = map(sem, (
            "spread", "xn", "xs_done", "rows_done", "bank_free", "turns"))
        stored = [sem(f"stored{b}") for b in range(LOT)] if rows_dma else []
        rows_out, rows_free = sem("rows_out"), sem("rows_free")
        n_dma = 4 if rows_dma else 0
        block = ctx.enter_context(nc.Block())
        chunk = lambda n: slice(n * CHUNK, (n + 1) * CHUNK) if isinstance(n, int) else bass.ds(n * CHUNK, CHUNK)

        def lots(eng, ahead, body):
            ahead(0, True)
            with eng.Fori(0, LOTS - 1) as i:
                body(i, False)
            body(LOTS - 1, True)

        @block.sync
        def _(sp):
            if weights is not None:
                sp.dma_start(w[:, :], weights).then_inc(w_in, 16)
                sp.wait_ge(w_in, 16)
            if rows_dma:
                with sp.Fori(0, LOTS) as i:
                    for b in range(LOT):
                        n = i * LOT + b
                        sp.wait_ge(rows_out, n + 1)
                        for dst in rows_dma(n):
                            sp.dma_start(dst, rows[:, b, :, :]).then_inc(stored[b], 16)
                    for b in range(LOT):
                        sp.wait_ge(stored[b], 16 * n_dma * (i + 1))
                        sp.sem_inc(rows_free, 1)

        @block.tensor
        def _(pe):
            if weights is not None:
                pe.wait_ge(w_in, 16)

            def means(i, first=False):
                for b in range(LOT):
                    n = i * LOT + b
                    if not first:
                        pe.wait_ge(xc_done, n - LOT + 1)
                        if row:
                            pe.wait_ge(bank_free, n - LOT + 1)
                    nc.tensor.matmul(ps[:, b, 0:CHUNK], core.mean_w[:, :], X[:, chunk(n)],
                                     start=True, stop=True).then_inc(mean_done, 1)

            def body(i, last):
                if not last:
                    means(i + 1)
                for b in range(LOT):
                    n = i * LOT + b
                    pe.wait_ge(sq_done, n + 1)
                    pe.wait_ge(std_done, i + 1)
                    for t in range(TPC):
                        mm = nc.tensor.matmul(ps[:, BANK_V, b * TPC + t:b * TPC + t + 1], sq[:, b, t * TILE:(t + 1) * TILE],
                                              core.mean_w[:, 0:1], start=True, stop=True)
                    mm.then_inc(var_done, 1)
                for b in range(LOT):
                    n = i * LOT + b
                    pe.wait_ge(diag_done, n + 1)
                    pe.wait_ge(xn_done, n + (LOT, 1, 1, 2)[b])
                    nc.tensor.matmul(spread(b), core.ones[:, :],
                                     diag[:, b, :, :].rearrange("p t k -> p (t k)"),
                                     start=True, stop=True).then_inc(spread_done, 1)
                if row:
                    for b in range(LOT):
                        n = i * LOT + b
                        pe.wait_ge(xs_done, n + 1)
                        if not last:
                            pe.wait_ge(xc_done, n + LOT + 1)
                        for t in range(TPC):
                            mm = nc.tensor.matmul(ps[:, b, t * row:(t + 1) * row],
                                                  xs[:, b, t * TILE:(t + 1) * TILE], w[:, :],
                                                  start=True, stop=True)
                        mm.then_inc(rows_done, 1)
            lots(pe, means, body)

        @block.vector
        def _(dve):
            dve.sem_inc(rstd_done, 1)
            dve.sem_inc(xn_done, LOT)

            def centre(i, first=False):
                for b in range(LOT):
                    n = i * LOT + b
                    dve.wait_ge(mean_done, n + 1)
                    nc.vector.tensor_tensor(XN[:, chunk(n)], X[:, chunk(n)], ps[:, b, 0:CHUNK],
                                            ALU.subtract).then_inc(xc_done, 1)

            def body(i, last):
                if not last:
                    centre(i + 1)
                dve.wait_ge(std_done, i + 2)
                dve.wait_ge(spread_done, (i + 1) * LOT)
                dve.reciprocal(rstd[:, :, :], std[:, :, :]).then_inc(rstd_done, 1)
                for b in range(LOT):
                    n = i * LOT + b
                    dve.wait_ge(rstd_done, i + 2)
                    nc.vector.tensor_tensor(
                        diag[:, b, :, :],
                        core.ident[:, :].rearrange("p (a k) -> p a k", a=1).to_broadcast([128, TPC, TILE]),
                        rstd[:, b, :].rearrange("p (t a) -> p t a", a=1).to_broadcast([128, TPC, TILE]),
                        ALU.mult).then_inc(diag_done, 1)
                for b in range(LOT):
                    n = i * LOT + b
                    dve.wait_ge(xc_done, n + 1)
                    dve.wait_ge(spread_done, n + 1 + LOT)
                    nc.vector.tensor_tensor(XN[:, chunk(n)], XN[:, chunk(n)], spread(b),
                                            ALU.mult).then_inc(xn_done, 1)
            lots(dve, centre, body)

        @block.gpsimd
        def _(pool):
            pool.sem_inc(spread_done, LOT)

            def squares(i, first=False):
                for b in range(LOT):
                    n = i * LOT + b
                    pool.wait_ge(xc_done, n + 1)
                    if not first:
                        pool.wait_ge(var_done, n - LOT + 1)
                    pool.tensor_tensor(sq[:, b, :], XN[:, chunk(n)], XN[:, chunk(n)],
                                       ALU.mult).then_inc(sq_done, 1)

            def body(i, last):
                if not last:
                    squares(i + 1)
            lots(pool, squares, body)

        @block.scalar
        def _(act):
            act.sem_inc(bank_free, LOT)
            act.sem_inc(std_done, 1)
            if rows_dma:
                act.sem_inc(rows_free, LOT)

            def body(i, last):
                act.wait_ge(var_done, (i + 1) * LOT)
                act.wait_ge(rstd_done, i + 1)
                nc.scalar.activation(std[:, :, :].rearrange("p b t -> p (b t)"), ps[:, BANK_V, 0:LOT * TPC], ACT.Sqrt,
                                     bias=core.eps[:, eps_col:eps_col + 1]).then_inc(std_done, 1)
                if row:
                    for b in range(LOT):
                        n = i * LOT + b
                        act.wait_ge(xn_done, n + 1 + LOT)
                        nc.scalar.activation(xs[:, b, :], XN[:, chunk(n)], ACT.Copy).then_inc(xs_done, 1)
                    for b in range(LOT):
                        n = i * LOT + b
                        act.wait_ge(rows_done, n + 1)
                        src = ps[:, b, 0:TPC * row].rearrange("p (t r) -> p t r", t=TPC)
                        if rows_dma:
                            act.wait_ge(rows_free, n + 1)
                            nc.scalar.activation(rows[:, b, :, :], src, ACT.Copy).then_inc(rows_out, 1)
                            act.wait_ge(rows_out, n + 1)
                            act.sem_inc(bank_free, 1)
                        else:
                            tiles = slice(n * TPC, (n + 1) * TPC) if last else bass.ds(n * TPC, TPC)
                            nc.scalar.activation(rows_to[:, tiles, :], src, ACT.Copy).then_inc(bank_free, 1)
            lots(act, lambda i, first: None, body)


def attention(core, p):
    nc, X, XN, ps = core.nc, core.X, core.XN, core.psum
    EPS = 1e-5
    RING = 6
    BLOCKS = TILE // DK
    PARTS = 3
    M0 = (BLOCKS - 1) * DK
    UNITS = 2 * CPI
    with ExitStack() as ctx:
        sem = lambda n: core.semaphore(ctx, f"at_{n}")
        sb = lambda n, s, d=F32: ctx.enter_context(nc.sbuf_tensor(f"at_{n}", s, d))
        w_f, w_g, w_h = sb("w_f", [128, BLOCKS, DK]), sb("w_g", [128, BLOCKS, DK]), sb("w_h", [128, D])
        fg_par = sb("fg_par", [128, 2, 5])
        h_par = sb("h_par", [128, 5, D])
        fg_inv, fg_shift = sb("fg_inv", [128, 2]), sb("fg_shift", [128, 2])
        h_inv, h_shift = sb("h_inv", [128, D]), sb("h_shift", [128, D])
        minus = sb("minus", [128, 2, 3])
        stack1, stack2 = sb("stack1", [128, 2, PIX], BF16), sb("stack2", [128, 2, PIX], BF16)
        feat, rest = sb("feat", [128, 2, CHUNK]), sb("rest", [128, 2, CHUNK])
        part1, part2 = sb("part1", [128, 2, CHUNK], BF16), sb("part2", [128, 2, CHUNK], BF16)
        hT = sb("hT", [128, TPI, D])
        probs = sb("probs", [128, RING, CHUNK])
        xi = probs
        assert RING * CHUNK == PIX
        xi_tile = lambda j: xi[:, j // TPC, j % TPC * TILE:(j % TPC + 1) * TILE]
        psum_rows = sb("den", [128, 2, CHUNK])
        mx, nmax = sb("mx", [128, TPI, 2]), sb("nmax", [128, TPI])
        m_parts, m_wide = sb("m_parts", [128, PARTS, TPI], BF16), sb("m_wide", [128, PARTS * TPI])
        mrow = sb("mrow", [PARTS * TPI, TILE], BF16)
        att = sb("att", [128, CHUNK])
        w_in, par, xi_ready, fg_mm, fg_out, h_mm, h_out = map(sem, (
            "w_in", "par", "xi_ready", "fg_mm", "fg_out", "h_mm", "h_out"))
        s_mm, s_max, nmaxT, mrow_done, mrow_in, made = map(sem, (
            "s_mm", "s_max", "nmaxT", "mrow", "mrow_in", "made"))
        st_mm, exp_done, pv_done, add_done, o_done, o_free, steps, m_steps = map(sem, (
            "st_mm", "exp", "pv", "add", "o_done", "o_free", "steps", "m_steps"))
        rest_done, part2_done, stacked, split_done, m_zero = map(sem, (
            "rest", "part2", "stacked", "split", "m_zero"))
        var_ready, sd_ready = sem("var_ready"), sem("sd_ready")
        turns = sem("turns")
        M_STEPS = 2 * PARTS + 1
        block = ctx.enter_context(nc.Block())

        @block.sync
        def _(sp):
            for r in range(BLOCKS):
                sp.dma_start(w_f[:, r, :], p["w_f"]).then_inc(w_in, 16)
                sp.dma_start(w_g[:, r, :], p["w_g"]).then_inc(w_in, 16)
                for k, which in enumerate("fg"):
                    for j, q in enumerate(("b", "gamma", "beta", "mean", "var")):
                        sp.dma_start(fg_par[r * DK:(r + 1) * DK, k, j:j + 1],
                                     p[f"{q}_{which}"].rearrange("(c a) -> c a", a=1)).then_inc(w_in, 16)
            sp.dma_start(w_h[:, :], p["w_h"]).then_inc(w_in, 16)
            for j, q in enumerate(("b", "gamma", "beta", "mean", "var")):
                sp.dma_start(h_par[:, j, :], p[f"{q}_h"].rearrange("(a c) -> a c", a=1)
                             .to_broadcast([128, D])).then_inc(w_in, 16)
            sp.wait_ge(w_in, 16 * (12 * BLOCKS + 6))
            with sp.Fori(0, IMAGES) as i:
                sp.wait_ge(mrow_done, i + 1)
                for k in range(PARTS):
                    sp.dma_start(stack2[M0 + k:M0 + k + 1, 1, :].rearrange("a (t n) -> a t n", t=TPI),
                                 mrow[k * TPI:(k + 1) * TPI, :]).then_inc(mrow_in, 16)
            sp.wait_ge(mrow_in, 16 * PARTS * IMAGES)

        @block.tensor
        def _(pe):
            pe.wait_ge(w_in, 16 * (12 * BLOCKS + 6))
            pe.wait_ge(par, 1)
            with pe.Fori(0, IMAGES) as i:
                pe.wait_ge(o_free, CPI * i + 2)
                pe.wait_ge(xi_ready, i + 1)
                for c in range(CPI):
                    for k, w in enumerate((w_f, w_g)):
                        q = 2 * c + k
                        if q >= 4:
                            pe.wait_ge(fg_out, UNITS * i + q - 3)
                        nc.tensor.matmul(ps[:, q % 4, 0:CHUNK], w[:, :, :].rearrange("p r c -> p (r c)"),
                                         xi[:, c, :], start=True, stop=True).then_inc(fg_mm, 1)
                    if c >= 3:
                        pe.wait_ge(h_out, CPI * i + c - 2)
                    for t in range(TPC):
                        out = ps[:, 4 + c % 3, t * TILE:(t + 1) * TILE]
                        nc.tensor.matmul(out, xi_tile(c * TPC + t), w_h[:, :], start=True, stop=False)
                        mm = nc.tensor.matmul(out, core.mean_w[:, :], h_shift[:, :], start=False, stop=True)
                    mm.then_inc(h_mm, 1)
                pe.wait_ge(h_out, CPI * (i + 1))
                pe.wait_ge(m_zero, i + 1)
                pe.wait_ge(split_done, UNITS * (i + 1) + 2)
                pe.wait_ge(stacked, UNITS * (i + 1))
                for t in range(TPI):
                    for k in range(2):
                        q = 2 * t + k
                        if q >= 2:
                            pe.wait_ge(s_max, 2 * TPI * i + q - 1)
                        for n, stack in enumerate((stack1, stack2)):
                            for c in range(3):
                                mm = nc.tensor.matmul(ps[:, 3 * k + c, 0:CHUNK],
                                                      stack[:, 1, t * TILE:(t + 1) * TILE],
                                                      stack[:, 0, (3 * k + c) * CHUNK:(3 * k + c + 1) * CHUNK],
                                                      start=n == 0, stop=n == 1)
                        mm.then_inc(s_mm, 1)
                pe.wait_ge(m_steps, M_STEPS * (i + 1))
                pe.sem_inc(turns, 1)
                nc.tensor.transpose(ps[0:PARTS * TPI, 6, 0:TILE], m_wide[:, :], core.ident[:, :]).then_inc(nmaxT, 1)
                pe.wait_ge(mrow_in, 16 * PARTS * (i + 1))
                pe.sem_inc(turns, 1)
                with pe.Fori(0, CPI // 2) as cc:
                    for par2 in range(2):
                        c = 2 * cc + par2
                        r = i * CPI + c
                        LAG = 2
                        pe.wait_ge(o_free, r + 1)
                        for j in range(TPI + LAG):
                            if j < TPI:
                                pe.wait_ge(exp_done, r * TPI + j + 1)
                                for n, stack in enumerate((stack1, stack2)):
                                    mm = nc.tensor.matmul(ps[:, j % 3, 0:CHUNK],
                                                          stack[:, 0, j * TILE:(j + 1) * TILE],
                                                          stack[:, 1, bass.ds(c * CHUNK, CHUNK)],
                                                          start=n == 0, stop=n == 1)
                                mm.then_inc(st_mm, 1)
                            if j >= LAG:
                                k = j - LAG
                                pe.wait_ge(exp_done, r * TPI + k + 1 + 3)
                                nc.tensor.matmul(ps[:, 3 + 2 * par2, 0:CHUNK], hT[:, k, :], probs[:, k % RING, :],
                                                 start=k == 0, stop=k == TPI - 1).then_inc(pv_done, 1)
                        pe.wait_ge(add_done, (r + 1) * TPI + RING)
                        nc.tensor.matmul(ps[:, 4 + 2 * par2, 0:CHUNK], core.ones[:, :], psum_rows[:, par2, :],
                                         start=True, stop=True).then_inc(o_done, 1)

        @block.scalar
        def _(act):
            act.sem_inc(exp_done, 3)
            act.wait_ge(var_ready, 2)
            for inv in (fg_inv, h_inv):
                act.activation(inv[:, :], inv[:, :], ACT.Sqrt).then_inc(sd_ready, 1)
            act.wait_ge(par, 1)
            with act.Fori(0, IMAGES) as i:
                act.wait_ge(o_free, CPI * i + 2)
                act.activation(xi[:, :, :].rearrange("p r c -> p (r c)"), XN[:, bass.ds(i * PIX, PIX)],
                               ACT.Copy).then_inc(xi_ready, 1)
                for q in range(UNITS + 1):
                    c, k = q // 2, q % 2
                    if q < UNITS:
                        act.wait_ge(fg_mm, UNITS * i + q + 1)
                        act.wait_ge(split_done, UNITS * i + q + 1)
                        for dst in (feat, part1):
                            ins = act.activation(dst[:, q % 2, :], ps[:, q % 4, 0:CHUNK], ACT.Relu,
                                                 bias=fg_shift[:, k:k + 1], scale=fg_inv[:, k:k + 1])
                        ins.then_inc(fg_out, 1)
                    if q >= 1:
                        act.wait_ge(rest_done, UNITS * i + q)
                        act.activation(part2[:, (q - 1) % 2, :], rest[:, (q - 1) % 2, :],
                                       ACT.Copy).then_inc(part2_done, 1)
                    if q % 2 == 1:
                        act.wait_ge(h_mm, CPI * i + c + 1)
                        act.activation(hT[:, c * TPC:(c + 1) * TPC, :],
                                       ps[:, 4 + c % 3, 0:CHUNK].rearrange("p (t o) -> p t o", t=TPC),
                                       ACT.Relu).then_inc(h_out, 1)
                act.wait_ge(nmaxT, i + 1)
                act.activation(mrow[:, :], ps[0:PARTS * TPI, 6, 0:TILE], ACT.Copy).then_inc(mrow_done, 1)
                with act.Fori(0, CPI) as c:
                    r = i * CPI + c
                    for j in range(TPI):
                        act.wait_ge(st_mm, r * TPI + j + 1)
                        act.wait_ge(pv_done, r * TPI + j + 1)
                        act.wait_ge(add_done, r * TPI + j + 1)
                        act.activation(probs[:, j % RING, :], ps[:, j % 3, 0:CHUNK],
                                       ACT.Exp).then_inc(exp_done, 1)

        @block.gpsimd
        def _(pool):
            pool.sem_inc(pv_done, RING)
            pool.memset(stack2[M0:TILE, 0, :], 0.0).then_inc(made, 1)
            pool.wait_ge(made, 1)
            pool.memset(stack2[M0:M0 + PARTS, 0, :], 1.0).then_inc(made, 1)
            for k, per_block in enumerate((((0, 0, -1, -1), (0, -1, -1, 0), (0, -1, 0, 0)),
                                           ((0, -1, 0, -1), (-1, 0, -1, 0), (-1, 0, -1, 0)))):
                for s, signs in enumerate(per_block):
                    for r, v in enumerate(signs):
                        pool.memset(minus[r * DK:(r + 1) * DK, k, s:s + 1], float(v)).then_inc(made, 1)
            pool.wait_ge(made, 2 + 6 * BLOCKS)

        @block.vector
        def _(dve):
            st = Steps(dve, steps)
            dve.sem_inc(add_done, RING)
            dve.sem_inc(split_done, 2)
            dve.wait_ge(w_in, 16 * (12 * BLOCKS + 6))
            sets = ((fg_inv[:, :], fg_shift[:, :], lambda j: fg_par[:, :, j]),
                    (h_inv[:, :], h_shift[:, :], lambda j: h_par[:, j, :]))
            for inv, shift, q in sets:
                dve.tensor_scalar(inv, q(4), EPS, None, ALU.add).then_inc(var_ready, 1)
            dve.wait_ge(sd_ready, 2)
            for inv, shift, q in sets:
                st(dve.reciprocal(inv, inv))
                st(dve.tensor_tensor(inv, inv, q(1), ALU.mult))
                st(dve.tensor_tensor(shift, q(3), inv, ALU.mult))
                st(dve.tensor_tensor(shift, q(2), shift, ALU.subtract))
                st(dve.tensor_tensor(q(0), q(0), inv, ALU.mult))
                st(dve.tensor_tensor(shift, shift, q(0), ALU.add))
            st(dve.tensor_tensor(w_h[:, :], w_h[:, :], h_inv[:, :], ALU.mult))
            dve.wait_ge(made, 2 + 6 * BLOCKS)
            dve.sem_inc(o_free, 2)
            dve.sem_inc(par, 1)

            def third(i, q):
                c, k = q // 2, q % 2
                dve.wait_ge(part2_done, UNITS * i + q + 1)
                dve.wait_ge(rest_done, UNITS * i + q + 1)
                dve.scalar_tensor_tensor(out=stack2[0:M0, k, c * CHUNK:(c + 1) * CHUNK], in0=part2[0:M0, q % 2, :],
                                         scalar=minus[0:M0, k, 2:3], in1=rest[0:M0, q % 2, :],
                                         op0=ALU.mult, op1=ALU.add).then_inc(split_done, 1)

            with dve.Fori(0, IMAGES) as i:
                dve.wait_ge(o_free, CPI * i + 2)
                dve.memset(stack2[M0:TILE, 1, :], 0.0).then_inc(m_zero, 1)
                for q in range(UNITS + 1):
                    if q < UNITS:
                        c, k = q // 2, q % 2
                        dve.wait_ge(fg_out, UNITS * i + q + 1)
                        if q >= 2:
                            dve.wait_ge(split_done, UNITS * i + q + 1)
                        for s, out in ((1, rest[:, q % 2, :]), (0, stack1[:, k, c * CHUNK:(c + 1) * CHUNK])):
                            dve.scalar_tensor_tensor(out=out, in0=part1[:, q % 2, :], scalar=minus[:, k, s:s + 1],
                                                     in1=feat[:, q % 2, :], op0=ALU.mult,
                                                     op1=ALU.add).then_inc(rest_done if s else stacked, 1)
                    if q >= 1:
                        third(i, q - 1)
                for t in range(TPI):
                    for k in range(2):
                        q = 2 * t + k
                        dve.wait_ge(s_mm, 2 * TPI * i + q + 1)
                        dve.tensor_reduce(mx[:, t, k:k + 1], ps[:, 3 * k:3 * k + 3, 0:CHUNK], AX.XY,
                                          ALU.max).then_inc(s_max, 1)
                dve.wait_ge(s_max, 2 * TPI * (i + 1))
                ms = Steps(dve, m_steps, M_STEPS * i)
                ms(dve.tensor_reduce(nmax[:, :], mx[:, :, :], AX.X, ALU.max, negate=True))
                for k in range(PARTS):
                    ms(dve.tensor_copy(m_parts[:, k, :], nmax[:, :]))
                    if k < PARTS - 1:
                        ms(dve.tensor_tensor(nmax[:, :], nmax[:, :], m_parts[:, k, :], ALU.subtract))
                ms(dve.tensor_copy(m_wide[:, :], m_parts[:, :, :].rearrange("p k t -> p (k t)")))
                assert ms.n == M_STEPS
                dve.sem_inc(turns, 1)
                with dve.Fori(0, CPI // 2) as cc:
                    for par2 in range(2):
                        c = 2 * cc + par2
                        r = i * CPI + c
                        total = psum_rows[:, par2, :]
                        for j in range(TPI):
                            dve.wait_ge(exp_done, r * TPI + j + 1 + 3)
                            if j == 0:
                                dve.tensor_copy(total, probs[:, 0, :]).then_inc(add_done, 1)
                            else:
                                dve.wait_ge(add_done, r * TPI + j + RING)
                                dve.tensor_tensor(total, total, probs[:, j % RING, :],
                                                  ALU.add).then_inc(add_done, 1)
                        dve.wait_ge(o_done, r + 1)
                        at = Steps(dve, steps, st.n + r * 3)
                        here = bass.ds(i * PIX + c * CHUNK, CHUNK)
                        at(dve.reciprocal(att[:, :], ps[:, 4 + 2 * par2, 0:CHUNK]))
                        at(dve.tensor_tensor(att[:, :], att[:, :], ps[:, 3 + 2 * par2, 0:CHUNK], ALU.mult))
                        at(dve.tensor_tensor(att[:, :], att[:, :], XN[:, here], ALU.mult))
                        dve.tensor_tensor(X[:, here], X[:, here], att[:, :], ALU.add).then_inc(o_free, 1)


def pick_two(nc, dve, st, val, n, first, second, key, best, rank, m1, m2):
    wide = lambda a: a.rearrange("p (t e) -> p t e", e=1).to_broadcast([128, TILES, n])
    ranks = rank.rearrange("p (t e) -> p t e", t=1).to_broadcast([128, TILES, n])
    for mask, m in ((first, m1), (second, m2)):
        st(dve.tensor_reduce(m, val, AX.X, ALU.max))
        st(dve.tensor_tensor(key, val, wide(m), ALU.is_equal))
        st(dve.tensor_tensor(key, key, ranks, ALU.mult))
        st(dve.tensor_reduce(best, key, AX.X, ALU.max))
        st(dve.tensor_tensor(mask, key, wide(best), ALU.is_equal))
        if mask is first:
            st(dve.tensor_scalar(key, mask, -BIG, None, ALU.mult))
            st(dve.tensor_tensor(val, val, key, ALU.add))


def route_by_logits(core, logits, gates):
    nc, n = core.nc, 8
    with ExitStack() as ctx:
        sb = lambda k, s: ctx.enter_context(nc.sbuf_tensor(f"r0_{k}", s, F32))
        first, key = sb("first", [128, TILES, n]), sb("key", [128, TILES, n])
        best, m1, m2, total = (sb(k, [128, TILES]) for k in ("best", "m1", "m2", "total"))
        rank = sb("rank", [128, n])
        steps, shifted, exped = (core.semaphore(ctx, f"r0_{k}") for k in ("steps", "shifted", "exped"))
        block = ctx.enter_context(nc.Block())
        wide = lambda a: a.rearrange("p (t e) -> p t e", e=1).to_broadcast([128, TILES, n])

        @block.scalar
        def _(act):
            act.wait_ge(shifted, 1)
            act.activation(logits[:, :, :], logits[:, :, :], ACT.Exp).then_inc(exped, 1)

        @block.vector
        def _(dve):
            st = Steps(dve, steps)
            for e in range(n):
                st.mark(dve.memset(rank[:, e:e + 1], float(n - e)))
            st(dve.tensor_reduce(m1[:, :], logits[:, :, :], AX.X, ALU.max))
            dve.tensor_tensor(logits[:, :, :], logits[:, :, :], wide(m1[:, :]), ALU.subtract).then_inc(shifted, 1)
            dve.wait_ge(exped, 1)
            st(dve.tensor_reduce(total[:, :], logits[:, :, :], AX.X, ALU.add))
            st(dve.reciprocal(total[:, :], total[:, :]))
            st(dve.tensor_tensor(logits[:, :, :], logits[:, :, :], wide(total[:, :]), ALU.mult))
            pick_two(nc, dve, st, logits[:, :, :], n, first[:, :, :], gates[:, :, :], key[:, :, :], best[:, :],
                     rank[:, :], m1[:, :], m2[:, :])
            st(dve.tensor_tensor(total[:, :], m1[:, :], m2[:, :], ALU.add))
            st(dve.tensor_scalar(total[:, :], total[:, :], 1e-12, None, ALU.max))
            st(dve.reciprocal(total[:, :], total[:, :]))
            for mask, m in ((first, m1), (gates, m2)):
                st(dve.tensor_tensor(m[:, :], m[:, :], total[:, :], ALU.mult))
                st(dve.tensor_tensor(mask[:, :, :], mask[:, :, :], wide(m[:, :]), ALU.mult))
            st(dve.tensor_tensor(gates[:, :, :], gates[:, :, :], first[:, :, :], ALU.add))


def experts(core, name, n_exp, gates, w1_d, b1_d, w2_d, b2_d, residual):
    nc, X, XN, ps = core.nc, core.X, core.XN, core.psum
    U = 8
    HALVES = U // n_exp
    CREDIT = 2 * HALVES
    with ExitStack() as ctx:
        sem = lambda k: core.semaphore(ctx, f"{name}_{k}")
        sb = lambda k, s: ctx.enter_context(nc.sbuf_tensor(f"{name}_{k}", s, F32))
        w1, w2, b1 = sb("w1", [128, U, 128]), sb("w2", [128, U, 128]), sb("b1", [128, U])
        b2, sel = sb("b2", [128, D]), sb("sel", [128, n_exp, 128])
        gt, gT = sb("gt", [128, 2, TPC, 128]), sb("gT", [128, 2, CHUNK])
        hid, hg = sb("hid", [128, 2, CHUNK]), sb("hg", [128, 2, CHUNK])
        w_in, made, gt_done, gT_mm, gT_out, b_mm, h_mm, h_act, hg_done, o_mm, x_half, x_done, w2_mm = map(sem, (
            "w_in", "made", "gt", "gT_mm", "gT_out", "b_mm", "h_mm", "h_act", "hg", "o_mm", "x_half", "x_done",
            "w2_mm"))
        gated, turns = sem("gated"), sem("turns")
        block = ctx.enter_context(nc.Block())
        BANK_T, BANK_B, BANK_H, BANK_O = 0, 1, 3, 5

        @block.sync
        def _(sp):
            sp.wait_ge(made, 4)
            sp.dma_start(w1[:, :, :].rearrange("p (e a) f -> p e (a f)", e=n_exp), w1_d).then_inc(w_in, 16)
            sp.dma_start(w2[:, :, :], w2_d).then_inc(w_in, 16)
            sp.dma_start(b1[:, :], b1_d).then_inc(w_in, 16)
            sp.dma_start(b2[0:n_exp, :], b2_d).then_inc(w_in, 16)
            sp.wait_ge(w_in, 64)

        @block.gpsimd
        def _(pool):
            pool.memset(sel[:, :, :], 0.0).then_inc(made, 1)
            pool.wait_ge(made, 1)
            pool.affine_select(out=sel[:, :, :], in_=sel[:, :, :], compare_op=ALU.not_equal, fill=1.0, base=0,
                               pattern=[[-1, n_exp], [0, 128]], channel_multiplier=1).then_inc(made, 1)
            pool.memset(gt[:, :, :, :], 0.0).then_inc(made, 1)
            pool.memset(b2[:, :], 0.0).then_inc(made, 1)
            pool.sem_inc(gated, 2)
            pool.wait_ge(made, 4)
            with pool.Fori(0, CHUNKS // 2) as i:
                for b in range(2):
                    n = 2 * i + b
                    pool.wait_ge(gated, n + 1)
                    pool.sem_inc(turns, 1)
                    pool.tensor_copy(gt[:, b, :, 0:n_exp], gates[:, bass.ds(n * TPC, TPC), :]).then_inc(gt_done, 1)

        @block.tensor
        def _(pe):
            pe.wait_ge(w_in, 64)
            pe.wait_ge(made, 4)
            with pe.Fori(0, CHUNKS // 2) as i:
                for b in range(2):
                    n = 2 * i + b
                    pe.wait_ge(gt_done, n + 1)
                    pe.wait_ge(gT_out, n + 1)
                    for t in range(TPC):
                        tr = nc.tensor.transpose(ps[:, BANK_T, t * TILE:(t + 1) * TILE], gt[:, b, t, :],
                                                 core.ident[:, :])
                    tr.then_inc(gT_mm, 1)
                    pe.wait_ge(gT_out, n + 2)
                    pe.wait_ge(x_done, n + 1)
                    pe.sem_inc(gated, 1)
                    out = ps[:, BANK_O + b, 0:CHUNK]
                    nc.tensor.matmul(out, b2[:, :], gT[:, b, :], start=True, stop=False)
                    for u in range(U + 1):
                        q = n * U + u
                        if u < U:
                            if u % HALVES == 0:
                                e = u // HALVES
                                pe.wait_ge(hg_done, (n * n_exp + e + 1) * HALVES)
                                nc.tensor.matmul(ps[:, BANK_B + e % 2, 0:CHUNK], sel[:, e, :], gT[:, b, :],
                                                 start=True, stop=True).then_inc(b_mm, 1)
                            pe.wait_ge(h_act, q + 1)
                            nc.tensor.matmul(ps[:, BANK_H + u % 2, 0:CHUNK], w1[:, u, :],
                                             XN[:, bass.ds(n * CHUNK, CHUNK)],
                                             start=True, stop=True).then_inc(h_mm, 1)
                        if u >= 1:
                            v = u - 1
                            pe.wait_ge(hg_done, q + CREDIT)
                            mm = nc.tensor.matmul(out, w2[:, v, :], hg[:, v % 2, :], start=False, stop=v == U - 1)
                            mm.then_inc(w2_mm, 1)

        @block.scalar
        def _(act):
            act.wait_ge(w_in, 64)
            act.sem_inc(gT_out, 1)
            act.sem_inc(h_act, 2)
            with act.Fori(0, CHUNKS // 2) as i:
                for b in range(2):
                    n = 2 * i + b
                    act.wait_ge(gT_mm, n + 1)
                    act.wait_ge(w2_mm, n * U + 2)
                    act.activation(gT[:, b, :], ps[:, BANK_T, 0:CHUNK], ACT.Copy).then_inc(gT_out, 1)
                    for u in range(U):
                        q = n * U + u
                        act.wait_ge(h_mm, q + 1)
                        act.wait_ge(hg_done, q - 1 + CREDIT)
                        act.activation(hid[:, u % 2, :], ps[:, BANK_H + u % 2, 0:CHUNK], ACT.Gelu,
                                       bias=b1[:, u:u + 1]).then_inc(h_act, 1)

        @block.vector
        def _(dve):
            dve.sem_inc(hg_done, CREDIT)
            dve.sem_inc(x_done, 2)
            dve.sem_inc(w2_mm, 2)
            with dve.Fori(0, CHUNKS // 2) as i:
                for b in range(2):
                    n = 2 * i + b
                    for u in range(U):
                        q = n * U + u
                        dve.wait_ge(h_act, q + 1 + 2)
                        dve.wait_ge(b_mm, n * n_exp + u // HALVES + 1)
                        dve.wait_ge(w2_mm, q + 1)
                        nc.vector.tensor_tensor(hg[:, u % 2, :], hid[:, u % 2, :],
                                                ps[:, BANK_B + u // HALVES % 2, 0:CHUNK],
                                                ALU.mult).then_inc(hg_done, 1)
                    here = bass.ds(n * CHUNK, CHUNK)
                    dve.wait_ge(w2_mm, (n + 1) * U + 2)
                    if residual:
                        nc.vector.tensor_tensor(X[:, here], X[:, here], XN[:, here], ALU.add).then_inc(x_half, 1)
                        dve.wait_ge(x_half, n + 1)
                    nc.vector.tensor_tensor(X[:, here], X[:, here], ps[:, BANK_O + b, 0:CHUNK],
                                            ALU.add).then_inc(x_done, 1)


def expert_phase_0(core, p):
    nc = core.nc
    with ExitStack() as ctx:
        logits = ctx.enter_context(nc.sbuf_tensor("logits", [128, TILES, 8], F32))
        gates = ctx.enter_context(nc.sbuf_tensor("gates0", [128, TILES, 8], F32))
        normalise(core, "ln2", 1, p["router_w"], 8, logits)
        route_by_logits(core, logits, gates)
        experts(core, "e0", 8, gates, p["w1"].rearrange("e d f -> d e f"), p["b1"],
                p["w2"].rearrange("e f c -> f e c"), p["b2"], True)


PAD = 64


CORNERS = (0, 1, SIDE, SIDE + 1)


def offsets(core, p, om, x_dram, table):
    nc, X, XN, ps = core.nc, core.X, core.XN, core.psum
    K3 = 3 * TAPS
    WIDE = SIDE + 2
    ROWS = CHUNK // SIDE
    with ExitStack() as ctx:
        sem = lambda k: core.semaphore(ctx, f"of_{k}")
        sb = lambda k, s: ctx.enter_context(nc.sbuf_tensor(f"of_{k}", s, F32))
        w, bias = sb("w", [128, TAPS, K3]), sb("bias", [K3, 1])
        zeros, zeros_made = sb("zeros", [PAD, D]), sem("zeros")
        padded, cols = sb("padded", [128, 2, WIDE, WIDE]), sb("cols", [K3, 2, CHUNK])
        w_in, zeroed, pad_done, conv_mm, conv_out, t_mm, t_out, saved, turns = map(sem, (
            "w_in", "zeroed", "pad", "conv_mm", "conv_out", "t_mm", "t_out", "saved", "turns"))
        block = ctx.enter_context(nc.Block())

        @block.sync
        def _(sp):
            sp.dma_start(w[:, :, :], p["w_off"]).then_inc(w_in, 16)
            sp.dma_start(bias[:, :], p["b_off"].rearrange("(c a) -> c a", a=1)).then_inc(w_in, 16)
            for b in range(IMAGES):
                sp.dma_start(x_dram[b, :, :], X[:, b * PIX:(b + 1) * PIX]).then_inc(saved, 16)
            sp.wait_ge(zeros_made, 1)
            ends = [(c, lo, hi) for c, back in enumerate(CORNERS)
                    for lo, hi in ((0, PAD - back), (T + PAD - back, T + PAD)) if hi > lo]
            for c, lo, hi in ends:
                sp.dma_start(table[lo:hi, c * D:(c + 1) * D], zeros[0:hi - lo, :]).then_inc(saved, 16)
            sp.wait_ge(w_in, 32)
            sp.wait_ge(saved, 16 * (IMAGES + len(ends)))

        @block.gpsimd
        def _(pool):
            pool.memset(zeros[:, :], 0.0).then_inc(zeros_made, 1)
            pool.memset(padded[:, :, :, :], 0.0).then_inc(zeroed, 1)
            pool.wait_ge(zeroed, 1)
            with pool.Fori(0, IMAGES // 2) as i:
                for b in range(2):
                    img = 2 * i + b
                    pool.wait_ge(conv_mm, (img + 1) * CPI)
                    pool.sem_inc(turns, 1)
                    pool.tensor_copy(padded[:, b, 1:1 + SIDE, 1:1 + SIDE],
                                     XN[:, bass.ds(img * PIX, PIX)].rearrange("p (y x) -> p y x", x=SIDE)
                                     ).then_inc(pad_done, 1)

        @block.tensor
        def _(pe):
            pe.sem_inc(conv_mm, 2 * CPI)
            pe.wait_ge(w_in, 32)
            with pe.Fori(0, IMAGES // 2) as i:
                for b in range(2):
                    img = 2 * i + b
                    pe.wait_ge(pad_done, img + 1)
                    for c in range(CPI + 1):
                        n = img * CPI + c
                        if c < CPI:
                            pe.wait_ge(conv_out, n + 1)
                            for k in range(TAPS):
                                y = ROWS * c + k // 3
                                mm = nc.tensor.matmul(ps[0:K3, c % 2, 0:CHUNK], w[:, k, :],
                                                      padded[:, b, y:y + ROWS, k % 3:k % 3 + SIDE],
                                                      start=k == 0, stop=k == TAPS - 1)
                            mm.then_inc(conv_mm, 1)
                        if c >= 1:
                            m = n - 1
                            pe.wait_ge(conv_out, m + 1 + 2)
                            pe.wait_ge(t_out, m + 1)
                            pe.sem_inc(turns, 1)
                            for t in range(TPC):
                                tr = nc.tensor.transpose(ps[:, 2 + (c - 1) % 2, t * K3:(t + 1) * K3],
                                                         cols[:, (c - 1) % 2, t * TILE:(t + 1) * TILE],
                                                         core.ident[0:K3, 0:K3])
                            tr.then_inc(t_mm, 1)

        @block.scalar
        def _(act):
            act.sem_inc(conv_out, 2)
            act.sem_inc(t_mm, 2)
            act.wait_ge(w_in, 32)
            with act.Fori(0, IMAGES) as img:
                for c in range(CPI):
                    n = img * CPI + c
                    act.wait_ge(conv_mm, n + 1 + 2 * CPI)
                    act.wait_ge(t_mm, n + 1)
                    act.activation(cols[:, c % 2, :], ps[0:K3, c % 2, 0:CHUNK], ACT.Identity,
                                   bias=bias[:, :]).then_inc(conv_out, 1)

        @block.vector
        def _(dve):
            dve.sem_inc(t_out, 2)
            with dve.Fori(0, IMAGES) as img:
                for c in range(CPI):
                    n = img * CPI + c
                    dve.wait_ge(t_mm, n + 1 + 2)
                    dve.tensor_copy(om[:, bass.ds(n * TPC, TPC), :],
                                    ps[:, 2 + c % 2, 0:TPC * K3].rearrange("p (t k) -> p t k", t=TPC)
                                    ).then_inc(t_out, 1)


def sample_points(core, om, index, corner_w):
    nc = core.nc
    N = TILES * TAPS
    TOP = SIDE - 2
    with ExitStack() as ctx:
        sem = lambda k: core.semaphore(ctx, f"sp_{k}")
        free = core.XN
        part = lambda k: free[:, k * N:(k + 1) * N]
        grid = lambda k: part(k).rearrange("p (t k) -> p t k", k=TAPS)
        point, low, over, near, far = (grid(k) for k in range(5))
        wy, wx, mask, base = [grid(5), grid(6)], [grid(7), grid(8)], grid(9), grid(10)
        flat = free[:, 11 * N:11 * N + 4 * TILES].rearrange("p (a t) -> p a t", a=4)
        row, col, pix, start = (flat[:, k, :] for k in range(4))
        cmp = free[:, 0:TILES * (SIDE - 1)].rearrange("p (t m) -> p t m", m=SIDE - 1)
        marks = ctx.enter_context(nc.sbuf_tensor("sp_marks", [128, SIDE - 1], F32))
        ints = ctx.enter_context(nc.sbuf_tensor("sp_ints", [128, TILES, TAPS], I32))
        small = ctx.enter_context(nc.sbuf_tensor("sp_small", [128, 2 * TILES + SIDE - 1], I32))
        made, steps, masked = sem("made"), sem("steps"), sem("masked")
        block = ctx.enter_context(nc.Block())

        @block.gpsimd
        def _(pool):
            pool.iota(small[:, 0:TILES], pattern=[[0, IMAGES], [TILE, TPI]], base=0,
                      channel_multiplier=1).then_inc(made, 1)
            pool.iota(small[:, TILES:2 * TILES], pattern=[[PIX, IMAGES], [0, TPI]], base=PAD,
                      channel_multiplier=0).then_inc(made, 1)
            pool.iota(small[:, 2 * TILES:], pattern=[[SIDE, SIDE - 1]], base=SIDE,
                      channel_multiplier=0).then_inc(made, 1)

        @block.scalar
        def _(act):
            act.activation(mask, om[:, :, 2 * TAPS:], ACT.Sigmoid).then_inc(masked, 1)

        @block.vector
        def _(dve):
            st = Steps(dve, steps)
            wide = lambda a: a.rearrange("p (t e) -> p t e", e=1)
            dve.wait_ge(made, 3)
            st.mark(dve.tensor_copy(pix, small[:, 0:TILES]))
            st.mark(dve.tensor_copy(start, small[:, TILES:2 * TILES]))
            st(dve.tensor_copy(marks[:, :], small[:, 2 * TILES:]))
            st(dve.tensor_tensor(cmp, wide(pix).to_broadcast([128, TILES, SIDE - 1]),
                                 marks[:, :].rearrange("p (t m) -> p t m", t=1).to_broadcast([128, TILES, SIDE - 1]),
                                 ALU.is_ge))
            st(dve.tensor_reduce(row, cmp, AX.X, ALU.add))
            st(dve.scalar_tensor_tensor(out=col, in0=row, scalar=-float(SIDE), in1=pix, op0=ALU.mult, op1=ALU.add))
            for axis, at, weights in ((0, row, wy), (1, col, wx)):
                for k in range(TAPS):
                    shift = float((k // 3 if axis == 0 else k % 3) - 1)
                    st.mark(dve.tensor_scalar(point[:, :, k:k + 1], wide(at), shift, None, ALU.add))
                st.done()
                st(dve.tensor_tensor(point, point, om[:, :, axis * TAPS:(axis + 1) * TAPS], ALU.add))
                st(dve.tensor_scalar(near, point, 0.0, float(TOP), ALU.max, ALU.min))
                st(dve.tensor_copy(ints[:, :, :], near))
                st(dve.tensor_copy(low, ints[:, :, :]))
                st(dve.tensor_tensor(over, low, near, ALU.is_gt))
                st(dve.tensor_tensor(low, low, over, ALU.subtract))
                st(dve.tensor_tensor(near, point, low, ALU.subtract))
                st(dve.tensor_scalar(far, near, 1.0, None, ALU.subtract))
                for k, dist in enumerate((near, far)):
                    st(dve.scalar_tensor_tensor(out=over, in0=dist, scalar=-1.0, in1=dist, op0=ALU.mult, op1=ALU.max))
                    st(dve.tensor_scalar(over, over, -1.0, 1.0, ALU.mult, ALU.add))
                    st(dve.tensor_scalar(weights[k], over, 0.0, None, ALU.max))
                if axis == 0:
                    st(dve.tensor_scalar(base, low, float(SIDE), None, ALU.mult))
                else:
                    st(dve.tensor_tensor(base, base, low, ALU.add))
            st(dve.tensor_tensor(base, base, wide(start).to_broadcast([128, TILES, TAPS]), ALU.add))
            st(dve.tensor_copy(index[:, :, :], base))
            dve.wait_ge(masked, 1)
            for a in range(2):
                st(dve.tensor_tensor(wy[a], wy[a], mask, ALU.mult))
                for b in range(2):
                    st(dve.tensor_tensor(corner_w[:, :, :, 2 * a + b], wy[a], wx[b], ALU.mult))


def deform(core, p, table, index, corner_w):
    nc, Y, ps = core.nc, core.X, core.psum
    RING = 3
    with ExitStack() as ctx:
        sem = lambda k: core.semaphore(ctx, f"df_{k}")
        sb = lambda k, s, d=F32: ctx.enter_context(nc.sbuf_tensor(f"df_{k}", s, d))
        BUFS = 3
        patches = core.XN[:, 0:BUFS * TAPS * 4 * D].rearrange("p (b k c) -> p b k c", b=BUFS, k=TAPS)
        ibuf = sb("ibuf", [128, BUFS, TAPS], I32)
        at = BUFS * TAPS * 4 * D
        diag = core.XN[:, at:at + RING * 4 * TILE].rearrange("p (r c n) -> p r c n", r=RING, c=4)
        at += RING * 4 * TILE
        blended = core.XN[:, at:at + RING * 3 * TILE].rearrange("p (r k n) -> p r k n", r=RING, k=3)
        w, bias = sb("w", [128, TAPS, D]), sb("bias", [128, 1])
        w_in, i_done, diag_done, tap_mm, blend_out, y_mm, y_out, turns = map(sem, (
            "w_in", "index", "diag", "tap_mm", "blend_out", "y_mm", "y_out", "turns"))
        in_ = [sem(f"in{b}") for b in range(BUFS)]
        block = ctx.enter_context(nc.Block())

        @block.sync
        def _(sp):
            sp.dma_start(w[:, :, :], p["weight"]).then_inc(w_in, 16)
            sp.dma_start(bias[:, :], p["bias"].rearrange("(c a) -> c a", a=1)).then_inc(w_in, 16)
            sp.wait_ge(w_in, 32)

        @block.gpsimd
        def _(pool):
            with pool.Fori(0, TILES // BUFS) as i:
                for b in range(BUFS):
                    t = BUFS * i + b
                    pool.wait_ge(tap_mm, TAPS * (t + 1))
                    pool.sem_inc(turns, 1)
                    pool.tensor_copy(ibuf[:, b, :], index[:, bass.ds(t, 1), :]).then_inc(i_done, 1)
                    pool.wait_ge(i_done, t + 1)
                    pool.sem_inc(turns, 1)
                    for k in range(TAPS):
                        pool.indirect_dma_start(
                            out=patches[:, b, k, :], out_offset=None, in_=table,
                            in_offset=bass.IndirectOffsetOnAxis(ap=ibuf[:, b, k:k + 1], axis=0)).then_inc(in_[b], 16)

        @block.tensor
        def _(pe):
            pe.sem_inc(tap_mm, BUFS * TAPS)
            pe.wait_ge(w_in, 32)
            with pe.Fori(0, TILES // (2 * BUFS)) as i:
                for u in range(2 * BUFS):
                    t = 2 * BUFS * i + u
                    b, o = u % BUFS, u % 2
                    pe.wait_ge(in_[b], 16 * TAPS * (2 * i + u // BUFS + 1))
                    for g in range(4):
                        if g < 3:
                            pe.wait_ge(blend_out, 3 * t + g + 1)
                            for k in range(3 * g, 3 * g + 3):
                                pe.wait_ge(diag_done, TAPS * t + k + 1)
                                for c in range(4):
                                    mm = nc.tensor.matmul(ps[:, g, (k % 3) * TILE:(k % 3 + 1) * TILE],
                                                          patches[:, b, k, c * D:(c + 1) * D], diag[:, k % RING, c, :],
                                                          start=c == 0, stop=c == 3)
                                mm.then_inc(tap_mm, 1)
                        if g == 0:
                            pe.wait_ge(y_out, t + 1)
                        else:
                            pe.wait_ge(blend_out, 3 * t + g + 3)
                            for k in range(3 * g - 3, 3 * g):
                                mm = nc.tensor.matmul(ps[:, 3 + o, 0:TILE], w[:, k, :],
                                                      blended[:, g - 1, k % 3, :],
                                                      start=k == 0, stop=k == TAPS - 1)
                    mm.then_inc(y_mm, 1)

        @block.scalar
        def _(act):
            act.sem_inc(blend_out, 3)
            act.sem_inc(y_out, 2)
            act.wait_ge(w_in, 32)
            with act.Fori(0, TILES // 2) as i:
                for b in range(2):
                    t = 2 * i + b
                    for g in range(3):
                        act.wait_ge(tap_mm, TAPS * t + 3 * g + 3 + BUFS * TAPS)
                        act.wait_ge(y_mm, t + 1)
                        act.activation(blended[:, g, :, :], ps[:, g, 0:3 * TILE].rearrange("p (k n) -> p k n", k=3),
                                       ACT.Copy).then_inc(blend_out, 1)
                    act.wait_ge(y_mm, t + 2)
                    act.activation(Y[:, bass.ds(t * TILE, TILE)], ps[:, 3 + b, 0:TILE], ACT.Identity,
                                   bias=bias[:, :]).then_inc(y_out, 1)

        @block.vector
        def _(dve):
            dve.sem_inc(y_mm, 1)
            with dve.Fori(0, TILES // 2) as i:
                for b in range(2):
                    t = 2 * i + b
                    for k in range(TAPS):
                        dve.wait_ge(tap_mm, TAPS * t + k + 1 + BUFS * TAPS - RING)
                        dve.tensor_tensor(
                            diag[:, k % RING, :, :],
                            core.ident[:, :].rearrange("p (c n) -> p c n", c=1).to_broadcast([128, 4, TILE]),
                            corner_w[:, bass.ds(t, 1), k, :].rearrange("p a (c n) -> p (a c) n", n=1)
                            .to_broadcast([128, 4, TILE]),
                            ALU.mult).then_inc(diag_done, 1)


def batch_norm(core, p, x_dram):
    nc, Y, ps = core.nc, core.X, core.psum
    LOT = 4
    with ExitStack() as ctx:
        sem = lambda k: core.semaphore(ctx, f"bn_{k}")
        sb = lambda k, s: ctx.enter_context(nc.sbuf_tensor(f"bn_{k}", s, F32))
        stats, agg, par = sb("stats", [128, CHUNKS, 6]), sb("agg", [128, 2]), sb("par", [128, 2])
        scale, shift, old = sb("scale", [128, 1]), sb("shift", [128, 1]), sb("old", [128, LOT, CHUNK])
        p_in, counted, steps, var_done, sd_done, ready, relu_done, x_done = map(sem, (
            "p_in", "counted", "steps", "var", "sd", "ready", "relu", "x"))
        old_in = [sem(f"old{b}") for b in range(LOT)]
        block = ctx.enter_context(nc.Block())

        @block.sync
        def _(sp):
            for j, q in enumerate(("gamma", "beta")):
                sp.dma_start(par[:, j:j + 1], p[q].rearrange("(c a) -> c a", a=1)).then_inc(p_in, 16)
            sp.wait_ge(p_in, 32)
            with sp.Fori(0, CHUNKS // LOT) as i:
                for b in range(LOT):
                    n = LOT * i + b
                    sp.wait_ge(x_done, n + 1)
                    sp.dma_start(old[:, b, :], x_dram[:, bass.ds(n * CHUNK, CHUNK)]).then_inc(old_in[b], 16)

        @block.vector
        def _(dve):
            st = Steps(dve, steps)
            dve.sem_inc(x_done, LOT)
            with dve.Fori(0, CHUNKS) as n:
                dve.bn_stats(stats[:, bass.ds(n, 1), :], Y[:, bass.ds(n * CHUNK, CHUNK)]).then_inc(counted, 1)
            dve.wait_ge(counted, CHUNKS)
            st(dve.bn_aggr(agg[:, :], stats[:, :, :]))
            dve.tensor_scalar(scale[:, :], agg[:, 1:2], 1e-5, None, ALU.add).then_inc(var_done, 1)
            dve.wait_ge(sd_done, 1)
            dve.wait_ge(p_in, 32)
            st(dve.reciprocal(scale[:, :], scale[:, :]))
            st(dve.tensor_tensor(scale[:, :], scale[:, :], par[:, 0:1], ALU.mult))
            st(dve.tensor_tensor(shift[:, :], scale[:, :], agg[:, 0:1], ALU.mult))
            dve.tensor_tensor(shift[:, :], par[:, 1:2], shift[:, :], ALU.subtract).then_inc(ready, 1)
            with dve.Fori(0, CHUNKS // LOT) as i:
                for b in range(LOT):
                    n = LOT * i + b
                    here = bass.ds(n * CHUNK, CHUNK)
                    dve.wait_ge(relu_done, n + 1)
                    dve.wait_ge(old_in[b], 16 * (i + 1))
                    dve.tensor_tensor(Y[:, here], Y[:, here], old[:, b, :], ALU.add).then_inc(x_done, 1)

        @block.scalar
        def _(act):
            act.wait_ge(var_done, 1)
            act.activation(scale[:, :], scale[:, :], ACT.Sqrt).then_inc(sd_done, 1)
            act.wait_ge(ready, 1)
            with act.Fori(0, CHUNKS) as n:
                here = bass.ds(n * CHUNK, CHUNK)
                act.activation(Y[:, here], Y[:, here], ACT.Relu, bias=shift[:, :],
                               scale=scale[:, :]).then_inc(relu_done, 1)


def deform_phase(core, p):
    nc = core.nc
    table = nc.dram_tensor("corner_table", (T + PAD, 4 * D), F32, kind="Internal").ap()
    x_dram = nc.dram_tensor("x_saved", (D, T), F32, kind="Internal").ap()
    by_image = x_dram.rearrange("c (b n) -> b c n", b=IMAGES)

    def stores(n):
        for c, back in enumerate(CORNERS):
            yield table[bass.ds(n * CHUNK + PAD - back, CHUNK), c * D:(c + 1) * D] \
                .rearrange("(t p) c -> p t c", p=TILE)

    with ExitStack() as ctx:
        sb = lambda k, s, d=F32: ctx.enter_context(nc.sbuf_tensor(f"dp_{k}", s, d))
        om = sb("om", [128, TILES, 3 * TAPS])
        normalise(core, "ln3", 0, None, D, None, stores)
        offsets(core, p, om, by_image, table)
        index, corner_w = sb("index", [128, TILES, TAPS], I32), sb("corner_w", [128, TILES, TAPS, 4])
        sample_points(core, om, index, corner_w)
        deform(core, p, table, index, corner_w)
    batch_norm(core, p, x_dram)


EDGES = 524288
WIDTH = EDGES // 128
RUN = 128
RUNS = EDGES // RUN
BLOCK = 128 * RUN
BLOCKS = RUNS // 128
DST_BIAS = 256
ID_BITS = 15
HEADS, GE = 4, 4
HF = HEADS * GE
SRC_ROW = HEADS + HF
STATE = HEADS + HEADS + HF
LEAK = 0.2


def sort_edges(core, edges, d, zeroed):
    nc, ps = core.nc, core.psum
    K = [core.XN[:, k * WIDTH:(k + 1) * WIDTH] for k in range(2)]
    W_BITS, BITS = WIDTH.bit_length() - 1, EDGES.bit_length() - 1
    half = lambda buf, j: buf.rearrange("p (u two l) -> p u two l", two=2, l=1 << j)
    with ExitStack() as ctx:
        sem = lambda k: core.semaphore(ctx, f"so_{k}")
        sign, bits = (ctx.enter_context(nc.sbuf_tensor(f"so_{k}", [128, 8], t)) for k, t in (("sign", F32), ("bits", I32)))
        loaded, lanes, steps, sorted_, t_mm, t_out, out_ready, stored = map(sem, (
            "loaded", "lanes", "steps", "sorted", "t_mm", "t_out", "out_ready", "stored"))
        block = ctx.enter_context(nc.Block())
        n_swaps = 2 * (BITS - W_BITS)
        ZEROS = 4096
        cleared = sem("cleared")
        zeros = ctx.enter_context(nc.sbuf_tensor("so_zeros", [128, ZEROS], F32))

        @block.gpsimd
        def _(pool):
            pool.iota(bits[:, :], pattern=[[0, 8]], base=0, channel_multiplier=1).then_inc(lanes, 1)
            pool.memset(zeros[:, :], 0.0).then_inc(lanes, 1)

        final, outs, cur_of_swap = [], {}, []

        @block.vector
        def _(dve):
            st = Steps(dve, steps)
            dve.wait_ge(lanes, 1)
            for b in range(7):
                st.mark(dve.tensor_scalar(bits[:, b:b + 1], bits[:, b:b + 1], b, 1, ALU.logical_shift_right,
                                          ALU.bitwise_and))
            st.done()
            st(dve.tensor_copy(sign[:, 0:7], bits[:, 0:7]))
            st(dve.tensor_scalar(sign[:, 0:7], sign[:, 0:7], -2.0, 1.0, ALU.mult, ALU.add))
            dve.wait_ge(loaded, 32)
            src, dst = K[0].bitcast(I32), K[1].bitcast(I32)
            st(dve.tensor_scalar(dst, dst, DST_BIAS, None, ALU.add))
            st(dve.tensor_scalar(dst, dst, ID_BITS, None, ALU.logical_shift_left))
            st(dve.tensor_tensor(src, src, dst, ALU.bitwise_or))
            cur, swaps = 0, 0

            def negate(k):
                part = half(K[cur], k)[:, :, 1, :]
                st(dve.tensor_scalar(part, part, -1.0, None, ALU.mult))

            def by_lane(b):
                st(dve.tensor_scalar(K[cur], K[cur], sign[:, b:b + 1], None, ALU.mult))

            def compare(j):
                nonlocal cur
                a, b = half(K[cur], j), half(K[1 - cur], j)
                st.mark(dve.tensor_tensor(b[:, :, 0, :], a[:, :, 0, :], a[:, :, 1, :], ALU.min))
                st(dve.tensor_tensor(b[:, :, 1, :], a[:, :, 0, :], a[:, :, 1, :], ALU.max))
                cur = 1 - cur

            def swap():
                nonlocal cur, swaps
                dve.sem_inc(sorted_, 1)
                swaps += 1
                cur_of_swap.append(cur)
                cur = 1 - cur
                dve.wait_ge(t_out, 8 * swaps)

            for k in range(1, BITS + 1):
                if k < W_BITS:
                    negate(k)
                elif k < BITS:
                    by_lane(k - W_BITS)
                if k > W_BITS:
                    swap()
                    for j in reversed(range(k - W_BITS)):
                        compare(j)
                    swap()
                for j in reversed(range(min(k, W_BITS))):
                    compare(j)
                if k < W_BITS:
                    negate(k)
                elif k < BITS:
                    by_lane(k - W_BITS)
            assert swaps == n_swaps - 0
            keys = K[cur]
            final.append(keys)
            dve.sem_inc(out_ready, 1)
            ikeys = keys.bitcast(I32)
            at = 2 * WIDTH
            source = core.XN[:, at:at + WIDTH].bitcast(I32)
            same = core.XN[:, at + WIDTH:at + 2 * WIDTH]
            target = K[1 - cur].bitcast(I32)
            at += 2 * WIDTH
            R = WIDTH // RUN
            first, last, run_target = (core.XN[:, at + k * R:at + (k + 1) * R] for k in range(3))
            by_run = lambda a: a.rearrange("p (r f) -> p r f", f=RUN)
            one = lambda a: a.rearrange("p (r f) -> p r f", f=1)
            st(dve.tensor_scalar(source, ikeys, (1 << ID_BITS) - 1, None, ALU.bitwise_and))
            dve.tensor_scalar(source, source, T - 1, None, ALU.min).then_inc(out_ready, 1)
            st(dve.tensor_scalar(target, ikeys, ID_BITS, None, ALU.logical_shift_right))
            st(dve.tensor_tensor(same[:, 1:WIDTH], target[:, 1:WIDTH], target[:, 0:WIDTH - 1], ALU.is_equal))
            dve.memset(by_run(same)[:, :, 0:1], 0.0).then_inc(out_ready, 1)
            st.mark(dve.tensor_copy(one(first), by_run(keys)[:, :, 0:1]))
            st(dve.tensor_copy(one(last), by_run(keys)[:, :, RUN - 1:RUN]))
            dve.sem_inc(out_ready, 1)
            dve.tensor_scalar(one(run_target.bitcast(I32)), by_run(target)[:, :, 0:1], -DST_BIAS, T - 1, ALU.add,
                              ALU.min).then_inc(out_ready, 1)
            outs.update(source=source, same=same, first=first, last=last, run_target=run_target.bitcast(I32))

        @block.tensor
        def _(pe):
            for n, cur in enumerate(cur_of_swap):
                pe.wait_ge(sorted_, n + 1)
                for q in range(8):
                    m = 8 * n + q
                    if m >= 4:
                        pe.wait_ge(t_out, m - 3)
                    for t in range(4):
                        tr = nc.tensor.transpose(ps[:, q % 4, t * 128:(t + 1) * 128],
                                                 K[cur][:, (4 * q + t) * 128:(4 * q + t + 1) * 128], core.ident[:, :])
                    tr.then_inc(t_mm, 1)

        @block.scalar
        def _(act):
            for n, cur in enumerate(cur_of_swap):
                for q in range(8):
                    act.wait_ge(t_mm, 8 * n + q + 1)
                    act.activation(K[1 - cur][:, q * 512:(q + 1) * 512], ps[:, q % 4, :], ACT.Copy).then_inc(t_out, 1)

        @block.sync
        def _(sp):
            for k in range(2):
                sp.dma_start(K[k].bitcast(I32), edges[k, :].rearrange("(p f) -> p f", p=128)).then_inc(loaded, 16)
            sp.wait_ge(lanes, 2)
            n = 0
            for table in zeroed:
                rows, width = table.shape
                per = rows * width // 128
                flat = table.rearrange("r c -> (r c)").rearrange("(p f) -> p f", p=128)
                for at in range(0, per, ZEROS):
                    size = min(ZEROS, per - at)
                    sp.dma_start(flat[:, at:at + size], zeros[:, 0:size]).then_inc(cleared, 16)
                    n += 16
            sp.wait_ge(cleared, n)
            sp.wait_ge(loaded, 32)
            sp.wait_ge(out_ready, 1)
            ordered = lambda a: a.rearrange("(p f) -> p f", p=128)
            sp.dma_start(ordered(d["keys"]), final[0]).then_inc(stored, 16)
            sp.wait_ge(out_ready, 5)
            sp.dma_start(ordered(d["source"]), outs["source"]).then_inc(stored, 16)
            sp.dma_start(ordered(d["same"]), outs["same"]).then_inc(stored, 16)
            sp.dma_start(ordered(d["first"]), outs["first"]).then_inc(stored, 16)
            sp.dma_start(ordered(d["last"]), outs["last"]).then_inc(stored, 16)
            sp.dma_start(ordered(d["run_target"]), outs["run_target"]).then_inc(stored, 16)
            sp.wait_ge(stored, 16 * 6)


def gather(core, name, table, width, index, tiles, lot, consume, sems=()):
    nc = core.nc
    lots = tiles // lot
    assert lots * lot == tiles
    with ExitStack() as ctx:
        sem = lambda k: core.semaphore(ctx, f"{name}_{k}")
        ibuf = ctx.enter_context(nc.sbuf_tensor(f"{name}_ibuf", [128, 2, lot], I32))
        rows = ctx.enter_context(nc.sbuf_tensor(f"{name}_rows", [128, 2, lot, width], F32))
        i_done, used, turns = sem("index"), sem("used"), sem("turns")
        in_ = [sem("in0"), sem("in1")]
        block = ctx.enter_context(nc.Block())

        @block.gpsimd
        def _(pool):
            def fetch(b, n):
                pool.wait_ge(i_done, n + 1)
                pool.wait_ge(used, n + 1)
                pool.sem_inc(turns, 1)
                for k in range(lot):
                    pool.indirect_dma_start(out=rows[:, b, k, :], out_offset=None, in_=table,
                                            in_offset=bass.IndirectOffsetOnAxis(ap=ibuf[:, b, k:k + 1], axis=0)
                                            ).then_inc(in_[b], 16)

            if lots > 1:
                with pool.Fori(0, lots // 2) as i:
                    for b in range(2):
                        fetch(b, 2 * i + b)
            if lots % 2:
                fetch(0, lots - 1)

        @block.vector
        def _(dve):
            dve.sem_inc(used, 2)

            def indices(b, n):
                dve.tensor_copy(ibuf[:, b, :], index[:, bass.ds(n * lot, lot)]).then_inc(i_done, 1)

            def take(b, n, times):
                dve.wait_ge(in_[b], 16 * lot * times)
                consume(dve, n, rows[:, b, :, :], used)

            if lots > 1:
                with dve.Fori(0, lots // 2) as i:
                    for b in range(2):
                        indices(b, 2 * i + b)
                    for b in range(2):
                        take(b, 2 * i + b, i + 1)
            if lots % 2:
                indices(0, lots - 1)
                take(0, lots - 1, lots // 2 + 1)


def find_starts(core, d, start, end):
    nc, ps = core.nc, core.psum
    N = TILES + 1
    S1 = RUNS // 64
    with ExitStack() as ctx:
        sb = lambda k, s, t=F32: ctx.enter_context(nc.sbuf_tensor(f"fs_{k}", s, t))
        least, iblk = sb("least", [128, N], I32), sb("iblk", [128, N], I32)
        blk, cnt, pos = sb("blk", [128, N]), sb("cnt", [128, N]), sb("pos", [128, N])
        next_lane, wrap = sb("next_lane", [128, 128]), sb("wrap", [128, 128])
        samples = core.XN[:, 0:RUNS]
        below = core.XN[:, RUNS:RUNS + N * S1].rearrange("p (t s) -> p t s", t=N)
        wide = lambda a, n: a.rearrange("p (t s) -> p t s", s=1).to_broadcast([128, a.shape[1], n])
        key = least[:, :].bitcast(F32)
        with ExitStack() as c2:
            sem = lambda k: core.semaphore(c2, f"fs_{k}")
            made, loaded, steps = sem("made"), sem("loaded"), sem("steps")
            block = c2.enter_context(nc.Block())

            @block.sync
            def _(sp):
                sp.dma_start(samples, d["first"].rearrange("(a f) -> a f", a=1).to_broadcast([128, RUNS])
                             ).then_inc(loaded, 16)
                sp.wait_ge(loaded, 16)

            @block.gpsimd
            def _(pool):
                pool.iota(least[:, :], pattern=[[TILE, N]], base=DST_BIAS, channel_multiplier=1).then_inc(made, 1)
                pool.memset(next_lane[:, :], 0.0).then_inc(made, 1)
                pool.memset(wrap[:, :], 0.0).then_inc(made, 1)
                pool.wait_ge(made, 3)
                pool.affine_select(out=next_lane[:, :], in_=next_lane[:, :], compare_op=ALU.not_equal, fill=1.0,
                                   base=-1, pattern=[[-1, 128]], channel_multiplier=1).then_inc(made, 1)
                pool.affine_select(out=wrap[:, :], in_=wrap[:, :], compare_op=ALU.not_equal, fill=1.0,
                                   base=127, pattern=[[-1, 128]], channel_multiplier=128).then_inc(made, 1)

            @block.vector
            def _(dve):
                st = Steps(dve, steps)
                dve.wait_ge(made, 3)
                st(dve.tensor_scalar(least[:, :], least[:, :], ID_BITS, None, ALU.logical_shift_left))
                dve.wait_ge(loaded, 16)
                coarse = samples.rearrange("p (a s f) -> p a s f", a=1, f=64)[:, :, :, 0].to_broadcast([128, N, S1])
                st(dve.tensor_tensor(below, coarse, wide(key, S1), ALU.is_lt))
                st(dve.tensor_reduce(blk[:, :], below, AX.X, ALU.add))
                st(dve.tensor_scalar(blk[:, :], blk[:, :], -1.0, 0.0, ALU.add, ALU.max))
                st(dve.tensor_copy(iblk[:, :], blk[:, :]))

        def count(width, lot):
            compared = core.semaphore(ctx, f"fs_compared{width}")

            def consume(dve, n, rows, used):
                here = bass.ds(n * lot, lot)
                dve.tensor_tensor(rows, rows, wide(key[:, here], width), ALU.is_lt).then_inc(compared, 1)
                dve.wait_ge(compared, n + 1)
                dve.tensor_reduce(cnt[:, here], rows, AX.X, ALU.add).then_inc(used, 1)
            return consume

        def finer(name, factor, to_int):
            steps = core.semaphore(ctx, name)
            with nc.Block() as block:
                @block.vector
                def _(dve):
                    st = Steps(dve, steps)
                    out = blk if to_int else pos
                    st(dve.scalar_tensor_tensor(out=out[:, :], in0=blk[:, :], scalar=float(factor), in1=cnt[:, :],
                                                op0=ALU.mult, op1=ALU.add))
                    if to_int:
                        st(dve.tensor_scalar(blk[:, :], blk[:, :], -1.0, 0.0, ALU.add, ALU.max))
                        st(dve.tensor_copy(iblk[:, :], blk[:, :]))

        gather(core, "fs_g2", d["first"].rearrange("(r s) -> r s", s=64), 64, iblk, N, 5, count(64, 5))
        finer("fs_finer2", 64, True)
        gather(core, "fs_g3", d["keys"].rearrange("(r s) -> r s", s=RUN), RUN, iblk, N, 5, count(RUN, 5))
        finer("fs_finer3", RUN, False)

        with ExitStack() as c3:
            moved, copied = (core.semaphore(c3, f"fs_{k}") for k in ("moved", "copied"))
            pairs_out = core.semaphore(c3, "fs_pairs_out")
            block = c3.enter_context(nc.Block())

            @block.tensor
            def _(pe):
                nc.tensor.matmul(ps[:, 0, 0:TILES], next_lane[:, :], pos[:, 0:TILES], start=True, stop=False)
                nc.tensor.matmul(ps[:, 0, 0:TILES], wrap[:, :], pos[:, 1:N], start=False, stop=True).then_inc(moved, 1)

            @block.vector
            def _(dve):
                st = Steps(dve, copied)
                dve.tensor_copy(start[:, :], pos[:, 0:TILES])
                dve.wait_ge(moved, 1)
                st(dve.tensor_copy(end[:, :], ps[:, 0, 0:TILES]))
                st(dve.tensor_scalar(blk[:, 0:1], end[:, TILES - 1:TILES], float(2 * BLOCK - 1), None, ALU.add))
                st(dve.tensor_copy(iblk[:, 0:1], blk[:, 0:1]))
                st(dve.tensor_scalar(iblk[:, 0:1], iblk[:, 0:1], (2 * BLOCK).bit_length() - 1, None,
                                     ALU.logical_shift_right))
                st(dve.tensor_scalar(iblk[:, 0:1], iblk[:, 0:1], 1, None, ALU.max))

            @block.sync
            def _(sp):
                sp.wait_ge(copied, 5)
                sp.dma_start(d["pairs"].rearrange("(p a) -> p a", a=1), iblk[127:128, 0:1]).then_inc(pairs_out, 16)
                sp.wait_ge(pairs_out, 16)


def index_phase(core, edges, start, end, zeroed):
    nc = core.nc
    shapes = dict(keys=(EDGES, F32), source=(EDGES, I32), same=(EDGES, F32), first=(RUNS, F32), last=(RUNS, F32),
                  run_target=(RUNS, I32), pairs=(1, I32))
    d = {k: nc.dram_tensor(f"edge_{k}", (n,), t, kind="Internal").ap() for k, (n, t) in shapes.items()}
    sort_edges(core, edges, d, zeroed)
    find_starts(core, d, start, end)
    return d


class Carver:

    def __init__(self, buf, parts=128):
        self.buf, self.at, self.parts = buf, 0, parts

    def __call__(self, *shape):
        n = 1
        for k in shape:
            n *= k
        piece = self.buf[0:self.parts, self.at:self.at + n]
        self.at += n
        assert self.at <= self.buf.shape[1]
        names = "abcd"[:len(shape)]
        return piece if len(shape) == 1 else piece.rearrange(
            f"p ({' '.join(names)}) -> p {' '.join(names)}", **dict(zip(names[1:], shape[1:])))


def source_tables(core, p, t, feats, tgt_score, start, end, xn_dram):
    nc, XN = core.nc, core.XN
    LOT = 8
    with ExitStack() as ctx:
        sem = lambda k: core.semaphore(ctx, f"st_{k}")
        sb = lambda k, s, d=F32: ctx.enter_context(nc.sbuf_tensor(f"st_{k}", s, d))
        rows, prod = sb("rows", [128, TILES, SRC_ROW]), sb("prod", [128, TILES, HF])
        att = sb("att", [128, 2, HF])
        where, empty, place = sb("where", [128, TILES]), sb("empty", [128, TILES]), sb("place", [128, TILES], I32)
        ibuf, sbuf = sb("ibuf", [128, 2, LOT], I32), sb("sbuf", [128, 2, LOT, HEADS])
        loaded, steps, made, ready, stored, saved, turns, i_done, spare = map(sem, (
            "loaded", "steps", "made", "ready", "stored", "saved", "turns", "i_done", "spare"))
        freed = sem("freed")
        placed_in = [sem("placed0"), sem("placed1")]
        block = ctx.enter_context(nc.Block())

        @block.sync
        def _(sp):
            for k, q in enumerate(("att_src", "att_dst")):
                sp.dma_start(att[:, k, :], p[q].rearrange("(a h) e -> a (h e)", a=1).to_broadcast([128, HF])
                             ).then_inc(loaded, 16)
            for b in range(IMAGES):
                here = slice(b * PIX, (b + 1) * PIX)
                sp.dma_start(xn_dram[:, here], XN[:, here]).then_inc(saved, 16)
            sp.wait_ge(ready, 1)
            sp.dma_start(t["sources"].rearrange("(t p) c -> p t c", p=TILE), rows[:, :, :]).then_inc(stored, 16)
            sp.dma_start(t["targets"].rearrange("(t p) c -> p t c", p=TILE), tgt_score[:, :, :]).then_inc(stored, 16)
            sp.wait_ge(loaded, 32)
            sp.wait_ge(saved, 16 * IMAGES)
            sp.wait_ge(stored, 32)

        @block.gpsimd
        def _(pool):
            pool.iota(place[:, :], pattern=[[TILE, TILES]], base=EDGES, channel_multiplier=1).then_inc(made, 1)
            with pool.Fori(0, TILES // LOT // 2) as i:
                for b in range(2):
                    pool.wait_ge(i_done, 2 * i + b + 1)
                    pool.sem_inc(turns, 1)
                    for k in range(LOT):
                        pool.indirect_dma_start(
                            out=t["placed"], out_offset=bass.IndirectOffsetOnAxis(ap=ibuf[:, b, k:k + 1], axis=0),
                            in_=sbuf[:, b, k, :], in_offset=None).then_inc(placed_in[b], 16)
                for b in range(2):
                    pool.wait_ge(placed_in[b], 16 * LOT * (i + 1))
                    pool.sem_inc(freed, 1)

        @block.vector
        def _(dve):
            st = Steps(dve, steps)
            dve.sem_inc(freed, 2)
            dve.wait_ge(loaded, 32)
            h = feats[:, :, :]
            by_head = lambda x: x.rearrange("p t (h e) -> p t h e", h=HEADS)
            wide = lambda k: att[:, k, :].rearrange("p (t c) -> p t c", t=1).to_broadcast([128, TILES, HF])
            st.mark(dve.tensor_copy(rows[:, :, HEADS:], h))
            st(dve.tensor_tensor(prod[:, :, :], h, wide(0), ALU.mult))
            st(dve.tensor_reduce(rows[:, :, 0:HEADS], by_head(prod[:, :, :]), AX.X, ALU.add))
            st(dve.tensor_tensor(prod[:, :, :], h, wide(1), ALU.mult))
            dve.tensor_reduce(tgt_score[:, :, :], by_head(prod[:, :, :]), AX.X, ALU.add).then_inc(ready, 1)
            dve.wait_ge(ready, 1)
            dve.wait_ge(made, 1)
            st(dve.tensor_copy(where[:, :], place[:, :]))
            st(dve.tensor_tensor(empty[:, :], start[:, :], end[:, :], ALU.is_equal))
            st(dve.tensor_tensor(where[:, :], where[:, :], start[:, :], ALU.subtract))
            st(dve.tensor_tensor(where[:, :], where[:, :], empty[:, :], ALU.mult))
            st(dve.tensor_tensor(where[:, :], where[:, :], start[:, :], ALU.add))
            st(dve.tensor_copy(place[:, :], where[:, :]))
            with dve.Fori(0, TILES // LOT // 2) as i:
                for b in range(2):
                    n = 2 * i + b
                    here = bass.ds(n * LOT, LOT)
                    dve.wait_ge(freed, n + 1)
                    dve.tensor_copy(ibuf[:, b, :], place[:, here]).then_inc(spare, 1)
                    dve.wait_ge(spare, n + 1)
                    dve.tensor_copy(sbuf[:, b, :, :], tgt_score[:, here, :]).then_inc(i_done, 1)


def edge_states(core, d, t):
    nc = core.nc
    with ExitStack() as ctx:
        sem = lambda k: core.semaphore(ctx, f"es_{k}")
        sb = lambda k, s, d_=F32: ctx.enter_context(nc.sbuf_tensor(f"es_{k}", s, d_))
        carve = Carver(core.XN)
        G, A, L = carve(2, RUN, SRC_ROW), carve(2, RUN, HEADS), carve(2, RUN, STATE)
        tgt, top, e, w = (carve(HEADS, RUN) for _ in range(4))
        m, decay = carve(HEADS, RUN + 1), carve(HEADS, RUN)
        msg = carve(HF, RUN)
        same, reset = sb("same", [128, 2, RUN]), sb("reset", [128, RUN])
        ibuf, rbuf = sb("ibuf", [128, 2, RUN], I32), sb("rbuf", [128, 2], I32)
        steps, used, in_rows, act_in, act_out, l_done, turns, zero = map(sem, (
            "steps", "used", "in_rows", "act_in", "act_out", "l_done", "turns", "zero"))
        idx_in, edge_in, rows_in, first_in, l_out = ([sem(f"{k}{b}") for b in range(2)] for k in (
            "idx", "edge", "rows", "first", "l_out"))
        N_STEPS, l_free = 19, sem("l_free")
        block = ctx.enter_context(nc.Block())
        blocks = lambda a: a.rearrange("(s p f) -> p s f", p=128, f=RUN)
        of_run = d["run_target"].rearrange("(s p a) -> p s a", p=128, a=1)
        placed = t["placed"][0:EDGES, :].rearrange("(s p f) h -> p s f h", p=128, f=RUN)
        states = t["states"].rearrange("(s p f) c -> p s f c", p=128, f=RUN)
        ends = t["ends"].rearrange("(s p) c -> p s c", p=128)

        def pairs(eng):
            return eng.value_load(d["pairs"].rearrange("(p a) -> p a", a=1), min_val=1, max_val=BLOCKS // 2)


        @block.sync
        def _(sp):
            with sp.Fori(0, pairs(sp)) as i:
                for b in range(2):
                    s = 2 * i + b
                    one = bass.ds(s, 1)
                    sp.wait_ge(used, s + 1)
                    sp.dma_start(ibuf[:, b:b + 1, :], blocks(d["source"])[:, one, :]).then_inc(idx_in[b], 16)
                    sp.dma_start(rbuf[:, b:b + 1].rearrange("p (s a) -> p s a", a=1), of_run[:, one, :]
                                 ).then_inc(idx_in[b], 16)
                    sp.dma_start(same[:, b:b + 1, :], blocks(d["same"])[:, one, :]).then_inc(edge_in[b], 16)
                    sp.dma_start(A[:, b:b + 1, :, :], placed[:, one, :, :]).then_inc(edge_in[b], 16)

        @block.scalar
        def _(act):
            with act.Fori(0, pairs(act)) as i:
                for b in range(2):
                    s = 2 * i + b
                    for k, x in enumerate((w, decay)):
                        act.wait_ge(act_in, 2 * s + k + 1)
                        act.activation(x, x, ACT.Exp).then_inc(act_out, 1)
                    act.wait_ge(l_done, s + 1)
                    act.dma_start(states[:, bass.ds(s, 1), :, :], L[:, b:b + 1, :, :]).then_inc(l_out[b], 16)
                    act.dma_start(ends[:, bass.ds(s, 1), :], L[:, b:b + 1, RUN - 1, :]).then_inc(l_out[b], 16)
                    act.wait_ge(l_out[b], 32 * (i + 1))
                    act.sem_inc(l_free, 1)

        @block.gpsimd
        def _(pool):
            with pool.Fori(0, pairs(pool)) as i:
                for b in range(2):
                    s = 2 * i + b
                    pool.wait_ge(idx_in[b], 32 * (i + 1))
                    pool.wait_ge(edge_in[b], 32 * (i + 1))
                    pool.wait_ge(used, s + 1)
                    pool.sem_inc(turns, 1)
                    pool.indirect_dma_start(
                        out=A[:, b, 0, :], out_offset=None, in_=t["targets"],
                        in_offset=bass.IndirectOffsetOnAxis(ap=rbuf[:, b:b + 1], axis=0)).then_inc(first_in[b], 16)
                    for f in range(RUN):
                        pool.indirect_dma_start(
                            out=G[:, b, f, :], out_offset=None, in_=t["sources"],
                            in_offset=bass.IndirectOffsetOnAxis(ap=ibuf[:, b, f:f + 1], axis=0)
                            ).then_inc(rows_in[b], 16)

        @block.vector
        def _(dve):
            dve.memset(m, 0.0).then_inc(zero, 1)
            dve.sem_inc(used, 2)
            dve.sem_inc(l_free, 2)
            dve.wait_ge(zero, 1)
            with dve.Fori(0, pairs(dve)) as i:
                for b in range(2):
                    s = 2 * i + b
                    st = Steps(dve, steps, s * N_STEPS)
                    dve.wait_ge(edge_in[b], 32 * (i + 1))
                    st(dve.tensor_scalar(reset[:, :], same[:, b, :], -1.0, BIG, ALU.add, ALU.mult))
                    dve.wait_ge(first_in[b], 16 * (i + 1))
                    for h in range(HEADS):
                        st.mark(dve.tensor_tensor_scan(out=tgt[:, h, :], data0=same[:, b, :], data1=A[:, b, :, h],
                                                       initial=0.0, op0=ALU.mult, op1=ALU.add))
                    dve.wait_ge(rows_in[b], 16 * RUN * (i + 1))
                    for h in range(HEADS):
                        st.mark(dve.tensor_tensor_scan(out=top[:, h, :], data0=reset[:, :], data1=G[:, b, :, h],
                                                       initial=0.0, op0=ALU.add, op1=ALU.max))
                    st.done()
                    src = G[:, b, :, 0:HEADS].rearrange("p f h -> p h f")
                    st.mark(dve.tensor_tensor(top, top, tgt, ALU.add))
                    st(dve.tensor_tensor(e, src, tgt, ALU.add))
                    now, before = m[:, :, 1:], m[:, :, 0:RUN]
                    st.mark(dve.scalar_tensor_tensor(out=now, in0=top, scalar=LEAK, in1=top, op0=ALU.mult,
                                                     op1=ALU.max))
                    st(dve.scalar_tensor_tensor(out=e, in0=e, scalar=LEAK, in1=e, op0=ALU.mult, op1=ALU.max))
                    st.mark(dve.tensor_tensor(decay, before, now, ALU.subtract))
                    dve.tensor_tensor(w, e, now, ALU.subtract).then_inc(act_in, 1)
                    st.done()
                    resets = reset[:, :].rearrange("p (h f) -> p h f", h=1).to_broadcast([128, HEADS, RUN])
                    dve.tensor_tensor(decay, decay, resets, ALU.min).then_inc(act_in, 1)
                    dve.wait_ge(l_free, s + 1)
                    out = L[:, b, :, :]
                    st(dve.tensor_copy(out[:, :, 0:HEADS].rearrange("p f h -> p h f"), now))
                    dve.wait_ge(act_out, 2 * s + 2)
                    for h in range(HEADS):
                        st.mark(dve.tensor_tensor(
                            msg[:, h * GE:(h + 1) * GE, :],
                            G[:, b, :, HEADS + h * GE:HEADS + (h + 1) * GE].rearrange("p f e -> p e f"),
                            w[:, h, :].rearrange("p (e f) -> p e f", e=1).to_broadcast([128, GE, RUN]), ALU.mult))
                    assert st.n == N_STEPS
                    st.done()
                    for c in range(HEADS + HF):
                        h = c if c < HEADS else (c - HEADS) // GE
                        x = w[:, h, :] if c < HEADS else msg[:, c - HEADS, :]
                        scan = dve.tensor_tensor_scan(out=out[:, :, HEADS + c], data0=decay[:, h, :], data1=x,
                                                      initial=0.0, op0=ALU.mult, op1=ALU.add)
                    scan.then_inc(l_done, 1)
                    dve.wait_ge(l_done, s + 1)
                    dve.sem_inc(used, 1)


def stitch_runs(core, d, t):
    nc, ps = core.nc, core.psum
    ROWS = HEADS + HF
    with ExitStack() as ctx:
        sem = lambda k: core.semaphore(ctx, f"sr_{k}")
        sb = lambda k, s, d_=F32: ctx.enter_context(nc.sbuf_tensor(f"sr_{k}", s, d_))
        wide = Carver(core.XN, ROWS)
        top, val, m, decay = wide(RUNS), wide(RUNS), wide(RUNS + 1), wide(RUNS)
        first, last = sb("first", [ROWS, RUNS]), sb("last", [ROWS, RUNS])
        ends = sb("ends", [128, BLOCKS, STATE])
        tops = sb("tops", [128, BLOCKS, ROWS])
        out = sb("out", [128, BLOCKS, 2 * ROWS])
        loaded, ends_in, steps, tops_done, t_mm, t_out, act_in, act_out, done, b_mm, b_out, stored = map(sem, (
            "loaded", "ends_in", "steps", "tops", "t_mm", "t_out", "act_in", "act_out", "done", "b_mm", "b_out",
            "stored"))
        block = ctx.enter_context(nc.Block())

        @block.sync
        def _(sp):
            sp.dma_start(ends[:, :, :], t["ends"].rearrange("(s p) c -> p s c", p=128)).then_inc(ends_in, 16)
            for k, x in (("first", first), ("last", last)):
                sp.dma_start(x[:, :], d[k].rearrange("(a r) -> a r", a=1).to_broadcast([ROWS, RUNS])
                             ).then_inc(loaded, 16)
            sp.wait_ge(b_out, 2 * BLOCKS // 4)
            sp.dma_start(t["carry"].rearrange("(s p) c -> p s c", p=128), out[:, :, :]).then_inc(stored, 16)
            sp.wait_ge(stored, 16)
            sp.wait_ge(loaded, 32)
            sp.wait_ge(ends_in, 16)

        @block.vector
        def _(dve):
            st = Steps(dve, steps)
            dve.wait_ge(ends_in, 16)
            dve.tensor_copy(tops[:, :, 0:HEADS], ends[:, :, 0:HEADS]).then_inc(tops_done, 1)
            for h in range(HEADS):
                dve.tensor_copy(tops[:, :, HEADS + h * GE:HEADS + (h + 1) * GE],
                                ends[:, :, h:h + 1].to_broadcast([128, BLOCKS, GE])).then_inc(tops_done, 1)
            dve.wait_ge(loaded, 32)
            f, l = first[:, :].bitcast(I32), last[:, :].bitcast(I32)
            st.mark(dve.tensor_scalar(f, f, ID_BITS, None, ALU.logical_shift_right))
            st(dve.tensor_scalar(l, l, ID_BITS, None, ALU.logical_shift_right))
            st(dve.tensor_tensor(decay, f, l, ALU.is_equal))
            st(dve.tensor_tensor(m[:, 1:RUNS], f[:, 1:], l[:, 0:RUNS - 1], ALU.is_equal))
            st(dve.tensor_tensor(decay[:, 1:], decay[:, 1:], m[:, 1:RUNS], ALU.mult))
            st(dve.memset(decay[:, 0:1], 0.0))
            reset = first[:, :]
            st(dve.tensor_scalar(reset, decay, -1.0, BIG, ALU.add, ALU.mult))
            st(dve.memset(m[:, 0:1], 0.0))
            dve.wait_ge(t_out, 2 * BLOCKS // 4)
            st(dve.tensor_tensor_scan(out=m[:, 1:], data0=reset, data1=top, initial=0.0, op0=ALU.add, op1=ALU.max))
            st.mark(dve.tensor_tensor(top, top, m[:, 1:], ALU.subtract))
            st(dve.tensor_tensor(decay, m[:, 0:RUNS], m[:, 1:], ALU.subtract))
            dve.tensor_tensor(decay, decay, reset, ALU.min).then_inc(act_in, 1)
            dve.wait_ge(act_out, 2)
            st(dve.tensor_tensor(val, val, top, ALU.mult))
            dve.tensor_tensor_scan(out=top, data0=decay, data1=val, initial=0.0, op0=ALU.mult,
                                   op1=ALU.add).then_inc(done, 1)

        @block.tensor
        def _(pe):
            pe.wait_ge(tops_done, 1 + HEADS)
            for n in range(2 * BLOCKS // 4):
                k, q = divmod(n, BLOCKS // 4)
                if n >= 4:
                    pe.wait_ge(t_out, n - 3)
                for j in range(4):
                    x = (tops[:, 4 * q + j, :], ends[:, 4 * q + j, HEADS:])[k]
                    tr = nc.tensor.transpose(ps[0:ROWS, n % 4, j * 128:(j + 1) * 128], x, core.ident[:, :])
                tr.then_inc(t_mm, 1)
            pe.wait_ge(done, 1)
            for n in range(2 * BLOCKS // 4):
                k, q = divmod(n, BLOCKS // 4)
                x = (m[:, 1:], top)[k]
                if n >= 4:
                    pe.wait_ge(b_out, n - 3)
                for j in range(4):
                    tr = nc.tensor.transpose(ps[:, 4 + n % 4, j * ROWS:(j + 1) * ROWS],
                                             x[:, (4 * q + j) * 128:(4 * q + j + 1) * 128],
                                             core.ident[0:ROWS, 0:ROWS])
                tr.then_inc(b_mm, 1)

        @block.scalar
        def _(act):
            for n in range(2 * BLOCKS // 4):
                k, q = divmod(n, BLOCKS // 4)
                act.wait_ge(t_mm, n + 1)
                act.activation((top, val)[k][:, q * 512:(q + 1) * 512], ps[0:ROWS, n % 4, :],
                               ACT.Copy).then_inc(t_out, 1)
            act.wait_ge(act_in, 1)
            act.activation(top, top, ACT.Exp).then_inc(act_out, 1)
            act.activation(decay, decay, ACT.Exp).then_inc(act_out, 1)
            for n in range(2 * BLOCKS // 4):
                k, q = divmod(n, BLOCKS // 4)
                act.wait_ge(b_mm, n + 1)
                act.activation(out[:, 4 * q:4 * q + 4, k * ROWS:(k + 1) * ROWS],
                               ps[:, 4 + n % 4, 0:4 * ROWS].rearrange("p (j c) -> p j c", j=4),
                               ACT.Copy).then_inc(b_out, 1)


def edge_ends(core, start, end, at_end, before, has):
    nc = core.nc
    with ExitStack() as ctx:
        sb = lambda k, s, d_=F32: ctx.enter_context(nc.sbuf_tensor(f"ee_{k}", s, d_))
        pos = sb("pos", [128, TILES])
        steps = core.semaphore(ctx, "ee_steps")
        block = ctx.enter_context(nc.Block())

        @block.vector
        def _(dve):
            st = Steps(dve, steps)
            st(dve.tensor_scalar(pos[:, :], end[:, :], -1.0, 0.0, ALU.add, ALU.max))
            st(dve.tensor_copy(at_end[:, :], pos[:, :]))
            st(dve.tensor_scalar(before[:, :], at_end[:, :], RUN.bit_length() - 1, None, ALU.logical_shift_right))
            st(dve.tensor_copy(pos[:, :], before[:, :]))
            st(dve.tensor_scalar(has[:, 1, :], pos[:, :], float(RUN), None, ALU.mult))
            st(dve.tensor_tensor(has[:, 1, :], start[:, :], has[:, 1, :], ALU.is_lt))
            st(dve.tensor_tensor(has[:, 0, :], start[:, :], end[:, :], ALU.is_lt))
            st(dve.tensor_tensor(has[:, 1, :], has[:, 1, :], has[:, 0, :], ALU.mult))
            st(dve.tensor_scalar(pos[:, :], pos[:, :], -1.0, 0.0, ALU.add, ALU.max))
            st(dve.tensor_copy(before[:, :], pos[:, :]))


def graph_gates(core, p, feats, tgt_score, has, at_run, carried, gates):
    nc = core.nc
    carve = Carver(core.XN)
    with ExitStack() as ctx:
        sem = lambda k: core.semaphore(ctx, f"gg_{k}")
        sb = lambda k, s, d_=F32: ctx.enter_context(nc.sbuf_tensor(f"gg_{k}", s, d_))
        par = sb("par", [128, 4, HF])
        rank = sb("rank", [128, GE])
        m0, m1, m2, top, den, tmp = (carve(TILES, HEADS) for _ in range(6))
        agg, prod = carve(TILES, HF), carve(TILES, HF)
        off, mean, var, best, first, second = (carve(TILES) for _ in range(6))
        score, mask, key = (carve(TILES, GE) for _ in range(3))
        loaded, steps, act_in, act_out = map(sem, ("loaded", "steps", "act_in", "act_out"))
        block = ctx.enter_context(nc.Block())

        @block.sync
        def _(sp):
            flat = {"att_src": p["att_src"].rearrange("h e -> (h e)")}
            for k, q in enumerate(("att_src", "b_gat", "ln_gamma", "ln_beta")):
                v = flat.get(q, p[q])
                sp.dma_start(par[:, k, :], v.rearrange("(a c) -> a c", a=1).to_broadcast([128, HF])
                             ).then_inc(loaded, 16)
            sp.wait_ge(loaded, 64)

        @block.scalar
        def _(act):
            act.wait_ge(act_in, 1)
            for n, x in enumerate((m0, m1, m2)):
                act.activation(x, x, ACT.Exp).then_inc(act_out, 1)
            act.wait_ge(act_in, 2)
            act.activation(var, var, ACT.Sqrt, bias=core.eps[:, 1:2]).then_inc(act_out, 1)
            act.wait_ge(act_in, 3)
            act.activation(second, second, ACT.Exp).then_inc(act_out, 1)

        @block.vector
        def _(dve):
            st = Steps(dve, steps)
            heads = lambda x: x.rearrange("p t (h e) -> p t h e", h=HEADS)
            per_head = lambda x: x.rearrange("p t (h e) -> p t h e", e=1).to_broadcast([128, TILES, HEADS, GE])
            wide = lambda x, n: x.rearrange("p (t n) -> p t n", n=1).to_broadcast([128, TILES, n])
            const = lambda k: par[:, k, :].rearrange("p (t c) -> p t c", t=1).to_broadcast([128, TILES, HF])
            h = feats[:, :, :]
            dve.wait_ge(loaded, 64)
            for e in range(GE):
                st.mark(dve.memset(rank[:, e:e + 1], float(GE - e)))
            st(dve.tensor_tensor(prod, h, const(0), ALU.mult))
            st(dve.tensor_reduce(m0, heads(prod), AX.X, ALU.add))
            st(dve.tensor_tensor(m0, m0, tgt_score[:, :, :], ALU.add))
            st(dve.scalar_tensor_tensor(out=m0, in0=m0, scalar=LEAK, in1=m0, op0=ALU.mult, op1=ALU.max))
            for k, (m, x) in enumerate(((m1, at_run), (m2, carried))):
                st(dve.tensor_scalar(off, has[:, k, :], -1.0, BIG, ALU.add, ALU.mult))
                st(dve.tensor_tensor(m, x[:, :, 0:HEADS], wide(off, HEADS), ALU.add))
            st(dve.tensor_tensor(top, m1, m2, ALU.max))
            st(dve.tensor_tensor(top, top, m0, ALU.max))
            for m in (m0, m1, m2):
                st(dve.tensor_tensor(m, m, top, ALU.subtract))
            dve.sem_inc(act_in, 1)
            dve.wait_ge(act_out, 3)
            st(dve.tensor_tensor(heads(agg), heads(h), per_head(m0), ALU.mult))
            den_of, agg_of = (at_run[:, :, HEADS:2 * HEADS], carried[:, :, HEADS + HF:2 * HEADS + HF]), \
                (at_run[:, :, 2 * HEADS:], carried[:, :, 2 * HEADS + HF:])
            st(dve.tensor_copy(den, m0))
            for m, dn, ag in zip((m1, m2), den_of, agg_of):
                st.mark(dve.tensor_tensor(tmp, dn, m, ALU.mult))
                st(dve.tensor_tensor(heads(prod), heads(ag), per_head(m), ALU.mult))
                st.mark(dve.tensor_tensor(den, den, tmp, ALU.add))
                st(dve.tensor_tensor(agg, agg, prod, ALU.add))
            st(dve.tensor_scalar(den, den, 1e-16, None, ALU.add))
            st(dve.reciprocal(den, den))
            st(dve.tensor_tensor(heads(agg), heads(agg), per_head(den), ALU.mult))
            st(dve.tensor_tensor(agg, agg, const(1), ALU.add))
            st(dve.tensor_reduce(mean, agg, AX.X, ALU.add))
            st(dve.tensor_scalar(mean, mean, 1.0 / HF, None, ALU.mult))
            st(dve.tensor_tensor(agg, agg, wide(mean, HF), ALU.subtract))
            st(dve.tensor_tensor(prod, agg, agg, ALU.mult))
            st(dve.tensor_reduce(var, prod, AX.X, ALU.add))
            st(dve.tensor_scalar(var, var, 1.0 / HF, None, ALU.mult))
            dve.sem_inc(act_in, 1)
            dve.wait_ge(act_out, 4)
            st(dve.reciprocal(var, var))
            st(dve.tensor_tensor(agg, agg, wide(var, HF), ALU.mult))
            st(dve.tensor_tensor(agg, agg, const(2), ALU.mult))
            st(dve.tensor_tensor(agg, agg, const(3), ALU.add))
            st(dve.tensor_reduce(score, agg.rearrange("p t (h e) -> p t e h", h=HEADS), AX.X, ALU.add))
            st(dve.tensor_scalar(score, score, 1.0 / HEADS, None, ALU.mult))
            pick_two(nc, dve, st, score, GE, mask, gates[:, :, :], key, best, rank[:, :], first, second)
            st(dve.tensor_tensor(second, second, first, ALU.subtract))
            dve.sem_inc(act_in, 1)
            dve.wait_ge(act_out, 5)
            st(dve.tensor_scalar(first, second, 1.0, None, ALU.add))
            st(dve.reciprocal(first, first))
            st(dve.tensor_tensor(second, second, first, ALU.mult))
            st(dve.tensor_tensor(mask, mask, wide(first, GE), ALU.mult))
            st(dve.tensor_tensor(gates[:, :, :], gates[:, :, :], wide(second, GE), ALU.mult))
            st(dve.tensor_tensor(gates[:, :, :], gates[:, :, :], mask, ALU.add))


def reload(core, xn_dram):
    nc = core.nc
    with ExitStack() as ctx:
        loaded = core.semaphore(ctx, "xn_loaded")
        block = ctx.enter_context(nc.Block())

        @block.sync
        def _(sp):
            for b in range(IMAGES):
                here = slice(b * PIX, (b + 1) * PIX)
                sp.dma_start(core.XN[:, here], xn_dram[:, here]).then_inc(loaded, 16)
            sp.wait_ge(loaded, 16 * IMAGES)


def graph_tables(nc):
    dram = lambda k, *s: nc.dram_tensor(f"graph_{k}", s, F32, kind="Internal").ap()
    return dict(sources=dram("sources", T, SRC_ROW), targets=dram("targets", T, HEADS),
                placed=dram("placed", EDGES + T, HEADS), states=dram("states", EDGES, STATE),
                ends=dram("ends", RUNS, STATE), carry=dram("carry", RUNS, 2 * (HEADS + HF)), xn=dram("xn", D, T))


def graph_phase(core, p, d, t, start, end):
    nc = core.nc
    xn_dram = t["xn"]
    with ExitStack() as outer:
        gates = outer.enter_context(nc.sbuf_tensor("gates1", [128, TILES, GE], F32))
        with ExitStack() as ctx:
            sb = lambda k, s, d_=F32: ctx.enter_context(nc.sbuf_tensor(f"gp_{k}", s, d_))
            feats, tgt_score = sb("feats", [128, TILES, HF]), sb("tgt", [128, TILES, HEADS])
            normalise(core, "ln4", 1, p["W_gat"], HF, feats)
            source_tables(core, p, t, feats, tgt_score, start, end, xn_dram)
            edge_states(core, d, t)
            stitch_runs(core, d, t)
            at_end, before = sb("at_end", [128, TILES], I32), sb("before", [128, TILES], I32)
            has = sb("has", [128, 2, TILES])
            edge_ends(core, start, end, at_end, before, has)
            tail = Carver(core.XN)
            tail.at = T - TILES * (STATE + 2 * (HEADS + HF))
            at_run, carried = tail(TILES, STATE), tail(TILES, 2 * (HEADS + HF))

            def keep(dst, name):
                def consume(dve, n, rows, used):
                    dve.tensor_copy(dst[:, bass.ds(n * 8, 8), :], rows).then_inc(used, 1)
                return consume

            gather(core, "ga", t["states"], STATE, at_end, TILES, 8, keep(at_run, "a"))
            gather(core, "gc", t["carry"], 2 * (HEADS + HF), before, TILES, 8, keep(carried, "c"))
            graph_gates(core, p, feats, tgt_score, has, at_run, carried, gates)
        reload(core, xn_dram)
        experts(core, "e1", GE, gates, p["W1"].rearrange("e d f -> d e f"), p["b1"],
                p["W2"].rearrange("e (a f) c -> f (e a) c", a=2), p["b2"], False)


def store(core, out):
    nc = core.nc
    with ExitStack() as ctx:
        stored = core.semaphore(ctx, "out_stored")
        block = ctx.enter_context(nc.Block())

        @block.sync
        def _(sp):
            for b in range(IMAGES):
                sp.dma_start(out[b, :, :], core.X[:, b * PIX:(b + 1) * PIX]).then_inc(stored, 16)
            sp.wait_ge(stored, 16 * IMAGES)


def metaformer(nc, p, out, stages="IABCD"):
    with ExitStack() as ctx:
        core = Core(nc, ctx)
        setup(core, p["x"])
        if "A" in stages:
            normalise(core, "ln1", 0, None, 0, None)
            attention(core, {k[8:].lower() if k[8] == "W" else k[8:]: v for k, v in p.items() if k.startswith("L0_conv_")})
        if "B" in stages:
            expert_phase_0(core, {k[7:]: v for k, v in p.items() if k.startswith("L0_ffn_")})
        if "I" in stages:
            start, end = (ctx.enter_context(nc.sbuf_tensor(k, [128, TILES], F32)) for k in ("start", "end"))
            tables = graph_tables(nc)
            edges = index_phase(core, p["L1_ffn_edge_index"], start, end,
                                [tables[k] for k in ("placed", "states", "ends")])
        if stages == "I":
            with nc.Block() as block:
                @block.vector
                def _(dve):
                    dve.tensor_copy(core.X[:, 0:TILES], start[:, :])
                    dve.tensor_copy(core.X[:, TILES:2 * TILES], end[:, :])
        if "C" in stages:
            deform_phase(core, {k[8:]: v for k, v in p.items() if k.startswith("L1_conv_")})
        if "D" in stages:
            graph_phase(core, {k[7:]: v for k, v in p.items() if k.startswith("L1_ffn_")}, edges, tables, start, end)
        store(core, out)


def kernel(**inputs):
    import numpy as _np
    import concourse.bacc as _bacc
    from concourse import mybir as _mybir
    from concourse.bass_utils import run_bass_kernel_spmd as _run

    laid = {k: _np.asarray(v) for k, v in inputs.items()}
    laid["x"] = laid["x"].reshape(IMAGES, D, PIX)
    for k in ("L0_conv_W_f", "L0_conv_W_g", "L0_conv_W_h", "L0_ffn_router_w"):
        laid[k] = laid[k].T
    laid["L0_ffn_b1"] = laid["L0_ffn_b1"].T
    laid["L1_ffn_b1"] = laid["L1_ffn_b1"].reshape(-1, 128).T
    for k in ("L1_conv_w_off", "L1_conv_weight"):
        laid[k] = laid[k].reshape(-1, D, TAPS).transpose(1, 2, 0)
    nc = _bacc.Bacc("TRN2", target_bir_lowering=False, num_devices=1)
    arrays, p = {}, {}
    for name, a in laid.items():
        a = _np.ascontiguousarray(a)
        arrays[f"in_{name}"] = a
        p[name] = nc.dram_tensor(f"in_{name}", a.shape, _mybir.dt.from_np(a.dtype), kind="ExternalInput").ap()
    out = nc.dram_tensor("out_0", (IMAGES, D, PIX), F32, kind="ExternalOutput").ap()
    metaformer(nc, p, out)
    r = _run(nc, [arrays], core_ids=[0])
    return r.results[0]["out_0"].reshape(IMAGES, D, SIDE, SIDE)
```

```python
import concourse.bass as bass
from concourse import mybir
from contextlib import ExitStack

F32 = mybir.dt.float32
I32 = mybir.dt.int32
BF16 = mybir.dt.bfloat16
ALU = mybir.AluOpType
ACT = mybir.ActivationFunctionType
AX = mybir.AxisListType

IMAGES, D, SIDE = 8, 128, 48
PIX = SIDE * SIDE
T = IMAGES * PIX
TILE = 128
TILES = T // TILE
CHUNK = 384
TPC = CHUNK // TILE
CHUNKS = T // CHUNK
CPI = PIX // CHUNK
TPI = PIX // TILE
DK = 32
TAPS = 9
BIG = 1.0e30


class Steps:

    def __init__(self, eng, sem, base=0):
        self.eng, self.sem, self.base, self.n = eng, sem, base, 0

    def mark(self, ins):
        ins.then_inc(self.sem, 1)
        self.n += 1
        return ins

    def done(self):
        self.eng.wait_ge(self.sem, self.base + self.n)

    def __call__(self, ins):
        self.mark(ins)
        self.done()


class Core:

    def __init__(self, nc, ctx):
        self.nc, self.ctx = nc, ctx
        self.X = ctx.enter_context(nc.sbuf_tensor("X", [128, T], F32))
        self.XN = ctx.enter_context(nc.sbuf_tensor("XN", [128, T], F32))
        self.psum = ctx.enter_context(nc.psum_tensor("psum", [128, 8, 512], F32))
        self.ident = ctx.enter_context(nc.sbuf_tensor("ident", [128, 128], F32))
        self.mean_w = ctx.enter_context(nc.sbuf_tensor("mean_w", [128, 128], F32))
        self.ones = ctx.enter_context(nc.sbuf_tensor("ones", [128, 128], F32))
        self.eps = ctx.enter_context(nc.sbuf_tensor("eps", [128, 2], F32))
        self.open = {}

    def semaphore(self, ctx, name):
        if id(ctx) not in self.open:
            mine = self.open[id(ctx)] = []

            def close():
                self.nc.clear_and_free_semaphores(mine)
                self.nc.all_engine_barrier()
                del self.open[id(ctx)]
            ctx.callback(close)
        handle = self.nc.alloc_semaphore(name=name)
        self.open[id(ctx)].append(handle)
        return handle


def setup(core):
    nc = core.nc
    with ExitStack() as ctx:
        zeroed = core.semaphore(ctx, "zeroed")
        made = core.semaphore(ctx, "made")
        block = ctx.enter_context(nc.Block())

        @block.gpsimd
        def _(pool):
            pool.memset(core.ident[:, :], 0.0).then_inc(zeroed, 1)
            pool.wait_ge(zeroed, 1)
            pool.affine_select(out=core.ident[:, :], in_=core.ident[:, :], compare_op=ALU.not_equal,
                               fill=1.0, base=0, pattern=[[-1, 128]], channel_multiplier=1).then_inc(made, 1)
            pool.wait_ge(made, 1)

        @block.vector
        def _(dve):
            dve.memset(core.mean_w[:, :], 1.0 / D)
            dve.memset(core.ones[:, :], 1.0)
            dve.memset(core.eps[:, 0:1], 1e-6)
            dve.memset(core.eps[:, 1:2], 1e-5)


def normalise(core, name, eps_col, weights, row, rows_to, rows_dma=None):
    nc, X, XN, ps = core.nc, core.X, core.XN, core.psum
    LOT = 4
    LOTS = CHUNKS // LOT
    BANK_V = 7
    spread = lambda b: ps[:, LOT + b % 3, 0:CHUNK]
    with ExitStack() as ctx:
        sem = lambda n: core.semaphore(ctx, f"{name}_{n}")
        sb = lambda n, s: ctx.enter_context(nc.sbuf_tensor(f"{name}_{n}", s, F32))
        sq, diag = sb("sq", [128, LOT, CHUNK]), sb("diag", [128, LOT, TPC, TILE])
        std, rstd = sb("std", [128, LOT, TPC]), sb("rstd", [128, LOT, TPC])
        w = sb("w", [128, row]) if weights is not None else core.ident
        if row:
            xs = sb("xs", [128, LOT, CHUNK])
        if rows_dma:
            rows = sb("rows", [128, LOT, TPC, row])
        w_in, mean_done, xc_done, sq_done, var_done, std_done, rstd_done, diag_done = map(sem, (
            "w_in", "mean", "xc", "sq", "var", "std", "rstd", "diag"))
        spread_done, xn_done, xs_done, rows_done, bank_free = map(sem, (
            "spread", "xn", "xs_done", "rows_done", "bank_free"))
        stored = [sem(f"stored{b}") for b in range(LOT)] if rows_dma else []
        rows_out, rows_free = sem("rows_out"), sem("rows_free")
        n_dma = 4 if rows_dma else 0
        block = ctx.enter_context(nc.Block())
        chunk = lambda n: slice(n * CHUNK, (n + 1) * CHUNK) if isinstance(n, int) else bass.ds(n * CHUNK, CHUNK)

        def lots(eng, ahead, body):
            ahead(0, True)
            with eng.Fori(0, LOTS - 1) as i:
                body(i, False)
            body(LOTS - 1, True)

        @block.sync
        def _(sp):
            if weights is not None:
                sp.dma_start(w[:, :], weights).then_inc(w_in, 16)
                sp.wait_ge(w_in, 16)
            if rows_dma:
                with sp.Fori(0, LOTS) as i:
                    for b in range(LOT):
                        n = i * LOT + b
                        sp.wait_ge(rows_out, n + 1)
                        for dst in rows_dma(n):
                            sp.dma_start(dst, rows[:, b, :, :]).then_inc(stored[b], 16)
                    for b in range(LOT):
                        sp.wait_ge(stored[b], 16 * n_dma * (i + 1))
                        sp.sem_inc(rows_free, 1)

        @block.tensor
        def _(pe):
            if weights is not None:
                pe.wait_ge(w_in, 16)

            def means(i, first=False):
                for b in range(LOT):
                    n = i * LOT + b
                    if not first:
                        pe.wait_ge(xc_done, n - LOT + 1)
                        if row:
                            pe.wait_ge(bank_free, n - LOT + 1)
                    nc.tensor.matmul(ps[:, b, 0:CHUNK], core.mean_w[:, :], X[:, chunk(n)],
                                     start=True, stop=True).then_inc(mean_done, 1)

            def body(i, last):
                if not last:
                    means(i + 1)
                for b in range(LOT):
                    n = i * LOT + b
                    pe.wait_ge(sq_done, n + 1)
                    pe.wait_ge(std_done, i + 1)
                    for t in range(TPC):
                        mm = nc.tensor.matmul(ps[:, BANK_V, b * TPC + t:b * TPC + t + 1], sq[:, b, t * TILE:(t + 1) * TILE],
                                              core.mean_w[:, 0:1], start=True, stop=True)
                    mm.then_inc(var_done, 1)
                for b in range(LOT):
                    n = i * LOT + b
                    pe.wait_ge(diag_done, n + 1)
                    pe.wait_ge(xn_done, n + (LOT, 1, 1, 2)[b])
                    nc.tensor.matmul(spread(b), core.ones[:, :],
                                     diag[:, b, :, :].rearrange("p t k -> p (t k)"),
                                     start=True, stop=True).then_inc(spread_done, 1)
                if row:
                    for b in range(LOT):
                        n = i * LOT + b
                        pe.wait_ge(xs_done, n + 1)
                        if not last:
                            pe.wait_ge(xc_done, n + LOT + 1)
                        for t in range(TPC):
                            mm = nc.tensor.matmul(ps[:, b, t * row:(t + 1) * row],
                                                  xs[:, b, t * TILE:(t + 1) * TILE], w[:, :],
                                                  start=True, stop=True)
                        mm.then_inc(rows_done, 1)
            lots(pe, means, body)

        @block.vector
        def _(dve):
            dve.sem_inc(rstd_done, 1)
            dve.sem_inc(xn_done, LOT)

            def centre(i, first=False):
                for b in range(LOT):
                    n = i * LOT + b
                    dve.wait_ge(mean_done, n + 1)
                    nc.vector.tensor_tensor(XN[:, chunk(n)], X[:, chunk(n)], ps[:, b, 0:CHUNK],
                                            ALU.subtract).then_inc(xc_done, 1)

            def body(i, last):
                if not last:
                    centre(i + 1)
                dve.wait_ge(std_done, i + 2)
                dve.wait_ge(spread_done, (i + 1) * LOT)
                dve.reciprocal(rstd[:, :, :], std[:, :, :]).then_inc(rstd_done, 1)
                for b in range(LOT):
                    n = i * LOT + b
                    dve.wait_ge(rstd_done, i + 2)
                    nc.vector.tensor_tensor(
                        diag[:, b, :, :],
                        core.ident[:, :].rearrange("p (a k) -> p a k", a=1).to_broadcast([128, TPC, TILE]),
                        rstd[:, b, :].rearrange("p (t a) -> p t a", a=1).to_broadcast([128, TPC, TILE]),
                        ALU.mult).then_inc(diag_done, 1)
                for b in range(LOT):
                    n = i * LOT + b
                    dve.wait_ge(xc_done, n + 1)
                    dve.wait_ge(spread_done, n + 1 + LOT)
                    nc.vector.tensor_tensor(XN[:, chunk(n)], XN[:, chunk(n)], spread(b),
                                            ALU.mult).then_inc(xn_done, 1)
            lots(dve, centre, body)

        @block.gpsimd
        def _(pool):
            pool.sem_inc(spread_done, LOT)

            def squares(i, first=False):
                for b in range(LOT):
                    n = i * LOT + b
                    pool.wait_ge(xc_done, n + 1)
                    if not first:
                        pool.wait_ge(var_done, n - LOT + 1)
                    pool.tensor_tensor(sq[:, b, :], XN[:, chunk(n)], XN[:, chunk(n)],
                                       ALU.mult).then_inc(sq_done, 1)

            def body(i, last):
                if not last:
                    squares(i + 1)
            lots(pool, squares, body)

        @block.scalar
        def _(act):
            act.sem_inc(bank_free, LOT)
            act.sem_inc(std_done, 1)
            if rows_dma:
                act.sem_inc(rows_free, LOT)

            def body(i, last):
                act.wait_ge(var_done, (i + 1) * LOT)
                act.wait_ge(rstd_done, i + 1)
                nc.scalar.activation(std[:, :, :].rearrange("p b t -> p (b t)"), ps[:, BANK_V, 0:LOT * TPC], ACT.Sqrt,
                                     bias=core.eps[:, eps_col:eps_col + 1]).then_inc(std_done, 1)
                if row:
                    for b in range(LOT):
                        n = i * LOT + b
                        act.wait_ge(xn_done, n + 1 + LOT)
                        nc.scalar.activation(xs[:, b, :], XN[:, chunk(n)], ACT.Copy).then_inc(xs_done, 1)
                    for b in range(LOT):
                        n = i * LOT + b
                        act.wait_ge(rows_done, n + 1)
                        src = ps[:, b, 0:TPC * row].rearrange("p (t r) -> p t r", t=TPC)
                        if rows_dma:
                            act.wait_ge(rows_free, n + 1)
                            nc.scalar.activation(rows[:, b, :, :], src, ACT.Copy).then_inc(rows_out, 1)
                            act.wait_ge(rows_out, n + 1)
                            act.sem_inc(bank_free, 1)
                        else:
                            tiles = slice(n * TPC, (n + 1) * TPC) if last else bass.ds(n * TPC, TPC)
                            nc.scalar.activation(rows_to[:, tiles, :], src, ACT.Copy).then_inc(bank_free, 1)
            lots(act, lambda i, first: None, body)


def attention(core, p):
    nc, X, XN, ps = core.nc, core.X, core.XN, core.psum
    EPS = 1e-5
    RING = 6
    BLOCKS = TILE // DK
    PARTS = 3
    M0 = (BLOCKS - 1) * DK
    UNITS = 2 * CPI
    unit = lambda q: (q % CPI, q // CPI)
    bank_of = lambda q: q % 4 if q < CPI else 7
    GROUPS = CPI // 2
    GT = TPI // GROUPS
    split_after = {TPC * c + 1: CPI + c + 1 for c in range(CPI - 1)}
    with ExitStack() as ctx:
        sem = lambda n: core.semaphore(ctx, f"at_{n}")
        sb = lambda n, s, d=F32: ctx.enter_context(nc.sbuf_tensor(f"at_{n}", s, d))
        w_f, w_g, w_h = sb("w_f", [128, BLOCKS, DK]), sb("w_g", [128, BLOCKS, DK]), sb("w_h", [128, D])
        fg_par = sb("fg_par", [128, 2, 5])
        h_par = sb("h_par", [128, 5, D])
        fg_inv, fg_shift = sb("fg_inv", [128, 2]), sb("fg_shift", [128, 2])
        h_inv, h_shift = sb("h_inv", [128, D]), sb("h_shift", [128, D])
        minus = sb("minus", [128, 2, 3])
        stack1, stack2 = sb("stack1", [128, 2, PIX], BF16), sb("stack2", [128, 2, PIX], BF16)
        feat, rest = sb("feat", [128, 2, CHUNK]), sb("rest", [128, 2, CHUNK])
        part1, part2 = sb("part1", [128, 2, CHUNK], BF16), sb("part2", [128, 2, CHUNK], BF16)
        hT = sb("hT", [128, TPI, D])
        probs = sb("probs", [128, RING, CHUNK])
        xi = probs
        assert RING * CHUNK == PIX
        xi_tile = lambda j: xi[:, j // TPC, j % TPC * TILE:(j % TPC + 1) * TILE]
        psum_rows = sb("den", [128, 2, CHUNK])
        mx, nmax = sb("mx", [128, TPI, 2]), sb("nmax", [128, TPI])
        m_parts, m_wide = sb("m_parts", [128, PARTS, TPI], BF16), sb("m_wide", [128, GROUPS, PARTS * GT])
        mrow = sb("mrow", [PARTS * GT, GROUPS, TILE], BF16)
        att = sb("att", [128, 2, CHUNK])
        w_in, par, xi_ready, fg_mm, fg_out, h_mm, h_out = map(sem, (
            "w_in", "par", "xi_ready", "fg_mm", "fg_out", "h_mm", "h_out"))
        s_mm, s_max, nmaxT, mrow_done, mrow_in, made = map(sem, (
            "s_mm", "s_max", "nmaxT", "mrow", "mrow_in", "made"))
        st_mm, exp_done, pv_done, add_done, o_done, o_free, steps, m_steps = map(sem, (
            "st_mm", "exp", "pv", "add", "o_done", "o_free", "steps", "m_steps"))
        rest_done, part2_done, stacked, split_done, m_zero = map(sem, (
            "rest", "part2", "stacked", "split", "m_zero"))
        var_ready, sd_ready, scaled, x_done = map(sem, ("var_ready", "sd_ready", "scaled", "x_done"))
        turns = sem("turns")
        M_STEPS = 2 * PARTS + 1
        block = ctx.enter_context(nc.Block())

        @block.sync
        def _(sp):
            for r in range(BLOCKS):
                sp.dma_start(w_f[:, r, :], p["w_f"]).then_inc(w_in, 16)
                sp.dma_start(w_g[:, r, :], p["w_g"]).then_inc(w_in, 16)
                for k, which in enumerate("fg"):
                    for j, q in enumerate(("b", "gamma", "beta", "mean", "var")):
                        sp.dma_start(fg_par[r * DK:(r + 1) * DK, k, j:j + 1],
                                     p[f"{q}_{which}"].rearrange("(c a) -> c a", a=1)).then_inc(w_in, 16)
            sp.dma_start(w_h[:, :], p["w_h"]).then_inc(w_in, 16)
            for j, q in enumerate(("b", "gamma", "beta", "mean", "var")):
                sp.dma_start(h_par[:, j, :], p[f"{q}_h"].rearrange("(a c) -> a c", a=1)
                             .to_broadcast([128, D])).then_inc(w_in, 16)
            sp.wait_ge(w_in, 16 * (12 * BLOCKS + 6))
            with sp.Fori(0, IMAGES) as i:
                for g in range(GROUPS):
                    n = i * GROUPS + g
                    sp.wait_ge(mrow_done, n + 1)
                    for k in range(PARTS):
                        sp.dma_start(stack2[M0 + k:M0 + k + 1, 1, g * GT * TILE:(g + 1) * GT * TILE]
                                     .rearrange("a (t n) -> a t n", t=GT),
                                     mrow[k * GT:(k + 1) * GT, g, :]).then_inc(mrow_in, 16)
                    sp.wait_ge(mrow_in, 16 * PARTS * (n + 1))
                    sp.sem_inc(turns, 1)

        @block.tensor
        def _(pe):
            pe.wait_ge(w_in, 16 * (12 * BLOCKS + 6))
            pe.wait_ge(par, 1)
            with pe.Fori(0, IMAGES) as i:
                pe.wait_ge(o_free, CPI * i + 2)
                pe.wait_ge(xi_ready, i + 1)

                def features(q):
                    c, k = unit(q)
                    nc.tensor.matmul(ps[:, bank_of(q), 0:CHUNK],
                                     (w_f, w_g)[k][:, :, :].rearrange("p r c -> p (r c)"), xi[:, c, :],
                                     start=True, stop=True).then_inc(fg_mm, 1)

                def turn_maxima(g):
                    pe.wait_ge(m_steps, M_STEPS * (GROUPS * i + g + 1))
                    if g:
                        pe.wait_ge(mrow_done, GROUPS * i + g)
                    pe.sem_inc(turns, 1)
                    nc.tensor.transpose(ps[0:PARTS * GT, 6, 0:TILE], m_wide[:, g, :],
                                        core.ident[:, :]).then_inc(nmaxT, 1)

                for c in range(CPI):
                    if c >= 4:
                        pe.wait_ge(fg_out, UNITS * i + c - 3)
                    features(c)
                    if c >= 3:
                        pe.wait_ge(h_out, CPI * i + c - 2)
                    for t in range(TPC):
                        out = ps[:, 4 + c % 3, t * TILE:(t + 1) * TILE]
                        nc.tensor.matmul(out, xi_tile(c * TPC + t), w_h[:, :], start=True, stop=False)
                        mm = nc.tensor.matmul(out, core.mean_w[:, :], h_shift[:, :], start=False, stop=True)
                    mm.then_inc(h_mm, 1)
                features(CPI)
                pe.wait_ge(h_out, CPI * (i + 1))
                pe.wait_ge(m_zero, i + 1)
                for t in range(TPI):
                    if t % TPC == 0:
                        pe.wait_ge(split_done, UNITS * i + CPI + t // TPC + 1 + 2)
                        pe.wait_ge(stacked, UNITS * i + CPI + t // TPC + 1)
                    for k in range(2):
                        q = 2 * t + k
                        if q >= 2:
                            pe.wait_ge(s_max, 2 * TPI * i + q - 1)
                        for n, stack in enumerate((stack1, stack2)):
                            for c in range(3):
                                mm = nc.tensor.matmul(ps[:, 3 * k + c, 0:CHUNK],
                                                      stack[:, 1, t * TILE:(t + 1) * TILE],
                                                      stack[:, 0, (3 * k + c) * CHUNK:(3 * k + c + 1) * CHUNK],
                                                      start=n == 0, stop=n == 1)
                        mm.then_inc(s_mm, 1)
                    if t + 1 in split_after:
                        q = split_after[t + 1]
                        pe.wait_ge(fg_out, UNITS * i + q)
                        features(q)
                    if t > GT and t % GT == 1:
                        turn_maxima(t // GT - 1)
                turn_maxima(GROUPS - 1)
                with pe.Fori(0, CPI // 2) as cc:
                    LAG, DEN_LAG = 2, 2
                    r0 = i * CPI + 2 * cc
                    pe.wait_ge(mrow_in, 16 * PARTS * (GROUPS * i + cc + 1))
                    pe.sem_inc(turns, 1)

                    def denominators(half):
                        pe.wait_ge(add_done, (r0 + half + 1) * TPI + RING)
                        nc.tensor.matmul(ps[:, 4 + 2 * half, 0:CHUNK], core.ones[:, :], psum_rows[:, half, :],
                                         start=True, stop=True).then_inc(o_done, 1)

                    for j in range(2 * TPI + LAG):
                        if j < 2 * TPI:
                            half, tile = divmod(j, TPI)
                            pe.wait_ge(exp_done, r0 * TPI + j + 1)
                            for n, stack in enumerate((stack1, stack2)):
                                mm = nc.tensor.matmul(ps[:, j % 3, 0:CHUNK],
                                                      stack[:, 0, tile * TILE:(tile + 1) * TILE],
                                                      stack[:, 1, bass.ds((2 * cc + half) * CHUNK, CHUNK)],
                                                      start=n == 0, stop=n == 1)
                            mm.then_inc(st_mm, 1)
                        if j >= LAG:
                            half, tile = divmod(j - LAG, TPI)
                            if tile == 0:
                                pe.wait_ge(o_free, r0 + half + 1)
                            pe.wait_ge(exp_done, r0 * TPI + j - LAG + 1 + 3)
                            nc.tensor.matmul(ps[:, 3 + 2 * half, 0:CHUNK], hT[:, tile, :],
                                             probs[:, tile % RING, :],
                                             start=tile == 0, stop=tile == TPI - 1).then_inc(pv_done, 1)
                        if j == TPI + DEN_LAG:
                            denominators(0)
                    denominators(1)

        @block.scalar
        def _(act):
            act.sem_inc(exp_done, 3)
            act.wait_ge(var_ready, 2)
            for inv in (fg_inv, h_inv):
                act.activation(inv[:, :], inv[:, :], ACT.Sqrt).then_inc(sd_ready, 1)
            act.wait_ge(par, 1)
            with act.Fori(0, IMAGES) as i:
                act.wait_ge(o_free, CPI * i + 2)
                act.activation(xi[:, :, :].rearrange("p r c -> p (r c)"), XN[:, bass.ds(i * PIX, PIX)],
                               ACT.Copy).then_inc(xi_ready, 1)

                def features_out(q):
                    c, k = unit(q)
                    act.wait_ge(fg_mm, UNITS * i + q + 1)
                    act.wait_ge(split_done, UNITS * i + q + 1)
                    for dst in (feat, part1):
                        ins = act.activation(dst[:, q % 2, :], ps[:, bank_of(q), 0:CHUNK], ACT.Relu,
                                             bias=fg_shift[:, k:k + 1], scale=fg_inv[:, k:k + 1])
                    ins.then_inc(fg_out, 1)

                def second_part(q):
                    act.wait_ge(rest_done, UNITS * i + q + 1)
                    act.activation(part2[:, q % 2, :], rest[:, q % 2, :], ACT.Copy).then_inc(part2_done, 1)

                def maxima_out(g):
                    act.wait_ge(nmaxT, GROUPS * i + g + 1)
                    act.activation(mrow[:, g, :], ps[0:PARTS * GT, 6, 0:TILE], ACT.Copy).then_inc(mrow_done, 1)

                for q in range(CPI):
                    features_out(q)
                    if q >= 1:
                        second_part(q - 1)
                    act.wait_ge(h_mm, CPI * i + q + 1)
                    act.activation(hT[:, q * TPC:(q + 1) * TPC, :],
                                   ps[:, 4 + q % 3, 0:CHUNK].rearrange("p (t o) -> p t o", t=TPC),
                                   ACT.Relu).then_inc(h_out, 1)
                features_out(CPI)
                second_part(CPI - 1)
                second_part(CPI)
                for t in range(TPI):
                    if t + 1 in split_after:
                        features_out(split_after[t + 1])
                        second_part(split_after[t + 1])
                    if t > GT and t % GT == 1:
                        maxima_out(t // GT - 1)
                maxima_out(GROUPS - 1)
                with act.Fori(0, CPI) as c:
                    r = i * CPI + c
                    for j in range(TPI):
                        act.wait_ge(st_mm, r * TPI + j + 1)
                        act.wait_ge(pv_done, r * TPI + j + 1)
                        act.wait_ge(add_done, r * TPI + j + 1)
                        act.activation(probs[:, j % RING, :], ps[:, j % 3, 0:CHUNK],
                                       ACT.Exp).then_inc(exp_done, 1)

        @block.gpsimd
        def _(pool):
            pool.sem_inc(pv_done, RING)
            pool.memset(stack2[M0:TILE, 0, :], 0.0).then_inc(made, 1)
            pool.wait_ge(made, 1)
            pool.memset(stack2[M0:M0 + PARTS, 0, :], 1.0).then_inc(made, 1)
            for k, per_block in enumerate((((0, 0, -1, -1), (0, -1, -1, 0), (0, -1, 0, 0)),
                                           ((0, -1, 0, -1), (-1, 0, -1, 0), (-1, 0, -1, 0)))):
                for s, signs in enumerate(per_block):
                    for r, v in enumerate(signs):
                        pool.memset(minus[r * DK:(r + 1) * DK, k, s:s + 1], float(v)).then_inc(made, 1)
            pool.wait_ge(made, 2 + 6 * BLOCKS)
            pool.sem_inc(x_done, 2)
            with pool.Fori(0, IMAGES * CPI // 2) as i:
                for half in range(2):
                    r = 2 * i + half
                    here = bass.ds(r * CHUNK, CHUNK)
                    pool.wait_ge(o_free, r + 1 + 2)
                    pool.tensor_tensor(att[:, half, :], att[:, half, :], XN[:, here], ALU.mult).then_inc(scaled, 1)
                    pool.wait_ge(scaled, r + 1)
                    pool.tensor_tensor(X[:, here], X[:, here], att[:, half, :], ALU.add).then_inc(x_done, 1)

        @block.vector
        def _(dve):
            st = Steps(dve, steps)
            dve.sem_inc(add_done, RING)
            dve.sem_inc(split_done, 2)
            dve.wait_ge(w_in, 16 * (12 * BLOCKS + 6))
            sets = ((fg_inv[:, :], fg_shift[:, :], lambda j: fg_par[:, :, j]),
                    (h_inv[:, :], h_shift[:, :], lambda j: h_par[:, j, :]))
            for inv, shift, q in sets:
                dve.tensor_scalar(inv, q(4), EPS, None, ALU.add).then_inc(var_ready, 1)
            dve.wait_ge(sd_ready, 2)
            for inv, shift, q in sets:
                st(dve.reciprocal(inv, inv))
                st(dve.tensor_tensor(inv, inv, q(1), ALU.mult))
                st(dve.tensor_tensor(shift, q(3), inv, ALU.mult))
                st(dve.tensor_tensor(shift, q(2), shift, ALU.subtract))
                st(dve.tensor_tensor(q(0), q(0), inv, ALU.mult))
                st(dve.tensor_tensor(shift, shift, q(0), ALU.add))
            st(dve.tensor_tensor(w_h[:, :], w_h[:, :], h_inv[:, :], ALU.mult))
            dve.wait_ge(made, 2 + 6 * BLOCKS)
            dve.sem_inc(o_free, 2)
            dve.sem_inc(par, 1)

            def third(i, q):
                c, k = unit(q)
                dve.wait_ge(part2_done, UNITS * i + q + 1)
                dve.wait_ge(rest_done, UNITS * i + q + 1)
                dve.scalar_tensor_tensor(out=stack2[0:M0, k, c * CHUNK:(c + 1) * CHUNK], in0=part2[0:M0, q % 2, :],
                                         scalar=minus[0:M0, k, 2:3], in1=rest[0:M0, q % 2, :],
                                         op0=ALU.mult, op1=ALU.add).then_inc(split_done, 1)

            def first_parts(i, q):
                c, k = unit(q)
                dve.wait_ge(fg_out, UNITS * i + q + 1)
                dve.wait_ge(split_done, UNITS * i + q + 1)
                for s, out in ((1, rest[:, q % 2, :]), (0, stack1[:, k, c * CHUNK:(c + 1) * CHUNK])):
                    dve.scalar_tensor_tensor(out=out, in0=part1[:, q % 2, :], scalar=minus[:, k, s:s + 1],
                                             in1=feat[:, q % 2, :], op0=ALU.mult,
                                             op1=ALU.add).then_inc(rest_done if s else stacked, 1)

            with dve.Fori(0, IMAGES) as i:
                dve.wait_ge(o_free, CPI * i + 2)
                dve.memset(stack2[M0:TILE, 1, :], 0.0).then_inc(m_zero, 1)
                for q in range(CPI + 1):
                    first_parts(i, q)
                    if q >= 1:
                        third(i, q - 1)
                third(i, CPI)
                for t in range(TPI):
                    for k in range(2):
                        q = 2 * t + k
                        dve.wait_ge(s_mm, 2 * TPI * i + q + 1)
                        dve.tensor_reduce(mx[:, t, k:k + 1], ps[:, 3 * k:3 * k + 3, 0:CHUNK], AX.XY,
                                          ALU.max).then_inc(s_max, 1)
                        if k == 0 and t - 1 in split_after:
                            third(i, split_after[t - 1])
                    if t in split_after:
                        first_parts(i, split_after[t])
                    if t % GT == GT - 1:
                        g = t // GT
                        own = slice(g * GT, (g + 1) * GT)
                        dve.wait_ge(s_max, 2 * (TPI * i + t + 1))
                        ms = Steps(dve, m_steps, M_STEPS * (GROUPS * i + g))
                        ms(dve.tensor_reduce(nmax[:, own], mx[:, own, :], AX.X, ALU.max, negate=True))
                        for k in range(PARTS):
                            ms(dve.tensor_copy(m_parts[:, k, own], nmax[:, own]))
                            if k < PARTS - 1:
                                ms(dve.tensor_tensor(nmax[:, own], nmax[:, own], m_parts[:, k, own], ALU.subtract))
                        ms(dve.tensor_copy(m_wide[:, g, :].rearrange("p (k t) -> p k t", k=PARTS),
                                           m_parts[:, :, own]))
                        assert ms.n == M_STEPS
                dve.sem_inc(turns, 1)
                with dve.Fori(0, CPI // 2) as cc:
                    for par2 in range(2):
                        c = 2 * cc + par2
                        r = i * CPI + c
                        total = psum_rows[:, par2, :]
                        for j in range(TPI):
                            dve.wait_ge(exp_done, r * TPI + j + 1 + 3)
                            if j == 0:
                                dve.tensor_copy(total, probs[:, 0, :]).then_inc(add_done, 1)
                            else:
                                dve.wait_ge(add_done, r * TPI + j + RING)
                                dve.tensor_tensor(total, total, probs[:, j % RING, :],
                                                  ALU.add).then_inc(add_done, 1)
                        dve.wait_ge(o_done, r + 1)
                        at = Steps(dve, steps, st.n + r)
                        dve.wait_ge(x_done, r + 1)
                        at(dve.reciprocal(att[:, par2, :], ps[:, 4 + 2 * par2, 0:CHUNK]))
                        dve.tensor_tensor(att[:, par2, :], att[:, par2, :], ps[:, 3 + 2 * par2, 0:CHUNK],
                                          ALU.mult).then_inc(o_free, 1)


def pick_two(nc, dve, st, val, n, first, second, key, best, rank, m1, m2):
    wide = lambda a: a.rearrange("p (t e) -> p t e", e=1).to_broadcast([128, TILES, n])
    ranks = rank.rearrange("p (t e) -> p t e", t=1).to_broadcast([128, TILES, n])
    for mask, m in ((first, m1), (second, m2)):
        st(dve.tensor_reduce(m, val, AX.X, ALU.max))
        st(dve.tensor_tensor(key, val, wide(m), ALU.is_equal))
        st(dve.tensor_tensor(key, key, ranks, ALU.mult))
        st(dve.tensor_reduce(best, key, AX.X, ALU.max))
        st(dve.tensor_tensor(mask, key, wide(best), ALU.is_equal))
        if mask is first:
            st(dve.tensor_scalar(key, mask, -BIG, None, ALU.mult))
            st(dve.tensor_tensor(val, val, key, ALU.add))


def route_by_logits(core, logits, gates):
    nc, n = core.nc, 8
    with ExitStack() as ctx:
        sb = lambda k, s: ctx.enter_context(nc.sbuf_tensor(f"r0_{k}", s, F32))
        first, key = sb("first", [128, TILES, n]), sb("key", [128, TILES, n])
        best, m1, m2, total = (sb(k, [128, TILES]) for k in ("best", "m1", "m2", "total"))
        rank = sb("rank", [128, n])
        steps, shifted, exped = (core.semaphore(ctx, f"r0_{k}") for k in ("steps", "shifted", "exped"))
        block = ctx.enter_context(nc.Block())
        wide = lambda a: a.rearrange("p (t e) -> p t e", e=1).to_broadcast([128, TILES, n])

        @block.scalar
        def _(act):
            act.wait_ge(shifted, 1)
            act.activation(logits[:, :, :], logits[:, :, :], ACT.Exp).then_inc(exped, 1)

        @block.vector
        def _(dve):
            st = Steps(dve, steps)
            for e in range(n):
                st.mark(dve.memset(rank[:, e:e + 1], float(n - e)))
            st(dve.tensor_reduce(m1[:, :], logits[:, :, :], AX.X, ALU.max))
            dve.tensor_tensor(logits[:, :, :], logits[:, :, :], wide(m1[:, :]), ALU.subtract).then_inc(shifted, 1)
            dve.wait_ge(exped, 1)
            st(dve.tensor_reduce(total[:, :], logits[:, :, :], AX.X, ALU.add))
            st(dve.reciprocal(total[:, :], total[:, :]))
            st(dve.tensor_tensor(logits[:, :, :], logits[:, :, :], wide(total[:, :]), ALU.mult))
            pick_two(nc, dve, st, logits[:, :, :], n, first[:, :, :], gates[:, :, :], key[:, :, :], best[:, :],
                     rank[:, :], m1[:, :], m2[:, :])
            st(dve.tensor_tensor(total[:, :], m1[:, :], m2[:, :], ALU.add))
            st(dve.tensor_scalar(total[:, :], total[:, :], 1e-12, None, ALU.max))
            st(dve.reciprocal(total[:, :], total[:, :]))
            for mask, m in ((first, m1), (gates, m2)):
                st(dve.tensor_tensor(m[:, :], m[:, :], total[:, :], ALU.mult))
                st(dve.tensor_tensor(mask[:, :, :], mask[:, :, :], wide(m[:, :]), ALU.mult))
            st(dve.tensor_tensor(gates[:, :, :], gates[:, :, :], first[:, :, :], ALU.add))


def experts(core, name, n_exp, gates, w1_d, b1_d, w2_d, b2_d, residual, out=None, saved=None):
    nc, X, XN, ps = core.nc, core.X, core.XN, core.psum
    U = 8
    HALVES = U // n_exp
    CREDIT = 2 * HALVES
    with ExitStack() as ctx:
        sem = lambda k: core.semaphore(ctx, f"{name}_{k}")
        sb = lambda k, s: ctx.enter_context(nc.sbuf_tensor(f"{name}_{k}", s, F32))
        w1, w2, b1 = sb("w1", [128, U, 128]), sb("w2", [128, U, 128]), sb("b1", [128, U])
        b2 = sb("b2", [128, D])
        PARTS = 3
        sel = ctx.enter_context(nc.sbuf_tensor(f"{name}_sel", [128, n_exp, 128], BF16))
        gTb = ctx.enter_context(nc.sbuf_tensor(f"{name}_gTb", [128, 2, CHUNK], BF16))
        parts = sb("parts", [128, TILES + TPC, PARTS, n_exp])
        left = sb("left", [128, TILES, n_exp])
        part = ctx.enter_context(nc.sbuf_tensor(f"{name}_part", [128, TILES, n_exp], BF16))
        gt, gT = sb("gt", [128, 2, TPC, 128]), sb("gT", [128, 2, CHUNK])
        hid, hg = sb("hid", [128, 2, CHUNK]), sb("hg", [128, 2, CHUNK])
        w_in, made, gt_done, gT_mm, gT_out, b_mm, h_mm, h_act, hg_done, x_half, x_done, w2_mm = map(sem, (
            "w_in", "made", "gt", "gT_mm", "gT_out", "b_mm", "h_mm", "h_act", "hg", "x_half", "x_done",
            "w2_mm"))
        gated, turns, split, stored, xn_ready = map(sem, ("gated", "turns", "split", "stored", "xn_ready"))
        image_in = [sem(f"image{b}") for b in range(IMAGES)] if saved is not None else []
        block = ctx.enter_context(nc.Block())
        MADE = 3 + PARTS
        SPLIT = 3 * PARTS
        LOT = 4
        AHEAD = 2
        BANK_T, BANK_B, BANK_H, BANK_O = 0, 1, 3, 5

        @block.sync
        def _(sp):
            sp.wait_ge(made, MADE)
            sp.dma_start(w1[:, :, :].rearrange("p (e a) f -> p e (a f)", e=n_exp), w1_d).then_inc(w_in, 16)
            sp.dma_start(w2[:, :, :], w2_d).then_inc(w_in, 16)
            sp.dma_start(b1[:, :], b1_d).then_inc(w_in, 16)
            for k in range(PARTS):
                sp.dma_start(b2[k * n_exp:(k + 1) * n_exp, :], b2_d).then_inc(w_in, 16)
            if saved is not None:
                for b in range(IMAGES):
                    sp.dma_start(XN[:, b * PIX:(b + 1) * PIX],
                                 saved[:, b * PIX:(b + 1) * PIX]).then_inc(image_in[b], 16)
            sp.wait_ge(w_in, 96)
            if saved is not None:
                for b in range(IMAGES):
                    sp.wait_ge(image_in[b], 16)
                    sp.sem_inc(xn_ready, CPI)
            if out is not None:
                with sp.Fori(0, IMAGES) as b:
                    sp.wait_ge(x_done, (b + 1) * CPI + 2)
                    sp.sem_inc(turns, 1)
                    sp.dma_start(out.rearrange("b c n -> c b n")[:, bass.ds(b, 1), :],
                                 X[:, bass.ds(b * PIX, PIX)].rearrange("c (b n) -> c b n", b=1)
                                 ).then_inc(stored, 16)
                sp.wait_ge(stored, 16 * IMAGES)

        @block.gpsimd
        def _(pool):
            pool.memset(sel[:, :, :], 0.0).then_inc(made, 1)
            pool.wait_ge(made, 1)
            for k in range(PARTS):
                pool.affine_select(out=sel[:, :, :], in_=sel[:, :, :], compare_op=ALU.not_equal, fill=1.0,
                                   base=-k * n_exp, pattern=[[-1, n_exp], [0, 128]],
                                   channel_multiplier=1).then_inc(made, 1)
                pool.wait_ge(made, 2 + k)
            pool.memset(gt[:, :, :, :], 0.0).then_inc(made, 1)
            pool.memset(b2[:, :], 0.0).then_inc(made, 1)
            pool.sem_inc(gated, 2)
            pool.wait_ge(made, MADE)
            pool.wait_ge(split, SPLIT)

            def fill(b, n):
                pool.wait_ge(gated, n + 1)
                pool.sem_inc(turns, 1)
                tiles = bass.ds(n * TPC, TPC) if not isinstance(n, int) else slice(n * TPC, (n + 1) * TPC)
                pool.tensor_copy(gt[:, b, :, 0:PARTS * n_exp],
                                 parts[:, tiles, :, :].rearrange("p t k e -> p t (k e)")).then_inc(gt_done, 1)
            fill(0, 0)
            with pool.Fori(0, CHUNKS // LOT) as i:
                for b in range(LOT):
                    fill((b + 1) % 2, i * LOT + b + 1)

        @block.tensor
        def _(pe):
            pe.wait_ge(w_in, 96)
            pe.wait_ge(made, MADE)

            def transpose_gates(b, n):
                pe.wait_ge(gt_done, n + 1)
                pe.wait_ge(gT_out, n + 1)
                for t in range(TPC):
                    tr = nc.tensor.transpose(ps[:, BANK_T, t * TILE:(t + 1) * TILE], gt[:, b, t, :],
                                             core.ident[:, :])
                tr.then_inc(gT_mm, 1)
            transpose_gates(0, 0)
            with pe.Fori(0, CHUNKS // LOT) as i:
                for j in range(LOT * U + 1):
                    if j < LOT * U:
                        b, u = divmod(j, U)
                        n = i * LOT + b
                        q = n * U + u
                        if u == 0:
                            pe.wait_ge(gT_out, n + 2)
                            if saved is not None:
                                pe.wait_ge(xn_ready, n + 1)
                            pe.wait_ge(x_done, n + 1)
                            pe.sem_inc(gated, 1)
                            nc.tensor.matmul(ps[:, BANK_O + b % 2, 0:CHUNK], b2[:, :], gT[:, b % 2, :],
                                             start=True, stop=False)
                        if u == AHEAD:
                            transpose_gates((b + 1) % 2, n + 1)
                        if u % HALVES == 0:
                            e = u // HALVES
                            pe.wait_ge(hg_done, (n * n_exp + e + 1) * HALVES)
                            nc.tensor.matmul(ps[:, BANK_B + e % 2, 0:CHUNK], sel[:, e, :], gTb[:, b % 2, :],
                                             start=True, stop=True).then_inc(b_mm, 1)
                        pe.wait_ge(h_act, q + 1)
                        nc.tensor.matmul(ps[:, BANK_H + u % 2, 0:CHUNK], w1[:, u, :],
                                         XN[:, bass.ds(n * CHUNK, CHUNK)],
                                         start=True, stop=True).then_inc(h_mm, 1)
                    if j >= 1:
                        b, v = divmod(j - 1, U)
                        pe.wait_ge(hg_done, (i * LOT * U + j) + CREDIT)
                        nc.tensor.matmul(ps[:, BANK_O + b % 2, 0:CHUNK], w2[:, v, :], hg[:, v % 2, :],
                                         start=False, stop=v == U - 1).then_inc(w2_mm, 1)

        @block.scalar
        def _(act):
            act.wait_ge(w_in, 96)
            act.sem_inc(gT_out, 1)
            act.sem_inc(h_act, 2)

            def take_gates(b, n):
                act.wait_ge(gT_mm, n + 1)
                act.activation(gTb[:, b, :], ps[:, BANK_T, 0:CHUNK], ACT.Copy)
                act.activation(gT[:, b, :], ps[:, BANK_T, 0:CHUNK], ACT.Copy).then_inc(gT_out, 1)
            take_gates(0, 0)
            with act.Fori(0, CHUNKS // LOT) as i:
                for b in range(LOT):
                    n = i * LOT + b
                    for u in range(U):
                        q = n * U + u
                        if u == AHEAD + 1:
                            act.wait_ge(w2_mm, n * U + 2)
                            take_gates((b + 1) % 2, n + 1)
                        act.wait_ge(h_mm, q + 1)
                        act.wait_ge(hg_done, q - 1 + CREDIT)
                        act.activation(hid[:, u % 2, :], ps[:, BANK_H + u % 2, 0:CHUNK], ACT.Gelu,
                                       bias=b1[:, u:u + 1]).then_inc(h_act, 1)

        @block.vector
        def _(dve):
            sp_ = Steps(dve, split)
            source = gates[:, :, :]
            for k in range(PARTS):
                sp_(dve.tensor_copy(part[:, :, :], source))
                sp_(dve.tensor_copy(parts[:, 0:TILES, k, :], part[:, :, :]))
                if k < PARTS - 1:
                    sp_(dve.tensor_tensor(left[:, :, :], source, part[:, :, :], ALU.subtract))
                    source = left[:, :, :]
            sp_(dve.memset(parts[:, TILES:, :, :], 0.0))
            assert sp_.n == SPLIT
            dve.sem_inc(hg_done, CREDIT)
            dve.sem_inc(x_done, 2)
            dve.sem_inc(w2_mm, 2)
            with dve.Fori(0, CHUNKS // LOT) as i:
                for b in range(LOT):
                    n = i * LOT + b
                    for u in range(U):
                        q = n * U + u
                        dve.wait_ge(h_act, q + 1 + 2)
                        dve.wait_ge(b_mm, n * n_exp + u // HALVES + 1)
                        dve.wait_ge(w2_mm, q + 1)
                        nc.vector.tensor_tensor(hg[:, u % 2, :], hid[:, u % 2, :],
                                                ps[:, BANK_B + u // HALVES % 2, 0:CHUNK],
                                                ALU.mult).then_inc(hg_done, 1)
                    here = bass.ds(n * CHUNK, CHUNK)
                    if residual:
                        nc.vector.tensor_tensor(X[:, here], X[:, here], XN[:, here], ALU.add).then_inc(x_half, 1)
                        dve.wait_ge(x_half, n + 1)
                    dve.wait_ge(w2_mm, (n + 1) * U + 2)
                    nc.vector.tensor_tensor(X[:, here], X[:, here], ps[:, BANK_O + b % 2, 0:CHUNK],
                                            ALU.add).then_inc(x_done, 1)


def expert_phase_0(core, p):
    nc = core.nc
    with ExitStack() as ctx:
        logits = ctx.enter_context(nc.sbuf_tensor("logits", [128, TILES, 8], F32))
        gates = ctx.enter_context(nc.sbuf_tensor("gates0", [128, TILES, 8], F32))
        normalise(core, "ln2", 1, p["router_w"], 8, logits)
        route_by_logits(core, logits, gates)
        experts(core, "e0", 8, gates, p["w1"].rearrange("e d f -> d e f"), p["b1"],
                p["w2"].rearrange("e f c -> f e c"), p["b2"], True)


PAD = 64


CORNERS = (0, 1, SIDE, SIDE + 1)


def offsets(core, p, om, x_dram, table):
    nc, X, XN, ps = core.nc, core.X, core.XN, core.psum
    K3 = 3 * TAPS
    WIDE = SIDE + 2
    ROWS = CHUNK // SIDE
    with ExitStack() as ctx:
        sem = lambda k: core.semaphore(ctx, f"of_{k}")
        sb = lambda k, s: ctx.enter_context(nc.sbuf_tensor(f"of_{k}", s, F32))
        SPAN = 32
        w, bias = sb("w", [128, 3, 128 // SPAN, SPAN]), sb("bias", [128, 1])
        sum_up = sb("sum_up", [128, K3])
        zeros, zeros_made = sb("zeros", [PAD, D]), sem("zeros")
        padded, cols = sb("padded", [128, 2, WIDE, WIDE]), sb("cols", [128, 2, CHUNK])
        w_in, zeroed, pad_done, conv_mm, conv_out, t_mm, t_out, saved, turns = map(sem, (
            "w_in", "zeroed", "pad", "conv_mm", "conv_out", "t_mm", "t_out", "saved", "turns"))
        block = ctx.enter_context(nc.Block())

        @block.sync
        def _(sp):
            sp.wait_ge(zeroed, 1)
            for y in range(3):
                sp.dma_start(w[:, y, 0:3, 0:K3], p["w_off"][:, 3 * y:3 * y + 3, :]).then_inc(w_in, 16)
            sp.dma_start(bias[SPAN:SPAN + K3, :], p["b_off"].rearrange("(c a) -> c a", a=1)).then_inc(w_in, 16)
            for b in range(IMAGES):
                sp.dma_start(x_dram[b, :, :], X[:, b * PIX:(b + 1) * PIX]).then_inc(saved, 16)
            sp.wait_ge(zeros_made, 1)
            ends = [(c, lo, hi) for c, back in enumerate(CORNERS)
                    for lo, hi in ((0, PAD - back), (T + PAD - back, T + PAD)) if hi > lo]
            for c, lo, hi in ends:
                sp.dma_start(table[lo:hi, c * D:(c + 1) * D], zeros[0:hi - lo, :]).then_inc(saved, 16)
            sp.wait_ge(w_in, 64)
            sp.wait_ge(saved, 16 * (IMAGES + len(ends)))

        @block.gpsimd
        def _(pool):
            pool.memset(w[:, :, :, :], 0.0).then_inc(zeroed, 1)
            pool.memset(zeros[:, :], 0.0).then_inc(zeros_made, 1)
            pool.memset(padded[:, :, :, :], 0.0).then_inc(zeroed, 1)
            pool.memset(cols[:, :, :], 0.0).then_inc(zeroed, 1)
            pool.memset(sum_up[:, :], 0.0).then_inc(zeroed, 1)
            for x in range(3):
                pool.wait_ge(zeroed, 4 + x)
                pool.affine_select(out=sum_up[:, :], in_=sum_up[:, :], compare_op=ALU.not_equal, fill=1.0,
                                   base=-x * SPAN, pattern=[[-1, K3]], channel_multiplier=1).then_inc(zeroed, 1)
            with pool.Fori(0, IMAGES // 2) as i:
                for b in range(2):
                    img = 2 * i + b
                    pool.wait_ge(conv_mm, (img + 1) * CPI)
                    pool.sem_inc(turns, 1)
                    pool.tensor_copy(padded[:, b, 1:1 + SIDE, 1:1 + SIDE],
                                     XN[:, bass.ds(img * PIX, PIX)].rearrange("p (y x) -> p y x", x=SIDE)
                                     ).then_inc(pad_done, 1)

        @block.tensor
        def _(pe):
            pe.sem_inc(conv_mm, 2 * CPI)
            pe.wait_ge(w_in, 64)
            pe.wait_ge(zeroed, 7)
            with pe.Fori(0, IMAGES // 2) as i:
                for b in range(2):
                    img = 2 * i + b
                    pe.wait_ge(pad_done, img + 1)
                    for c in range(CPI + 1):
                        n = img * CPI + c
                        if c < CPI:
                            pe.wait_ge(conv_out, n + 1)
                            for k in range(3):
                                y = ROWS * c + k
                                mm = nc.tensor.matmul(ps[:, c % 2, 0:CHUNK],
                                                      w[:, k, :, :].rearrange("p x o -> p (x o)"),
                                                      padded[:, b, y:y + ROWS, 1:1 + SIDE],
                                                      start=k == 0, stop=k == 2)
                            mm.then_inc(conv_mm, 1)
                        if c >= 1:
                            m = n - 1
                            pe.wait_ge(conv_out, m + 1 + 2)
                            pe.wait_ge(t_out, m + 1)
                            pe.sem_inc(turns, 1)
                            for t in range(TPC):
                                tr = nc.tensor.matmul(ps[:, 2 + (c - 1) % 2, t * K3:(t + 1) * K3],
                                                      cols[:, (c - 1) % 2, t * TILE:(t + 1) * TILE],
                                                      sum_up[:, :], start=True, stop=True)
                            tr.then_inc(t_mm, 1)

        @block.scalar
        def _(act):
            act.sem_inc(conv_out, 2)
            act.sem_inc(t_mm, 2)
            act.wait_ge(w_in, 64)
            act.wait_ge(zeroed, 3)
            with act.Fori(0, IMAGES) as img:
                for c in range(CPI):
                    n = img * CPI + c
                    act.wait_ge(conv_mm, n + 1 + 2 * CPI)
                    act.wait_ge(t_mm, n + 1)
                    rows = lambda a: a.rearrange("p (y x) -> p y x", x=SIDE)
                    for x, to, of in ((0, 1, 0), (2, 0, 1), (1, 0, 0)):
                        n_px = SIDE - (x != 1)
                        block_rows = slice(x * SPAN, x * SPAN + K3)
                        dst = rows(cols[block_rows, c % 2, :])[:, :, to:to + n_px]
                        src = rows(ps[block_rows, c % 2, 0:CHUNK])[:, :, of:of + n_px]
                        if x == 1:
                            act.activation(dst, src, ACT.Identity, bias=bias[block_rows, :]).then_inc(conv_out, 1)
                        else:
                            act.activation(dst, src, ACT.Copy)

        @block.vector
        def _(dve):
            dve.sem_inc(t_out, 2)
            with dve.Fori(0, IMAGES) as img:
                for c in range(CPI):
                    n = img * CPI + c
                    dve.wait_ge(t_mm, n + 1 + 2)
                    dve.tensor_copy(om[:, bass.ds(n * TPC, TPC), :],
                                    ps[:, 2 + c % 2, 0:TPC * K3].rearrange("p (t k) -> p t k", t=TPC)
                                    ).then_inc(t_out, 1)


def sample_points(core, om, index, corner_w):
    nc = core.nc
    N = TILES * TAPS
    TOP = SIDE - 2
    with ExitStack() as ctx:
        sem = lambda k: core.semaphore(ctx, f"sp_{k}")
        free = core.XN
        part = lambda k: free[:, k * N:(k + 1) * N]
        grid = lambda k: part(k).rearrange("p (t k) -> p t k", k=TAPS)
        point, low, over, near, far = (grid(k) for k in range(5))
        wy, wx, mask, base = [grid(5), grid(6)], [grid(7), grid(8)], grid(9), grid(10)
        flat = free[:, 11 * N:11 * N + 4 * TILES].rearrange("p (a t) -> p a t", a=4)
        row, col, pix, start = (flat[:, k, :] for k in range(4))
        cmp = free[:, 0:TILES * (SIDE - 1)].rearrange("p (t m) -> p t m", m=SIDE - 1)
        marks = ctx.enter_context(nc.sbuf_tensor("sp_marks", [128, SIDE - 1], F32))
        ints = ctx.enter_context(nc.sbuf_tensor("sp_ints", [128, TILES, TAPS], I32))
        small = ctx.enter_context(nc.sbuf_tensor("sp_small", [128, 2 * TILES + SIDE - 1], I32))
        made, steps, masked = sem("made"), sem("steps"), sem("masked")
        block = ctx.enter_context(nc.Block())

        @block.gpsimd
        def _(pool):
            pool.iota(small[:, 0:TILES], pattern=[[0, IMAGES], [TILE, TPI]], base=0,
                      channel_multiplier=1).then_inc(made, 1)
            pool.iota(small[:, TILES:2 * TILES], pattern=[[PIX, IMAGES], [0, TPI]], base=PAD,
                      channel_multiplier=0).then_inc(made, 1)
            pool.iota(small[:, 2 * TILES:], pattern=[[SIDE, SIDE - 1]], base=SIDE,
                      channel_multiplier=0).then_inc(made, 1)

        @block.scalar
        def _(act):
            act.activation(mask, om[:, :, 2 * TAPS:], ACT.Sigmoid).then_inc(masked, 1)

        @block.vector
        def _(dve):
            st = Steps(dve, steps)
            wide = lambda a: a.rearrange("p (t e) -> p t e", e=1)
            dve.wait_ge(made, 3)
            st.mark(dve.tensor_copy(pix, small[:, 0:TILES]))
            st.mark(dve.tensor_copy(start, small[:, TILES:2 * TILES]))
            st(dve.tensor_copy(marks[:, :], small[:, 2 * TILES:]))
            st(dve.tensor_tensor(cmp, wide(pix).to_broadcast([128, TILES, SIDE - 1]),
                                 marks[:, :].rearrange("p (t m) -> p t m", t=1).to_broadcast([128, TILES, SIDE - 1]),
                                 ALU.is_ge))
            st(dve.tensor_reduce(row, cmp, AX.X, ALU.add))
            st(dve.scalar_tensor_tensor(out=col, in0=row, scalar=-float(SIDE), in1=pix, op0=ALU.mult, op1=ALU.add))
            for axis, at, weights in ((0, row, wy), (1, col, wx)):
                for k in range(TAPS):
                    shift = float((k // 3 if axis == 0 else k % 3) - 1)
                    st.mark(dve.tensor_scalar(point[:, :, k:k + 1], wide(at), shift, None, ALU.add))
                st.done()
                st(dve.tensor_tensor(point, point, om[:, :, axis * TAPS:(axis + 1) * TAPS], ALU.add))
                st(dve.tensor_scalar(near, point, 0.0, float(TOP), ALU.max, ALU.min))
                st(dve.tensor_copy(ints[:, :, :], near))
                st(dve.tensor_copy(low, ints[:, :, :]))
                st(dve.tensor_tensor(over, low, near, ALU.is_gt))
                st(dve.tensor_tensor(low, low, over, ALU.subtract))
                st(dve.tensor_tensor(near, point, low, ALU.subtract))
                st(dve.tensor_scalar(far, near, 1.0, None, ALU.subtract))
                for k, dist in enumerate((near, far)):
                    st(dve.scalar_tensor_tensor(out=over, in0=dist, scalar=-1.0, in1=dist, op0=ALU.mult, op1=ALU.max))
                    st(dve.tensor_scalar(over, over, -1.0, 1.0, ALU.mult, ALU.add))
                    st(dve.tensor_scalar(weights[k], over, 0.0, None, ALU.max))
                if axis == 0:
                    st(dve.tensor_scalar(base, low, float(SIDE), None, ALU.mult))
                else:
                    st(dve.tensor_tensor(base, base, low, ALU.add))
            st(dve.tensor_tensor(base, base, wide(start).to_broadcast([128, TILES, TAPS]), ALU.add))
            st(dve.tensor_copy(index[:, :, :], base))
            dve.wait_ge(masked, 1)
            for a in range(2):
                st(dve.tensor_tensor(wy[a], wy[a], mask, ALU.mult))
                for b in range(2):
                    st(dve.tensor_tensor(corner_w[:, :, :, 2 * a + b], wy[a], wx[b], ALU.mult))


def deform(core, p, table, index, corner_w):
    nc, Y, ps = core.nc, core.X, core.psum
    RING = 3
    with ExitStack() as ctx:
        sem = lambda k: core.semaphore(ctx, f"df_{k}")
        sb = lambda k, s, d=F32: ctx.enter_context(nc.sbuf_tensor(f"df_{k}", s, d))
        BUFS = 3
        patches = core.XN[:, 0:BUFS * TAPS * 4 * D].rearrange("p (b k c) -> p b k c", b=BUFS, k=TAPS)
        ibuf = sb("ibuf", [128, BUFS, TAPS], I32)
        at = BUFS * TAPS * 4 * D
        diag = core.XN[:, at:at + RING * 4 * TILE].rearrange("p (r c n) -> p r c n", r=RING, c=4)
        at += RING * 4 * TILE
        blended = core.XN[:, at:at + RING * 3 * TILE].rearrange("p (r k n) -> p r k n", r=RING, k=3)
        w, bias = sb("w", [128, TAPS, D]), sb("bias", [128, 1])
        w_in, i_done, diag_done, tap_mm, blend_out, y_mm, y_out, turns = map(sem, (
            "w_in", "index", "diag", "tap_mm", "blend_out", "y_mm", "y_out", "turns"))
        in_ = [sem(f"in{b}") for b in range(BUFS)]
        block = ctx.enter_context(nc.Block())

        @block.sync
        def _(sp):
            sp.dma_start(w[:, :, :], p["weight"]).then_inc(w_in, 16)
            sp.dma_start(bias[:, :], p["bias"].rearrange("(c a) -> c a", a=1)).then_inc(w_in, 16)
            sp.wait_ge(w_in, 32)

        @block.gpsimd
        def _(pool):
            with pool.Fori(0, TILES // BUFS) as i:
                for b in range(BUFS):
                    t = BUFS * i + b
                    pool.wait_ge(tap_mm, TAPS * (t + 1))
                    pool.sem_inc(turns, 1)
                    pool.tensor_copy(ibuf[:, b, :], index[:, bass.ds(t, 1), :]).then_inc(i_done, 1)
                    pool.wait_ge(i_done, t + 1)
                    pool.sem_inc(turns, 1)
                    for k in range(TAPS):
                        pool.indirect_dma_start(
                            out=patches[:, b, k, :], out_offset=None, in_=table,
                            in_offset=bass.IndirectOffsetOnAxis(ap=ibuf[:, b, k:k + 1], axis=0)).then_inc(in_[b], 16)

        @block.tensor
        def _(pe):
            pe.sem_inc(tap_mm, BUFS * TAPS)
            pe.wait_ge(w_in, 32)
            with pe.Fori(0, TILES // (2 * BUFS)) as i:
                for u in range(2 * BUFS):
                    t = 2 * BUFS * i + u
                    b, o = u % BUFS, u % 2
                    pe.wait_ge(in_[b], 16 * TAPS * (2 * i + u // BUFS + 1))
                    for g in range(4):
                        if g < 3:
                            pe.wait_ge(blend_out, 3 * t + g + 1)
                            for k in range(3 * g, 3 * g + 3):
                                pe.wait_ge(diag_done, TAPS * t + k + 1)
                                for c in range(4):
                                    mm = nc.tensor.matmul(ps[:, g, (k % 3) * TILE:(k % 3 + 1) * TILE],
                                                          patches[:, b, k, c * D:(c + 1) * D], diag[:, k % RING, c, :],
                                                          start=c == 0, stop=c == 3)
                                mm.then_inc(tap_mm, 1)
                        if g == 0:
                            pe.wait_ge(y_out, t + 1)
                        else:
                            pe.wait_ge(blend_out, 3 * t + g + 3)
                            for k in range(3 * g - 3, 3 * g):
                                mm = nc.tensor.matmul(ps[:, 3 + o, 0:TILE], w[:, k, :],
                                                      blended[:, g - 1, k % 3, :],
                                                      start=k == 0, stop=k == TAPS - 1)
                    mm.then_inc(y_mm, 1)

        @block.scalar
        def _(act):
            act.sem_inc(blend_out, 3)
            act.sem_inc(y_out, 2)
            act.wait_ge(w_in, 32)
            with act.Fori(0, TILES // 2) as i:
                for b in range(2):
                    t = 2 * i + b
                    for g in range(3):
                        act.wait_ge(tap_mm, TAPS * t + 3 * g + 3 + BUFS * TAPS)
                        act.wait_ge(y_mm, t + 1)
                        act.activation(blended[:, g, :, :], ps[:, g, 0:3 * TILE].rearrange("p (k n) -> p k n", k=3),
                                       ACT.Copy).then_inc(blend_out, 1)
                    act.wait_ge(y_mm, t + 2)
                    act.activation(Y[:, bass.ds(t * TILE, TILE)], ps[:, 3 + b, 0:TILE], ACT.Identity,
                                   bias=bias[:, :]).then_inc(y_out, 1)

        @block.vector
        def _(dve):
            dve.sem_inc(y_mm, 1)
            with dve.Fori(0, TILES // 2) as i:
                for b in range(2):
                    t = 2 * i + b
                    for k in range(TAPS):
                        dve.wait_ge(tap_mm, TAPS * t + k + 1 + BUFS * TAPS - RING)
                        dve.tensor_tensor(
                            diag[:, k % RING, :, :],
                            core.ident[:, :].rearrange("p (c n) -> p c n", c=1).to_broadcast([128, 4, TILE]),
                            corner_w[:, bass.ds(t, 1), k, :].rearrange("p a (c n) -> p (a c) n", n=1)
                            .to_broadcast([128, 4, TILE]),
                            ALU.mult).then_inc(diag_done, 1)


def batch_norm(core, p, x_dram):
    nc, Y = core.nc, core.X
    LOT = 4
    with ExitStack() as ctx:
        sem = lambda k: core.semaphore(ctx, f"bn_{k}")
        sb = lambda k, s: ctx.enter_context(nc.sbuf_tensor(f"bn_{k}", s, F32))
        stats, agg, par = sb("stats", [128, CHUNKS, 6]), sb("agg", [128, 2]), sb("par", [128, 2])
        scale, shift, old = sb("scale", [128, 1]), sb("shift", [128, 1]), sb("old", [128, LOT, CHUNK])
        p_in, counted, steps, var_done, sd_done, ready, relu_done, x_done = map(sem, (
            "p_in", "counted", "steps", "var", "sd", "ready", "relu", "x"))
        old_in = [sem(f"old{b}") for b in range(LOT)]
        block = ctx.enter_context(nc.Block())

        @block.sync
        def _(sp):
            for j, q in enumerate(("gamma", "beta")):
                sp.dma_start(par[:, j:j + 1], p[q].rearrange("(c a) -> c a", a=1)).then_inc(p_in, 16)
            sp.wait_ge(p_in, 32)
            with sp.Fori(0, CHUNKS // LOT) as i:
                for b in range(LOT):
                    n = LOT * i + b
                    sp.wait_ge(x_done, n + 1)
                    sp.dma_start(old[:, b, :], x_dram[:, bass.ds(n * CHUNK, CHUNK)]).then_inc(old_in[b], 16)

        @block.vector
        def _(dve):
            st = Steps(dve, steps)
            dve.sem_inc(x_done, LOT)
            with dve.Fori(0, CHUNKS) as n:
                dve.bn_stats(stats[:, bass.ds(n, 1), :], Y[:, bass.ds(n * CHUNK, CHUNK)]).then_inc(counted, 1)
            dve.wait_ge(counted, CHUNKS)
            st(dve.bn_aggr(agg[:, :], stats[:, :, :]))
            dve.tensor_scalar(scale[:, :], agg[:, 1:2], 1e-5, None, ALU.add).then_inc(var_done, 1)
            dve.wait_ge(sd_done, 1)
            dve.wait_ge(p_in, 32)
            st(dve.reciprocal(scale[:, :], scale[:, :]))
            st(dve.tensor_tensor(scale[:, :], scale[:, :], par[:, 0:1], ALU.mult))
            st(dve.tensor_tensor(shift[:, :], scale[:, :], agg[:, 0:1], ALU.mult))
            dve.tensor_tensor(shift[:, :], par[:, 1:2], shift[:, :], ALU.subtract).then_inc(ready, 1)
            with dve.Fori(0, CHUNKS // LOT) as i:
                for b in range(LOT):
                    n = LOT * i + b
                    here = bass.ds(n * CHUNK, CHUNK)
                    dve.wait_ge(relu_done, n + 1)
                    dve.wait_ge(old_in[b], 16 * (i + 1))
                    dve.tensor_tensor(Y[:, here], Y[:, here], old[:, b, :], ALU.add).then_inc(x_done, 1)

        @block.scalar
        def _(act):
            act.wait_ge(var_done, 1)
            act.activation(scale[:, :], scale[:, :], ACT.Sqrt).then_inc(sd_done, 1)
            act.wait_ge(ready, 1)
            with act.Fori(0, CHUNKS) as n:
                here = bass.ds(n * CHUNK, CHUNK)
                act.activation(Y[:, here], Y[:, here], ACT.Relu, bias=shift[:, :],
                               scale=scale[:, :]).then_inc(relu_done, 1)


def deform_phase(core, p):
    nc = core.nc
    table = nc.dram_tensor("corner_table", (T + PAD, 4 * D), F32, kind="Internal").ap()
    x_dram = nc.dram_tensor("x_saved", (D, T), F32, kind="Internal").ap()
    by_image = x_dram.rearrange("c (b n) -> b c n", b=IMAGES)

    def stores(n):
        for c, back in enumerate(CORNERS):
            yield table[bass.ds(n * CHUNK + PAD - back, CHUNK), c * D:(c + 1) * D] \
                .rearrange("(t p) c -> p t c", p=TILE)

    with ExitStack() as ctx:
        sb = lambda k, s, d=F32: ctx.enter_context(nc.sbuf_tensor(f"dp_{k}", s, d))
        om = sb("om", [128, TILES, 3 * TAPS])
        normalise(core, "ln3", 0, None, D, None, stores)
        offsets(core, p, om, by_image, table)
        index, corner_w = sb("index", [128, TILES, TAPS], I32), sb("corner_w", [128, TILES, TAPS, 4])
        sample_points(core, om, index, corner_w)
        deform(core, p, table, index, corner_w)
    batch_norm(core, p, x_dram)


EDGES = 524288
WIDTH = EDGES // 128
RUN = 128
RUNS = EDGES // RUN
BLOCK = 128 * RUN
BLOCKS = RUNS // 128
DST_BIAS = 256
ID_BITS = 15
HEADS, GE = 4, 4
HF = HEADS * GE
SRC_ROW = HEADS + HF
STATE = HEADS + HEADS + HF
LEAK = 0.2


def sort_edges(core, edges, x, d, zeroed):
    nc, ps = core.nc, core.psum
    K = [core.XN[:, k * WIDTH:(k + 1) * WIDTH] for k in range(2)]
    W_BITS, BITS = WIDTH.bit_length() - 1, EDGES.bit_length() - 1
    half = lambda buf, j: buf.rearrange("p (u two l) -> p u two l", two=2, l=1 << j)
    with ExitStack() as ctx:
        sem = lambda k: core.semaphore(ctx, f"so_{k}")
        sign, turn, bits = (ctx.enter_context(nc.sbuf_tensor(f"so_{k}", [128, 8], t))
                            for k, t in (("sign", F32), ("turn", F32), ("bits", I32)))
        loaded, lanes, steps, sorted_, t_mm, t_out, out_ready, stored = map(sem, (
            "loaded", "lanes", "steps", "sorted", "t_mm", "t_out", "out_ready", "stored"))
        block = ctx.enter_context(nc.Block())
        n_swaps = 2 * (BITS - W_BITS)
        ZEROS = 4096
        cleared, x_loaded = sem("cleared"), sem("x_loaded")
        zeros = ctx.enter_context(nc.sbuf_tensor("so_zeros", [128, ZEROS], F32))

        @block.gpsimd
        def _(pool):
            pool.iota(bits[:, :], pattern=[[0, 8]], base=0, channel_multiplier=1).then_inc(lanes, 1)
            pool.memset(zeros[:, :], 0.0).then_inc(lanes, 1)

        final, outs, cur_of_swap = [], {}, []

        @block.vector
        def _(dve):
            st = Steps(dve, steps)
            dve.wait_ge(lanes, 1)
            for b in range(7):
                st.mark(dve.tensor_scalar(bits[:, b:b + 1], bits[:, b:b + 1], b, 1, ALU.logical_shift_right,
                                          ALU.bitwise_and))
            st.done()
            st(dve.tensor_copy(sign[:, 0:7], bits[:, 0:7]))
            st(dve.tensor_scalar(sign[:, 0:7], sign[:, 0:7], -2.0, 1.0, ALU.mult, ALU.add))
            st(dve.tensor_tensor(turn[:, 0:6], sign[:, 0:6], sign[:, 1:7], ALU.mult))
            dve.wait_ge(loaded, 32)
            src, dst = K[0].bitcast(I32), K[1].bitcast(I32)
            st(dve.tensor_scalar(dst, dst, DST_BIAS, None, ALU.add))
            st(dve.tensor_scalar(dst, dst, ID_BITS, None, ALU.logical_shift_left))
            st(dve.tensor_tensor(src, src, dst, ALU.bitwise_or))
            cur, swaps = 0, 0

            def negate(k):
                part = half(K[cur], k)[:, :, 1, :]
                st(dve.tensor_scalar(part, part, -1.0, None, ALU.mult))

            def renegate(k):
                part = K[cur].rearrange("p (u l) -> p u l", l=4 << k)[:, :, 1 << k:3 << k]
                st(dve.tensor_scalar(part, part, -1.0, None, ALU.mult))

            def by_lane(signs, b):
                st(dve.tensor_scalar(K[cur], K[cur], signs[:, b:b + 1], None, ALU.mult))

            def compare(j):
                nonlocal cur
                a, b = half(K[cur], j), half(K[1 - cur], j)
                st.mark(dve.tensor_tensor(b[:, :, 0, :], a[:, :, 0, :], a[:, :, 1, :], ALU.min))
                st(dve.tensor_tensor(b[:, :, 1, :], a[:, :, 0, :], a[:, :, 1, :], ALU.max))
                cur = 1 - cur

            def swap():
                nonlocal cur, swaps
                dve.sem_inc(sorted_, 1)
                swaps += 1
                cur_of_swap.append(cur)
                cur = 1 - cur
                dve.wait_ge(t_out, 8 * swaps)

            negate(1)
            for k in range(1, BITS + 1):
                if k > W_BITS:
                    swap()
                    for j in reversed(range(k - W_BITS)):
                        compare(j)
                    swap()
                for j in reversed(range(min(k, W_BITS))):
                    compare(j)
                if k < W_BITS - 1:
                    renegate(k)
                elif k == W_BITS - 1:
                    negate(k)
                    by_lane(sign, 0)
                elif k < BITS - 1:
                    by_lane(turn, k - W_BITS)
                elif k == BITS - 1:
                    by_lane(sign, k - W_BITS)
            assert swaps == n_swaps
            keys = K[cur]
            final.append(keys)
            dve.sem_inc(out_ready, 1)
            ikeys = keys.bitcast(I32)
            at = 2 * WIDTH
            source = core.XN[:, at:at + WIDTH].bitcast(I32)
            same = core.XN[:, at + WIDTH:at + 2 * WIDTH]
            target = K[1 - cur].bitcast(I32)
            at += 2 * WIDTH
            R = WIDTH // RUN
            first, last, run_target = (core.XN[:, at + k * R:at + (k + 1) * R] for k in range(3))
            by_run = lambda a: a.rearrange("p (r f) -> p r f", f=RUN)
            one = lambda a: a.rearrange("p (r f) -> p r f", f=1)
            st(dve.tensor_scalar(source, ikeys, (1 << ID_BITS) - 1, None, ALU.bitwise_and))
            dve.tensor_scalar(source, source, T - 1, None, ALU.min).then_inc(out_ready, 1)
            st(dve.tensor_scalar(target, ikeys, ID_BITS, None, ALU.logical_shift_right))
            st(dve.tensor_tensor(same[:, 1:WIDTH], target[:, 1:WIDTH], target[:, 0:WIDTH - 1], ALU.is_equal))
            dve.memset(by_run(same)[:, :, 0:1], 0.0).then_inc(out_ready, 1)
            st.mark(dve.tensor_copy(one(first), by_run(keys)[:, :, 0:1]))
            st(dve.tensor_copy(one(last), by_run(keys)[:, :, RUN - 1:RUN]))
            dve.sem_inc(out_ready, 1)
            dve.tensor_scalar(one(run_target.bitcast(I32)), by_run(target)[:, :, 0:1], -DST_BIAS, T - 1, ALU.add,
                              ALU.min).then_inc(out_ready, 1)
            outs.update(source=source, same=same, first=first, last=last, run_target=run_target.bitcast(I32))

        @block.tensor
        def _(pe):
            for n, cur in enumerate(cur_of_swap):
                pe.wait_ge(sorted_, n + 1)
                for q in range(8):
                    m = 8 * n + q
                    if m >= 4:
                        pe.wait_ge(t_out, m - 3)
                    for t in range(4):
                        tr = nc.tensor.transpose(ps[:, q % 4, t * 128:(t + 1) * 128],
                                                 K[cur][:, (4 * q + t) * 128:(4 * q + t + 1) * 128], core.ident[:, :])
                    tr.then_inc(t_mm, 1)

        @block.scalar
        def _(act):
            for n, cur in enumerate(cur_of_swap):
                for q in range(8):
                    act.wait_ge(t_mm, 8 * n + q + 1)
                    act.activation(K[1 - cur][:, q * 512:(q + 1) * 512], ps[:, q % 4, :], ACT.Copy).then_inc(t_out, 1)

        @block.sync
        def _(sp):
            for k in range(2):
                sp.dma_start(K[k].bitcast(I32), edges[k, :].rearrange("(p f) -> p f", p=128)).then_inc(loaded, 16)
            for b in range(IMAGES):
                sp.dma_start(core.X[:, b * PIX:(b + 1) * PIX], x[b, :, :]).then_inc(x_loaded, 16)
            sp.wait_ge(lanes, 2)
            n = 0
            for table in zeroed:
                rows, width = table.shape
                per = rows * width // 128
                flat = table.rearrange("r c -> (r c)").rearrange("(p f) -> p f", p=128)
                for at in range(0, per, ZEROS):
                    size = min(ZEROS, per - at)
                    sp.dma_start(flat[:, at:at + size], zeros[:, 0:size]).then_inc(cleared, 16)
                    n += 16
            sp.wait_ge(cleared, n)
            sp.wait_ge(x_loaded, 16 * IMAGES)
            sp.wait_ge(loaded, 32)
            sp.wait_ge(out_ready, 1)
            ordered = lambda a: a.rearrange("(p f) -> p f", p=128)
            sp.dma_start(ordered(d["keys"]), final[0]).then_inc(stored, 16)
            sp.wait_ge(out_ready, 5)
            sp.dma_start(ordered(d["source"]), outs["source"]).then_inc(stored, 16)
            sp.dma_start(ordered(d["same"]), outs["same"]).then_inc(stored, 16)
            sp.dma_start(ordered(d["first"]), outs["first"]).then_inc(stored, 16)
            sp.dma_start(ordered(d["last"]), outs["last"]).then_inc(stored, 16)
            sp.dma_start(ordered(d["run_target"]), outs["run_target"]).then_inc(stored, 16)
            sp.wait_ge(stored, 16 * 6)


def gather(core, name, table, width, index, tiles, lot, consume, sems=()):
    nc = core.nc
    lots = tiles // lot
    assert lots * lot == tiles
    with ExitStack() as ctx:
        sem = lambda k: core.semaphore(ctx, f"{name}_{k}")
        ibuf = ctx.enter_context(nc.sbuf_tensor(f"{name}_ibuf", [128, 2, lot], I32))
        rows = ctx.enter_context(nc.sbuf_tensor(f"{name}_rows", [128, 2, lot, width], F32))
        i_done, used, turns = sem("index"), sem("used"), sem("turns")
        in_ = [sem("in0"), sem("in1")]
        block = ctx.enter_context(nc.Block())

        @block.gpsimd
        def _(pool):
            def fetch(b, n):
                pool.wait_ge(i_done, n + 1)
                pool.wait_ge(used, n + 1)
                pool.sem_inc(turns, 1)
                for k in range(lot):
                    pool.indirect_dma_start(out=rows[:, b, k, :], out_offset=None, in_=table,
                                            in_offset=bass.IndirectOffsetOnAxis(ap=ibuf[:, b, k:k + 1], axis=0)
                                            ).then_inc(in_[b], 16)

            if lots > 1:
                with pool.Fori(0, lots // 2) as i:
                    for b in range(2):
                        fetch(b, 2 * i + b)
            if lots % 2:
                fetch(0, lots - 1)

        @block.vector
        def _(dve):
            dve.sem_inc(used, 2)

            def indices(b, n):
                dve.tensor_copy(ibuf[:, b, :], index[:, bass.ds(n * lot, lot)]).then_inc(i_done, 1)

            def take(b, n, times):
                dve.wait_ge(in_[b], 16 * lot * times)
                consume(dve, n, rows[:, b, :, :], used)

            if lots > 1:
                with dve.Fori(0, lots // 2) as i:
                    for b in range(2):
                        indices(b, 2 * i + b)
                    for b in range(2):
                        take(b, 2 * i + b, i + 1)
            if lots % 2:
                indices(0, lots - 1)
                take(0, lots - 1, lots // 2 + 1)


def find_starts(core, d, start, end):
    nc, ps = core.nc, core.psum
    N = TILES + 1
    GROUPS = RUNS // 128
    with ExitStack() as ctx:
        sb = lambda k, s, t=F32: ctx.enter_context(nc.sbuf_tensor(f"fs_{k}", s, t))
        least, iblk = sb("least", [128, N], I32), sb("iblk", [128, N], I32)
        blk, cnt, pos = sb("blk", [128, N]), sb("cnt", [128, N]), sb("pos", [128, N])
        next_lane, wrap = sb("next_lane", [128, 128]), sb("wrap", [128, 128])
        sb2 = lambda k, s: sb(k, s, BF16)
        lower_lane, same_tile, lower_tile, ones = (sb2("lower_lane", [128, GROUPS, 128]),
                                                   sb2("same_tile", [128, GROUPS, N]),
                                                   sb2("lower_tile", [128, GROUPS, N]), sb2("ones", [128, 128]))
        firsts, ints = sb("firsts", [128, GROUPS]), sb("ints", [128, 2, GROUPS], I32)
        tile_lane, counts = sb("tile_lane", [128, 2, GROUPS]), sb("counts", [128, N])
        icounts = sb("icounts", [128, N], I32)
        wide = lambda a, n: a.rearrange("p (t s) -> p t s", s=1).to_broadcast([128, a.shape[1], n])
        key = least[:, :].bitcast(F32)
        with ExitStack() as c2:
            sem = lambda k: core.semaphore(c2, f"fs_{k}")
            made, loaded, steps, compared, counted = map(sem, ("made", "loaded", "steps", "compared", "counted"))
            block = c2.enter_context(nc.Block())

            @block.sync
            def _(sp):
                sp.dma_start(firsts[:, :], d["first"].rearrange("(p g) -> p g", p=128)).then_inc(loaded, 16)
                sp.wait_ge(loaded, 16)

            @block.gpsimd
            def _(pool):
                pool.iota(least[:, :], pattern=[[TILE, N]], base=DST_BIAS, channel_multiplier=1).then_inc(made, 1)
                pool.memset(next_lane[:, :], 0.0).then_inc(made, 1)
                pool.memset(wrap[:, :], 0.0).then_inc(made, 1)
                pool.wait_ge(made, 3)
                pool.affine_select(out=next_lane[:, :], in_=next_lane[:, :], compare_op=ALU.not_equal, fill=1.0,
                                   base=-1, pattern=[[-1, 128]], channel_multiplier=1).then_inc(made, 1)
                pool.affine_select(out=wrap[:, :], in_=wrap[:, :], compare_op=ALU.not_equal, fill=1.0,
                                   base=127, pattern=[[-1, 128]], channel_multiplier=128).then_inc(made, 1)
                pool.iota(icounts[:, :], pattern=[[1, N]], base=0, channel_multiplier=0).then_inc(made, 1)
                pool.memset(ones[:, :], 1.0).then_inc(made, 1)

            @block.tensor
            def _(pe):
                pe.wait_ge(compared, 3)
                pe.wait_ge(made, 7)
                for g in range(GROUPS):
                    nc.tensor.matmul(ps[:, 0, 0:N], lower_lane[:, g, :], same_tile[:, g, :],
                                     start=g == 0, stop=False)
                    mm = nc.tensor.matmul(ps[:, 0, 0:N], ones[:, :], lower_tile[:, g, :],
                                          start=False, stop=g == GROUPS - 1)
                mm.then_inc(counted, 1)

            @block.vector
            def _(dve):
                st = Steps(dve, steps)
                dve.wait_ge(made, 7)
                st(dve.tensor_scalar(least[:, :], least[:, :], ID_BITS, None, ALU.logical_shift_left))
                st(dve.tensor_copy(counts[:, :], icounts[:, :]))
                dve.wait_ge(loaded, 16)
                tile, lane = ints[:, 0, :], ints[:, 1, :]
                st(dve.tensor_scalar(lane, firsts[:, :].bitcast(I32), ID_BITS, None, ALU.logical_shift_right))
                st(dve.tensor_scalar(lane, lane, -DST_BIAS, None, ALU.add))
                st(dve.tensor_scalar(tile, lane, TILE.bit_length() - 1, None, ALU.logical_shift_right))
                st(dve.tensor_scalar(lane, lane, TILE - 1, None, ALU.bitwise_and))
                st(dve.tensor_copy(tile_lane[:, :, :], ints[:, :, :]))
                of = lambda k, n: tile_lane[:, k, :].rearrange("p (g n) -> p g n", n=1).to_broadcast([128, GROUPS, n])
                upto = lambda n: counts[:, 0:n].rearrange("p (g n) -> p g n", g=1).to_broadcast([128, GROUPS, n])
                dve.tensor_tensor(lower_lane[:, :, :], of(1, 128), upto(128), ALU.is_lt).then_inc(compared, 1)
                dve.tensor_tensor(same_tile[:, :, :], of(0, N), upto(N), ALU.is_equal).then_inc(compared, 1)
                dve.tensor_tensor(lower_tile[:, :, :], of(0, N), upto(N), ALU.is_lt).then_inc(compared, 1)
                dve.wait_ge(counted, 1)
                st(dve.tensor_copy(blk[:, :], ps[:, 0, 0:N]))
                st(dve.tensor_scalar(blk[:, :], blk[:, :], -1.0, 0.0, ALU.add, ALU.max))
                st(dve.tensor_copy(iblk[:, :], blk[:, :]))

        def count(width, lot):
            compared = core.semaphore(ctx, f"fs_compared{width}")

            def consume(dve, n, rows, used):
                here = bass.ds(n * lot, lot)
                dve.tensor_tensor(rows, rows, wide(key[:, here], width), ALU.is_lt).then_inc(compared, 1)
                dve.wait_ge(compared, n + 1)
                dve.tensor_reduce(cnt[:, here], rows, AX.X, ALU.add).then_inc(used, 1)
            return consume

        gather(core, "fs_keys", d["keys"].rearrange("(r s) -> r s", s=RUN), RUN, iblk, N, 5, count(RUN, 5))

        with ExitStack() as c3:
            placed, moved, copied = (core.semaphore(c3, f"fs_{k}") for k in ("placed", "moved", "copied"))
            pairs_out = core.semaphore(c3, "fs_pairs_out")
            block = c3.enter_context(nc.Block())

            @block.tensor
            def _(pe):
                pe.wait_ge(placed, 1)
                nc.tensor.matmul(ps[:, 0, 0:TILES], next_lane[:, :], pos[:, 0:TILES], start=True, stop=False)
                nc.tensor.matmul(ps[:, 0, 0:TILES], wrap[:, :], pos[:, 1:N], start=False, stop=True).then_inc(moved, 1)

            @block.vector
            def _(dve):
                st = Steps(dve, copied)
                dve.scalar_tensor_tensor(out=pos[:, :], in0=blk[:, :], scalar=float(RUN), in1=cnt[:, :],
                                         op0=ALU.mult, op1=ALU.add).then_inc(placed, 1)
                dve.wait_ge(placed, 1)
                dve.tensor_copy(start[:, :], pos[:, 0:TILES])
                dve.wait_ge(moved, 1)
                st(dve.tensor_copy(end[:, :], ps[:, 0, 0:TILES]))
                st(dve.tensor_scalar(blk[:, 0:1], end[:, TILES - 1:TILES], float(2 * BLOCK - 1), None, ALU.add))
                st(dve.tensor_copy(iblk[:, 0:1], blk[:, 0:1]))
                st(dve.tensor_scalar(iblk[:, 0:1], iblk[:, 0:1], (2 * BLOCK).bit_length() - 1, None,
                                     ALU.logical_shift_right))
                st(dve.tensor_scalar(iblk[:, 0:1], iblk[:, 0:1], 1, None, ALU.max))

            @block.sync
            def _(sp):
                sp.wait_ge(copied, 5)
                sp.dma_start(d["pairs"].rearrange("(p a) -> p a", a=1), iblk[127:128, 0:1]).then_inc(pairs_out, 16)
                sp.wait_ge(pairs_out, 16)


def index_phase(core, edges, x, start, end, zeroed):
    nc = core.nc
    shapes = dict(keys=(EDGES, F32), source=(EDGES, I32), same=(EDGES, F32), first=(RUNS, F32), last=(RUNS, F32),
                  run_target=(RUNS, I32), pairs=(1, I32))
    d = {k: nc.dram_tensor(f"edge_{k}", (n,), t, kind="Internal").ap() for k, (n, t) in shapes.items()}
    sort_edges(core, edges, x, d, zeroed)
    find_starts(core, d, start, end)
    return d


class Carver:

    def __init__(self, buf, parts=128):
        self.buf, self.at, self.parts = buf, 0, parts

    def __call__(self, *shape):
        n = 1
        for k in shape:
            n *= k
        piece = self.buf[0:self.parts, self.at:self.at + n]
        self.at += n
        assert self.at <= self.buf.shape[1]
        names = "abcd"[:len(shape)]
        return piece if len(shape) == 1 else piece.rearrange(
            f"p ({' '.join(names)}) -> p {' '.join(names)}", **dict(zip(names[1:], shape[1:])))


def source_tables(core, p, t, feats, tgt_score, start, end, xn_dram):
    nc, XN = core.nc, core.XN
    LOT = 8
    with ExitStack() as ctx:
        sem = lambda k: core.semaphore(ctx, f"st_{k}")
        sb = lambda k, s, d=F32: ctx.enter_context(nc.sbuf_tensor(f"st_{k}", s, d))
        rows, prod = sb("rows", [128, TILES, SRC_ROW]), sb("prod", [128, TILES, HF])
        att = sb("att", [128, 2, HF])
        where, empty, place = sb("where", [128, TILES]), sb("empty", [128, TILES]), sb("place", [128, TILES], I32)
        ibuf, sbuf = sb("ibuf", [128, 2, LOT], I32), sb("sbuf", [128, 2, LOT, HEADS])
        loaded, steps, made, ready, stored, saved, turns, i_done, spare = map(sem, (
            "loaded", "steps", "made", "ready", "stored", "saved", "turns", "i_done", "spare"))
        freed = sem("freed")
        placed_in = [sem("placed0"), sem("placed1")]
        block = ctx.enter_context(nc.Block())

        @block.sync
        def _(sp):
            for k, q in enumerate(("att_src", "att_dst")):
                sp.dma_start(att[:, k, :], p[q].rearrange("(a h) e -> a (h e)", a=1).to_broadcast([128, HF])
                             ).then_inc(loaded, 16)
            for b in range(IMAGES):
                here = slice(b * PIX, (b + 1) * PIX)
                sp.dma_start(xn_dram[:, here], XN[:, here]).then_inc(saved, 16)
            sp.wait_ge(ready, 1)
            sp.dma_start(t["sources"].rearrange("(t p) c -> p t c", p=TILE), rows[:, :, :]).then_inc(stored, 16)
            sp.dma_start(t["targets"].rearrange("(t p) c -> p t c", p=TILE), tgt_score[:, :, :]).then_inc(stored, 16)
            sp.wait_ge(loaded, 32)
            sp.wait_ge(saved, 16 * IMAGES)
            sp.wait_ge(stored, 32)

        @block.gpsimd
        def _(pool):
            pool.iota(place[:, :], pattern=[[TILE, TILES]], base=EDGES, channel_multiplier=1).then_inc(made, 1)
            with pool.Fori(0, TILES // LOT // 2) as i:
                for b in range(2):
                    pool.wait_ge(i_done, 2 * i + b + 1)
                    pool.sem_inc(turns, 1)
                    for k in range(LOT):
                        pool.indirect_dma_start(
                            out=t["placed"], out_offset=bass.IndirectOffsetOnAxis(ap=ibuf[:, b, k:k + 1], axis=0),
                            in_=sbuf[:, b, k, :], in_offset=None).then_inc(placed_in[b], 16)
                for b in range(2):
                    pool.wait_ge(placed_in[b], 16 * LOT * (i + 1))
                    pool.sem_inc(freed, 1)

        @block.vector
        def _(dve):
            st = Steps(dve, steps)
            dve.sem_inc(freed, 2)
            dve.wait_ge(loaded, 32)
            h = feats[:, :, :]
            by_head = lambda x: x.rearrange("p t (h e) -> p t h e", h=HEADS)
            wide = lambda k: att[:, k, :].rearrange("p (t c) -> p t c", t=1).to_broadcast([128, TILES, HF])
            st.mark(dve.tensor_copy(rows[:, :, HEADS:], h))
            st(dve.tensor_tensor(prod[:, :, :], h, wide(0), ALU.mult))
            st(dve.tensor_reduce(rows[:, :, 0:HEADS], by_head(prod[:, :, :]), AX.X, ALU.add))
            st(dve.tensor_tensor(prod[:, :, :], h, wide(1), ALU.mult))
            dve.tensor_reduce(tgt_score[:, :, :], by_head(prod[:, :, :]), AX.X, ALU.add).then_inc(ready, 1)
            dve.wait_ge(ready, 1)
            dve.wait_ge(made, 1)
            st(dve.tensor_copy(where[:, :], place[:, :]))
            st(dve.tensor_tensor(empty[:, :], start[:, :], end[:, :], ALU.is_equal))
            st(dve.tensor_tensor(where[:, :], where[:, :], start[:, :], ALU.subtract))
            st(dve.tensor_tensor(where[:, :], where[:, :], empty[:, :], ALU.mult))
            st(dve.tensor_tensor(where[:, :], where[:, :], start[:, :], ALU.add))
            st(dve.tensor_copy(place[:, :], where[:, :]))
            with dve.Fori(0, TILES // LOT // 2) as i:
                for b in range(2):
                    n = 2 * i + b
                    here = bass.ds(n * LOT, LOT)
                    dve.wait_ge(freed, n + 1)
                    dve.tensor_copy(ibuf[:, b, :], place[:, here]).then_inc(spare, 1)
                    dve.wait_ge(spare, n + 1)
                    dve.tensor_copy(sbuf[:, b, :, :], tgt_score[:, here, :]).then_inc(i_done, 1)


def edge_states(core, d, t):
    nc = core.nc
    with ExitStack() as ctx:
        sem = lambda k: core.semaphore(ctx, f"es_{k}")
        sb = lambda k, s, d_=F32: ctx.enter_context(nc.sbuf_tensor(f"es_{k}", s, d_))
        carve = Carver(core.XN)
        G, A, L = carve(2, RUN, SRC_ROW), carve(2, RUN, HEADS), carve(2, RUN, STATE)
        tgt, top, e, w = (carve(HEADS, RUN) for _ in range(4))
        m, decay = carve(HEADS, RUN + 1), carve(HEADS, RUN)
        msg = carve(HF, RUN)
        same, reset = sb("same", [128, 2, RUN]), sb("reset", [128, RUN])
        ibuf, rbuf = sb("ibuf", [128, 2, RUN], I32), sb("rbuf", [128, 2], I32)
        steps, used, in_rows, act_in, act_out, l_done, turns, zero = map(sem, (
            "steps", "used", "in_rows", "act_in", "act_out", "l_done", "turns", "zero"))
        idx_in, edge_in, rows_in, first_in, l_out = ([sem(f"{k}{b}") for b in range(2)] for k in (
            "idx", "edge", "rows", "first", "l_out"))
        N_STEPS, l_free = 19, sem("l_free")
        block = ctx.enter_context(nc.Block())
        blocks = lambda a: a.rearrange("(s p f) -> p s f", p=128, f=RUN)
        of_run = d["run_target"].rearrange("(s p a) -> p s a", p=128, a=1)
        placed = t["placed"][0:EDGES, :].rearrange("(s p f) h -> p s f h", p=128, f=RUN)
        states = t["states"].rearrange("(s p f) c -> p s f c", p=128, f=RUN)
        ends = t["ends"].rearrange("(s p) c -> p s c", p=128)

        def pairs(eng):
            return eng.value_load(d["pairs"].rearrange("(p a) -> p a", a=1), min_val=1, max_val=BLOCKS // 2)


        @block.sync
        def _(sp):
            with sp.Fori(0, pairs(sp)) as i:
                for b in range(2):
                    s = 2 * i + b
                    one = bass.ds(s, 1)
                    sp.wait_ge(used, s + 1)
                    sp.dma_start(ibuf[:, b:b + 1, :], blocks(d["source"])[:, one, :]).then_inc(idx_in[b], 16)
                    sp.dma_start(rbuf[:, b:b + 1].rearrange("p (s a) -> p s a", a=1), of_run[:, one, :]
                                 ).then_inc(idx_in[b], 16)
                    sp.dma_start(same[:, b:b + 1, :], blocks(d["same"])[:, one, :]).then_inc(edge_in[b], 16)
                    sp.dma_start(A[:, b:b + 1, :, :], placed[:, one, :, :]).then_inc(edge_in[b], 16)

        @block.scalar
        def _(act):
            with act.Fori(0, pairs(act)) as i:
                for b in range(2):
                    s = 2 * i + b
                    for k, x in enumerate((w, decay)):
                        act.wait_ge(act_in, 2 * s + k + 1)
                        act.activation(x, x, ACT.Exp).then_inc(act_out, 1)
                    act.wait_ge(l_done, s + 1)
                    act.dma_start(states[:, bass.ds(s, 1), :, :], L[:, b:b + 1, :, :]).then_inc(l_out[b], 16)
                    act.dma_start(ends[:, bass.ds(s, 1), :], L[:, b:b + 1, RUN - 1, :]).then_inc(l_out[b], 16)
                    act.wait_ge(l_out[b], 32 * (i + 1))
                    act.sem_inc(l_free, 1)

        @block.gpsimd
        def _(pool):
            with pool.Fori(0, pairs(pool)) as i:
                for b in range(2):
                    s = 2 * i + b
                    pool.wait_ge(idx_in[b], 32 * (i + 1))
                    pool.wait_ge(edge_in[b], 32 * (i + 1))
                    pool.wait_ge(used, s + 1)
                    pool.sem_inc(turns, 1)
                    pool.indirect_dma_start(
                        out=A[:, b, 0, :], out_offset=None, in_=t["targets"],
                        in_offset=bass.IndirectOffsetOnAxis(ap=rbuf[:, b:b + 1], axis=0)).then_inc(first_in[b], 16)
                    for f in range(RUN):
                        pool.indirect_dma_start(
                            out=G[:, b, f, :], out_offset=None, in_=t["sources"],
                            in_offset=bass.IndirectOffsetOnAxis(ap=ibuf[:, b, f:f + 1], axis=0)
                            ).then_inc(rows_in[b], 16)

        @block.vector
        def _(dve):
            dve.memset(m, 0.0).then_inc(zero, 1)
            dve.sem_inc(used, 2)
            dve.sem_inc(l_free, 2)
            dve.wait_ge(zero, 1)
            with dve.Fori(0, pairs(dve)) as i:
                for b in range(2):
                    s = 2 * i + b
                    st = Steps(dve, steps, s * N_STEPS)
                    dve.wait_ge(edge_in[b], 32 * (i + 1))
                    st(dve.tensor_scalar(reset[:, :], same[:, b, :], -1.0, BIG, ALU.add, ALU.mult))
                    dve.wait_ge(first_in[b], 16 * (i + 1))
                    for h in range(HEADS):
                        st.mark(dve.tensor_tensor_scan(out=tgt[:, h, :], data0=same[:, b, :], data1=A[:, b, :, h],
                                                       initial=0.0, op0=ALU.mult, op1=ALU.add))
                    dve.wait_ge(rows_in[b], 16 * RUN * (i + 1))
                    for h in range(HEADS):
                        st.mark(dve.tensor_tensor_scan(out=top[:, h, :], data0=reset[:, :], data1=G[:, b, :, h],
                                                       initial=0.0, op0=ALU.add, op1=ALU.max))
                    st.done()
                    src = G[:, b, :, 0:HEADS].rearrange("p f h -> p h f")
                    st.mark(dve.tensor_tensor(top, top, tgt, ALU.add))
                    st(dve.tensor_tensor(e, src, tgt, ALU.add))
                    now, before = m[:, :, 1:], m[:, :, 0:RUN]
                    st.mark(dve.scalar_tensor_tensor(out=now, in0=top, scalar=LEAK, in1=top, op0=ALU.mult,
                                                     op1=ALU.max))
                    st(dve.scalar_tensor_tensor(out=e, in0=e, scalar=LEAK, in1=e, op0=ALU.mult, op1=ALU.max))
                    st.mark(dve.tensor_tensor(decay, before, now, ALU.subtract))
                    dve.tensor_tensor(w, e, now, ALU.subtract).then_inc(act_in, 1)
                    st.done()
                    resets = reset[:, :].rearrange("p (h f) -> p h f", h=1).to_broadcast([128, HEADS, RUN])
                    dve.tensor_tensor(decay, decay, resets, ALU.min).then_inc(act_in, 1)
                    dve.wait_ge(l_free, s + 1)
                    out = L[:, b, :, :]
                    st(dve.tensor_copy(out[:, :, 0:HEADS].rearrange("p f h -> p h f"), now))
                    dve.wait_ge(act_out, 2 * s + 2)
                    for h in range(HEADS):
                        st.mark(dve.tensor_tensor(
                            msg[:, h * GE:(h + 1) * GE, :],
                            G[:, b, :, HEADS + h * GE:HEADS + (h + 1) * GE].rearrange("p f e -> p e f"),
                            w[:, h, :].rearrange("p (e f) -> p e f", e=1).to_broadcast([128, GE, RUN]), ALU.mult))
                    assert st.n == N_STEPS
                    st.done()
                    for c in range(HEADS + HF):
                        h = c if c < HEADS else (c - HEADS) // GE
                        x = w[:, h, :] if c < HEADS else msg[:, c - HEADS, :]
                        scan = dve.tensor_tensor_scan(out=out[:, :, HEADS + c], data0=decay[:, h, :], data1=x,
                                                      initial=0.0, op0=ALU.mult, op1=ALU.add)
                    scan.then_inc(l_done, 1)
                    dve.wait_ge(l_done, s + 1)
                    dve.sem_inc(used, 1)


def stitch_runs(core, d, t):
    nc, ps = core.nc, core.psum
    ROWS = HEADS + HF
    with ExitStack() as ctx:
        sem = lambda k: core.semaphore(ctx, f"sr_{k}")
        sb = lambda k, s, d_=F32: ctx.enter_context(nc.sbuf_tensor(f"sr_{k}", s, d_))
        wide = Carver(core.XN, ROWS)
        top, val, m, decay = wide(RUNS), wide(RUNS), wide(RUNS + 1), wide(RUNS)
        first, last = sb("first", [ROWS, RUNS]), sb("last", [ROWS, RUNS])
        ends = sb("ends", [128, BLOCKS, STATE])
        tops = sb("tops", [128, BLOCKS, ROWS])
        out = sb("out", [128, BLOCKS, 2 * ROWS])
        loaded, ends_in, steps, tops_done, t_mm, t_out, act_in, act_out, done, b_mm, b_out, stored = map(sem, (
            "loaded", "ends_in", "steps", "tops", "t_mm", "t_out", "act_in", "act_out", "done", "b_mm", "b_out",
            "stored"))
        block = ctx.enter_context(nc.Block())

        @block.sync
        def _(sp):
            sp.dma_start(ends[:, :, :], t["ends"].rearrange("(s p) c -> p s c", p=128)).then_inc(ends_in, 16)
            for k, x in (("first", first), ("last", last)):
                sp.dma_start(x[:, :], d[k].rearrange("(a r) -> a r", a=1).to_broadcast([ROWS, RUNS])
                             ).then_inc(loaded, 16)
            sp.wait_ge(b_out, 2 * BLOCKS // 4)
            sp.dma_start(t["carry"].rearrange("(s p) c -> p s c", p=128), out[:, :, :]).then_inc(stored, 16)
            sp.wait_ge(stored, 16)
            sp.wait_ge(loaded, 32)
            sp.wait_ge(ends_in, 16)

        @block.vector
        def _(dve):
            st = Steps(dve, steps)
            dve.wait_ge(ends_in, 16)
            dve.tensor_copy(tops[:, :, 0:HEADS], ends[:, :, 0:HEADS]).then_inc(tops_done, 1)
            for h in range(HEADS):
                dve.tensor_copy(tops[:, :, HEADS + h * GE:HEADS + (h + 1) * GE],
                                ends[:, :, h:h + 1].to_broadcast([128, BLOCKS, GE])).then_inc(tops_done, 1)
            dve.wait_ge(loaded, 32)
            f, l = first[:, :].bitcast(I32), last[:, :].bitcast(I32)
            st.mark(dve.tensor_scalar(f, f, ID_BITS, None, ALU.logical_shift_right))
            st(dve.tensor_scalar(l, l, ID_BITS, None, ALU.logical_shift_right))
            st(dve.tensor_tensor(decay, f, l, ALU.is_equal))
            st(dve.tensor_tensor(m[:, 1:RUNS], f[:, 1:], l[:, 0:RUNS - 1], ALU.is_equal))
            st(dve.tensor_tensor(decay[:, 1:], decay[:, 1:], m[:, 1:RUNS], ALU.mult))
            st(dve.memset(decay[:, 0:1], 0.0))
            reset = first[:, :]
            st(dve.tensor_scalar(reset, decay, -1.0, BIG, ALU.add, ALU.mult))
            st(dve.memset(m[:, 0:1], 0.0))
            dve.wait_ge(t_out, 2 * BLOCKS // 4)
            st(dve.tensor_tensor_scan(out=m[:, 1:], data0=reset, data1=top, initial=0.0, op0=ALU.add, op1=ALU.max))
            st.mark(dve.tensor_tensor(top, top, m[:, 1:], ALU.subtract))
            st(dve.tensor_tensor(decay, m[:, 0:RUNS], m[:, 1:], ALU.subtract))
            dve.tensor_tensor(decay, decay, reset, ALU.min).then_inc(act_in, 1)
            dve.wait_ge(act_out, 2)
            st(dve.tensor_tensor(val, val, top, ALU.mult))
            dve.tensor_tensor_scan(out=top, data0=decay, data1=val, initial=0.0, op0=ALU.mult,
                                   op1=ALU.add).then_inc(done, 1)

        @block.tensor
        def _(pe):
            pe.wait_ge(tops_done, 1 + HEADS)
            for n in range(2 * BLOCKS // 4):
                k, q = divmod(n, BLOCKS // 4)
                if n >= 4:
                    pe.wait_ge(t_out, n - 3)
                for j in range(4):
                    x = (tops[:, 4 * q + j, :], ends[:, 4 * q + j, HEADS:])[k]
                    tr = nc.tensor.transpose(ps[0:ROWS, n % 4, j * 128:(j + 1) * 128], x, core.ident[:, :])
                tr.then_inc(t_mm, 1)
            pe.wait_ge(done, 1)
            for n in range(2 * BLOCKS // 4):
                k, q = divmod(n, BLOCKS // 4)
                x = (m[:, 1:], top)[k]
                if n >= 4:
                    pe.wait_ge(b_out, n - 3)
                for j in range(4):
                    tr = nc.tensor.transpose(ps[:, 4 + n % 4, j * ROWS:(j + 1) * ROWS],
                                             x[:, (4 * q + j) * 128:(4 * q + j + 1) * 128],
                                             core.ident[0:ROWS, 0:ROWS])
                tr.then_inc(b_mm, 1)

        @block.scalar
        def _(act):
            for n in range(2 * BLOCKS // 4):
                k, q = divmod(n, BLOCKS // 4)
                act.wait_ge(t_mm, n + 1)
                act.activation((top, val)[k][:, q * 512:(q + 1) * 512], ps[0:ROWS, n % 4, :],
                               ACT.Copy).then_inc(t_out, 1)
            act.wait_ge(act_in, 1)
            act.activation(top, top, ACT.Exp).then_inc(act_out, 1)
            act.activation(decay, decay, ACT.Exp).then_inc(act_out, 1)
            for n in range(2 * BLOCKS // 4):
                k, q = divmod(n, BLOCKS // 4)
                act.wait_ge(b_mm, n + 1)
                act.activation(out[:, 4 * q:4 * q + 4, k * ROWS:(k + 1) * ROWS],
                               ps[:, 4 + n % 4, 0:4 * ROWS].rearrange("p (j c) -> p j c", j=4),
                               ACT.Copy).then_inc(b_out, 1)


def edge_ends(core, start, end, at_end, before, has):
    nc = core.nc
    with ExitStack() as ctx:
        sb = lambda k, s, d_=F32: ctx.enter_context(nc.sbuf_tensor(f"ee_{k}", s, d_))
        pos = sb("pos", [128, TILES])
        steps = core.semaphore(ctx, "ee_steps")
        block = ctx.enter_context(nc.Block())

        @block.vector
        def _(dve):
            st = Steps(dve, steps)
            st(dve.tensor_scalar(pos[:, :], end[:, :], -1.0, 0.0, ALU.add, ALU.max))
            st(dve.tensor_copy(at_end[:, :], pos[:, :]))
            st(dve.tensor_scalar(before[:, :], at_end[:, :], RUN.bit_length() - 1, None, ALU.logical_shift_right))
            st(dve.tensor_copy(pos[:, :], before[:, :]))
            st(dve.tensor_scalar(has[:, 1, :], pos[:, :], float(RUN), None, ALU.mult))
            st(dve.tensor_tensor(has[:, 1, :], start[:, :], has[:, 1, :], ALU.is_lt))
            st(dve.tensor_tensor(has[:, 0, :], start[:, :], end[:, :], ALU.is_lt))
            st(dve.tensor_tensor(has[:, 1, :], has[:, 1, :], has[:, 0, :], ALU.mult))
            st(dve.tensor_scalar(pos[:, :], pos[:, :], -1.0, 0.0, ALU.add, ALU.max))
            st(dve.tensor_copy(before[:, :], pos[:, :]))


def graph_gates(core, p, feats, tgt_score, has, at_run, carried, gates):
    nc = core.nc
    carve = Carver(core.XN)
    with ExitStack() as ctx:
        sem = lambda k: core.semaphore(ctx, f"gg_{k}")
        sb = lambda k, s, d_=F32: ctx.enter_context(nc.sbuf_tensor(f"gg_{k}", s, d_))
        par = sb("par", [128, 4, HF])
        rank = sb("rank", [128, GE])
        m0, m1, m2, top, den, tmp = (carve(TILES, HEADS) for _ in range(6))
        agg, prod = carve(TILES, HF), carve(TILES, HF)
        off, mean, var, best, first, second = (carve(TILES) for _ in range(6))
        score, mask, key = (carve(TILES, GE) for _ in range(3))
        loaded, steps, act_in, act_out = map(sem, ("loaded", "steps", "act_in", "act_out"))
        block = ctx.enter_context(nc.Block())

        @block.sync
        def _(sp):
            flat = {"att_src": p["att_src"].rearrange("h e -> (h e)")}
            for k, q in enumerate(("att_src", "b_gat", "ln_gamma", "ln_beta")):
                v = flat.get(q, p[q])
                sp.dma_start(par[:, k, :], v.rearrange("(a c) -> a c", a=1).to_broadcast([128, HF])
                             ).then_inc(loaded, 16)
            sp.wait_ge(loaded, 64)

        @block.scalar
        def _(act):
            act.wait_ge(act_in, 1)
            for n, x in enumerate((m0, m1, m2)):
                act.activation(x, x, ACT.Exp).then_inc(act_out, 1)
            act.wait_ge(act_in, 2)
            act.activation(var, var, ACT.Sqrt, bias=core.eps[:, 1:2]).then_inc(act_out, 1)
            act.wait_ge(act_in, 3)
            act.activation(second, second, ACT.Exp).then_inc(act_out, 1)

        @block.vector
        def _(dve):
            st = Steps(dve, steps)
            heads = lambda x: x.rearrange("p t (h e) -> p t h e", h=HEADS)
            per_head = lambda x: x.rearrange("p t (h e) -> p t h e", e=1).to_broadcast([128, TILES, HEADS, GE])
            wide = lambda x, n: x.rearrange("p (t n) -> p t n", n=1).to_broadcast([128, TILES, n])
            const = lambda k: par[:, k, :].rearrange("p (t c) -> p t c", t=1).to_broadcast([128, TILES, HF])
            h = feats[:, :, :]
            dve.wait_ge(loaded, 64)
            for e in range(GE):
                st.mark(dve.memset(rank[:, e:e + 1], float(GE - e)))
            st(dve.tensor_tensor(prod, h, const(0), ALU.mult))
            st(dve.tensor_reduce(m0, heads(prod), AX.X, ALU.add))
            st(dve.tensor_tensor(m0, m0, tgt_score[:, :, :], ALU.add))
            st(dve.scalar_tensor_tensor(out=m0, in0=m0, scalar=LEAK, in1=m0, op0=ALU.mult, op1=ALU.max))
            for k, (m, x) in enumerate(((m1, at_run), (m2, carried))):
                st(dve.tensor_scalar(off, has[:, k, :], -1.0, BIG, ALU.add, ALU.mult))
                st(dve.tensor_tensor(m, x[:, :, 0:HEADS], wide(off, HEADS), ALU.add))
            st(dve.tensor_tensor(top, m1, m2, ALU.max))
            st(dve.tensor_tensor(top, top, m0, ALU.max))
            for m in (m0, m1, m2):
                st(dve.tensor_tensor(m, m, top, ALU.subtract))
            dve.sem_inc(act_in, 1)
            dve.wait_ge(act_out, 3)
            st(dve.tensor_tensor(heads(agg), heads(h), per_head(m0), ALU.mult))
            den_of, agg_of = (at_run[:, :, HEADS:2 * HEADS], carried[:, :, HEADS + HF:2 * HEADS + HF]), \
                (at_run[:, :, 2 * HEADS:], carried[:, :, 2 * HEADS + HF:])
            st(dve.tensor_copy(den, m0))
            for m, dn, ag in zip((m1, m2), den_of, agg_of):
                st.mark(dve.tensor_tensor(tmp, dn, m, ALU.mult))
                st(dve.tensor_tensor(heads(prod), heads(ag), per_head(m), ALU.mult))
                st.mark(dve.tensor_tensor(den, den, tmp, ALU.add))
                st(dve.tensor_tensor(agg, agg, prod, ALU.add))
            st(dve.tensor_scalar(den, den, 1e-16, None, ALU.add))
            st(dve.reciprocal(den, den))
            st(dve.tensor_tensor(heads(agg), heads(agg), per_head(den), ALU.mult))
            st(dve.tensor_tensor(agg, agg, const(1), ALU.add))
            st(dve.tensor_reduce(mean, agg, AX.X, ALU.add))
            st(dve.tensor_scalar(mean, mean, 1.0 / HF, None, ALU.mult))
            st(dve.tensor_tensor(agg, agg, wide(mean, HF), ALU.subtract))
            st(dve.tensor_tensor(prod, agg, agg, ALU.mult))
            st(dve.tensor_reduce(var, prod, AX.X, ALU.add))
            st(dve.tensor_scalar(var, var, 1.0 / HF, None, ALU.mult))
            dve.sem_inc(act_in, 1)
            dve.wait_ge(act_out, 4)
            st(dve.reciprocal(var, var))
            st(dve.tensor_tensor(agg, agg, wide(var, HF), ALU.mult))
            st(dve.tensor_tensor(agg, agg, const(2), ALU.mult))
            st(dve.tensor_tensor(agg, agg, const(3), ALU.add))
            st(dve.tensor_reduce(score, agg.rearrange("p t (h e) -> p t e h", h=HEADS), AX.X, ALU.add))
            st(dve.tensor_scalar(score, score, 1.0 / HEADS, None, ALU.mult))
            pick_two(nc, dve, st, score, GE, mask, gates[:, :, :], key, best, rank[:, :], first, second)
            st(dve.tensor_tensor(second, second, first, ALU.subtract))
            dve.sem_inc(act_in, 1)
            dve.wait_ge(act_out, 5)
            st(dve.tensor_scalar(first, second, 1.0, None, ALU.add))
            st(dve.reciprocal(first, first))
            st(dve.tensor_tensor(second, second, first, ALU.mult))
            st(dve.tensor_tensor(mask, mask, wide(first, GE), ALU.mult))
            st(dve.tensor_tensor(gates[:, :, :], gates[:, :, :], wide(second, GE), ALU.mult))
            st(dve.tensor_tensor(gates[:, :, :], gates[:, :, :], mask, ALU.add))


def graph_tables(nc):
    dram = lambda k, *s: nc.dram_tensor(f"graph_{k}", s, F32, kind="Internal").ap()
    return dict(sources=dram("sources", T, SRC_ROW), targets=dram("targets", T, HEADS),
                placed=dram("placed", EDGES + T, HEADS), states=dram("states", EDGES, STATE),
                ends=dram("ends", RUNS, STATE), carry=dram("carry", RUNS, 2 * (HEADS + HF)), xn=dram("xn", D, T))


def graph_phase(core, p, d, t, start, end, out):
    nc = core.nc
    xn_dram = t["xn"]
    with ExitStack() as outer:
        gates = outer.enter_context(nc.sbuf_tensor("gates1", [128, TILES, GE], F32))
        with ExitStack() as ctx:
            sb = lambda k, s, d_=F32: ctx.enter_context(nc.sbuf_tensor(f"gp_{k}", s, d_))
            feats, tgt_score = sb("feats", [128, TILES, HF]), sb("tgt", [128, TILES, HEADS])
            normalise(core, "ln4", 1, p["W_gat"], HF, feats)
            source_tables(core, p, t, feats, tgt_score, start, end, xn_dram)
            edge_states(core, d, t)
            stitch_runs(core, d, t)
            at_end, before = sb("at_end", [128, TILES], I32), sb("before", [128, TILES], I32)
            has = sb("has", [128, 2, TILES])
            edge_ends(core, start, end, at_end, before, has)
            tail = Carver(core.XN)
            tail.at = T - TILES * (STATE + 2 * (HEADS + HF))
            at_run, carried = tail(TILES, STATE), tail(TILES, 2 * (HEADS + HF))

            def keep(dst, name):
                def consume(dve, n, rows, used):
                    dve.tensor_copy(dst[:, bass.ds(n * 8, 8), :], rows).then_inc(used, 1)
                return consume

            gather(core, "ga", t["states"], STATE, at_end, TILES, 8, keep(at_run, "a"))
            gather(core, "gc", t["carry"], 2 * (HEADS + HF), before, TILES, 8, keep(carried, "c"))
            graph_gates(core, p, feats, tgt_score, has, at_run, carried, gates)
        experts(core, "e1", GE, gates, p["W1"].rearrange("e d f -> d e f"), p["b1"],
                p["W2"].rearrange("e (a f) c -> f (e a) c", a=2), p["b2"], False, out,
                xn_dram)


def metaformer(nc, p, out):
    with ExitStack() as ctx:
        core = Core(nc, ctx)
        setup(core)
        start, end = (ctx.enter_context(nc.sbuf_tensor(k, [128, TILES], F32)) for k in ("start", "end"))
        tables = graph_tables(nc)
        edges = index_phase(core, p["L1_ffn_edge_index"], p["x"], start, end,
                            [tables[k] for k in ("placed", "states", "ends")])
        normalise(core, "ln1", 0, None, 0, None)
        attention(core, {k[8:].lower() if k[8] == "W" else k[8:]: v for k, v in p.items() if k.startswith("L0_conv_")})
        expert_phase_0(core, {k[7:]: v for k, v in p.items() if k.startswith("L0_ffn_")})
        deform_phase(core, {k[8:]: v for k, v in p.items() if k.startswith("L1_conv_")})
        graph_phase(core, {k[7:]: v for k, v in p.items() if k.startswith("L1_ffn_")}, edges, tables, start, end,
                    out)


def kernel(**inputs):
    import numpy as _np
    import concourse.bacc as _bacc
    from concourse import mybir as _mybir
    from concourse.bass_utils import run_bass_kernel_spmd as _run

    laid = {k: _np.asarray(v) for k, v in inputs.items()}
    laid["x"] = laid["x"].reshape(IMAGES, D, PIX)
    for k in ("L0_conv_W_f", "L0_conv_W_g", "L0_conv_W_h", "L0_ffn_router_w"):
        laid[k] = laid[k].T
    laid["L0_ffn_b1"] = laid["L0_ffn_b1"].T
    laid["L1_ffn_b1"] = laid["L1_ffn_b1"].reshape(-1, 128).T
    for k in ("L1_conv_w_off", "L1_conv_weight"):
        laid[k] = laid[k].reshape(-1, D, TAPS).transpose(1, 2, 0)
    nc = _bacc.Bacc("TRN2", target_bir_lowering=False, num_devices=1)
    arrays, p = {}, {}
    for name, a in laid.items():
        a = _np.ascontiguousarray(a)
        arrays[f"in_{name}"] = a
        p[name] = nc.dram_tensor(f"in_{name}", a.shape, _mybir.dt.from_np(a.dtype), kind="ExternalInput").ap()
    out = nc.dram_tensor("out_0", (IMAGES, D, PIX), F32, kind="ExternalOutput").ap()
    metaformer(nc, p, out)
    r = _run(nc, [arrays], core_ids=[0])
    return r.results[0]["out_0"].reshape(IMAGES, D, SIDE, SIDE)
```
